# Optimizing a Trainium2 kernel written in Bass

```python
import numpy as np
import jax
import jax.numpy as jnp

def _softmax(x, axis=-1):
    return jax.nn.softmax(x, axis=axis)

def _gelu(x):
    return jax.nn.gelu(x, approximate=True)

def _silu(x):
    return jax.nn.silu(x)

def _sigmoid(x):
    return jax.nn.sigmoid(x)

def _layernorm(x, axis=-1, eps=1e-05):
    m = jnp.mean(x, axis=axis, keepdims=True)
    v = jnp.var(x, axis=axis, keepdims=True)
    return (x - m) / jnp.sqrt(v + eps)

def _scatter_add(tgt, idx, src, axis=0):
    return tgt.at[idx].add(src)

def _segment_sum(src, seg, n):
    return jax.ops.segment_sum(src, seg, n)
kernel_name = 'mk_sandwich_d1_jaxref_r4_a1aa4c'

def setup_inputs(seed: int=0):
    np.random.seed(seed)
    _w = jnp.asarray

    def _L0_attn_setup():
        import jax, jax.numpy as jnp
        import numpy as np
        from jax import lax
        D_MODEL = 256
        BATCH, SEQ = (4, 2048)

        def _binary_operator_diag(q_i, q_j):
            a_i, b_i = q_i
            a_j, b_j = q_j
            return (a_i * a_j, a_j * b_i + b_j)

        def _parallel_scan(a, b):
            a = jnp.moveaxis(a, 1, 0)
            b = jnp.moveaxis(b, 1, 0)
            _, h = lax.associative_scan(_binary_operator_diag, (a, b))
            return jnp.moveaxis(h, 0, 1)
        key = jax.random.key(seed)
        k_x, k_wz, k_wh = jax.random.split(key, 3)
        scale = 1.0 / np.sqrt(D_MODEL)
        x = jax.random.normal(k_x, (BATCH, SEQ, D_MODEL), dtype=jnp.float32)
        Wz = jax.random.normal(k_wz, (D_MODEL, D_MODEL), dtype=jnp.float32) * scale
        bz = jnp.zeros((D_MODEL,), dtype=jnp.float32)
        Wh = jax.random.normal(k_wh, (D_MODEL, D_MODEL), dtype=jnp.float32) * scale
        bh = jnp.zeros((D_MODEL,), dtype=jnp.float32)
        return {'x': x, 'Wz': Wz, 'bz': bz, 'Wh': Wh, 'bh': bh}
    _L0_attn_in = _L0_attn_setup()

    def _L0_ffn_setup():
        import jax, jax.numpy as jnp
        import numpy as np
        B, L, D = (4, 512, 256)
        H = 16
        E = 16
        NS = 16
        S = NS // E
        F = 1024
        EPS = 1e-05

        def _layernorm(x, g, b):
            mu = jnp.mean(x, axis=-1, keepdims=True)
            var = jnp.mean(jnp.square(x - mu), axis=-1, keepdims=True)
            return (x - mu) * jax.lax.rsqrt(var + EPS) * g + b

        def _mha(q, k, v, Wq, bq, Wk, bk, Wv, bv, Wo, bo):
            Bq, Lq, Dm = q.shape
            dh = Dm // H
            qh = (q @ Wq + bq).reshape(Bq, Lq, H, dh)
            kh = (k @ Wk + bk).reshape(Bq, -1, H, dh)
            vh = (v @ Wv + bv).reshape(Bq, -1, H, dh)
            scores = jnp.einsum('bqhd,bkhd->bhqk', qh, kh) / jnp.asarray(np.sqrt(dh), q.dtype)
            attn = jax.nn.softmax(scores, axis=-1)
            out = jnp.einsum('bhqk,bkhd->bqhd', attn, vh).reshape(Bq, Lq, Dm)
            return out @ Wo + bo
        key = jax.random.key(seed)
        ks = jax.random.split(key, 32)
        s = 0.02
        d = {}
        d['x'] = jax.random.normal(ks[0], (B, L, D), jnp.float32)
        d['slot_query'] = jax.random.normal(ks[1], (1, NS, D), jnp.float32) * 0.01
        for i, nm in enumerate(['d_Wq', 'd_Wk', 'd_Wv', 'd_Wo']):
            d[nm] = jax.random.normal(ks[2 + i], (D, D), jnp.float32) * s
        for nm in ['d_bq', 'd_bk', 'd_bv', 'd_bo']:
            d[nm] = jnp.zeros((D,), jnp.float32)
        for i, nm in enumerate(['c_Wq', 'c_Wk', 'c_Wv', 'c_Wo']):
            d[nm] = jax.random.normal(ks[6 + i], (D, D), jnp.float32) * s
        for nm in ['c_bq', 'c_bk', 'c_bv', 'c_bo']:
            d[nm] = jnp.zeros((D,), jnp.float32)
        d['e_ln_g'] = jnp.ones((E, D), jnp.float32)
        d['e_ln_b'] = jnp.zeros((E, D), jnp.float32)
        d['e_W1'] = jax.random.normal(ks[10], (E, D, F), jnp.float32) * s
        d['e_b1'] = jnp.zeros((E, F), jnp.float32)
        d['e_Wg'] = jax.random.normal(ks[11], (E, D, F), jnp.float32) * s
        d['e_bg'] = jnp.zeros((E, F), jnp.float32)
        d['e_W2'] = jax.random.normal(ks[12], (E, F, D), jnp.float32) * s
        d['e_b2'] = jnp.zeros((E, D), jnp.float32)
        return d
    _L0_ffn_in = _L0_ffn_setup()
    _d = {'L0_attn_x': _L0_attn_in['x'], 'L0_attn_Wz': _L0_attn_in['Wz'], 'L0_attn_bz': _L0_attn_in['bz'], 'L0_attn_Wh': _L0_attn_in['Wh'], 'L0_attn_bh': _L0_attn_in['bh'], 'L0_ffn_slot_query': _L0_ffn_in['slot_query'], 'L0_ffn_d_Wq': _L0_ffn_in['d_Wq'], 'L0_ffn_d_Wk': _L0_ffn_in['d_Wk'], 'L0_ffn_d_Wv': _L0_ffn_in['d_Wv'], 'L0_ffn_d_Wo': _L0_ffn_in['d_Wo'], 'L0_ffn_d_bq': _L0_ffn_in['d_bq'], 'L0_ffn_d_bk': _L0_ffn_in['d_bk'], 'L0_ffn_d_bv': _L0_ffn_in['d_bv'], 'L0_ffn_d_bo': _L0_ffn_in['d_bo'], 'L0_ffn_c_Wq': _L0_ffn_in['c_Wq'], 'L0_ffn_c_Wk': _L0_ffn_in['c_Wk'], 'L0_ffn_c_Wv': _L0_ffn_in['c_Wv'], 'L0_ffn_c_Wo': _L0_ffn_in['c_Wo'], 'L0_ffn_c_bq': _L0_ffn_in['c_bq'], 'L0_ffn_c_bk': _L0_ffn_in['c_bk'], 'L0_ffn_c_bv': _L0_ffn_in['c_bv'], 'L0_ffn_c_bo': _L0_ffn_in['c_bo'], 'L0_ffn_e_ln_g': _L0_ffn_in['e_ln_g'], 'L0_ffn_e_ln_b': _L0_ffn_in['e_ln_b'], 'L0_ffn_e_W1': _L0_ffn_in['e_W1'], 'L0_ffn_e_b1': _L0_ffn_in['e_b1'], 'L0_ffn_e_Wg': _L0_ffn_in['e_Wg'], 'L0_ffn_e_bg': _L0_ffn_in['e_bg'], 'L0_ffn_e_W2': _L0_ffn_in['e_W2'], 'L0_ffn_e_b2': _L0_ffn_in['e_b2']}
    _x0 = _d['L0_attn_x']
    _d['L0_attn_x'] = jax.random.normal(jax.random.fold_in(jax.random.key(seed), 1), (16, 1024, 256), dtype=_x0.dtype)
    del _x0
    return _d

def reference(L0_attn_x, L0_attn_Wz, L0_attn_bz, L0_attn_Wh, L0_attn_bh, L0_ffn_slot_query, L0_ffn_d_Wq, L0_ffn_d_Wk, L0_ffn_d_Wv, L0_ffn_d_Wo, L0_ffn_d_bq, L0_ffn_d_bk, L0_ffn_d_bv, L0_ffn_d_bo, L0_ffn_c_Wq, L0_ffn_c_Wk, L0_ffn_c_Wv, L0_ffn_c_Wo, L0_ffn_c_bq, L0_ffn_c_bk, L0_ffn_c_bv, L0_ffn_c_bo, L0_ffn_e_ln_g, L0_ffn_e_ln_b, L0_ffn_e_W1, L0_ffn_e_b1, L0_ffn_e_Wg, L0_ffn_e_bg, L0_ffn_e_W2, L0_ffn_e_b2):

    def _L0_attn_ref(x, Wz, bz, Wh, bh):
        import jax, jax.numpy as jnp
        import numpy as np
        from jax import lax
        D_MODEL = 256
        BATCH, SEQ = (4, 2048)

        def _binary_operator_diag(q_i, q_j):
            a_i, b_i = q_i
            a_j, b_j = q_j
            return (a_i * a_j, a_j * b_i + b_j)

        def _parallel_scan(a, b):
            a = jnp.moveaxis(a, 1, 0)
            b = jnp.moveaxis(b, 1, 0)
            _, h = lax.associative_scan(_binary_operator_diag, (a, b))
            return jnp.moveaxis(h, 0, 1)
        z_pre = jnp.einsum('bsd,de->bse', x, Wz) + bz
        h_tilde = jnp.einsum('bsd,de->bse', x, Wh) + bh
        z = jax.nn.sigmoid(z_pre)
        a = 1.0 - z
        b = z * h_tilde
        return _parallel_scan(a, b)

    def _L0_ffn_ref(x, slot_query, d_Wq, d_Wk, d_Wv, d_Wo, d_bq, d_bk, d_bv, d_bo, c_Wq, c_Wk, c_Wv, c_Wo, c_bq, c_bk, c_bv, c_bo, e_ln_g, e_ln_b, e_W1, e_b1, e_Wg, e_bg, e_W2, e_b2):
        import jax, jax.numpy as jnp
        import numpy as np
        B, L, D = (4, 512, 256)
        H = 16
        E = 16
        NS = 16
        S = NS // E
        F = 1024
        EPS = 1e-05

        def _layernorm(x, g, b):
            mu = jnp.mean(x, axis=-1, keepdims=True)
            var = jnp.mean(jnp.square(x - mu), axis=-1, keepdims=True)
            return (x - mu) * jax.lax.rsqrt(var + EPS) * g + b

        def _mha(q, k, v, Wq, bq, Wk, bk, Wv, bv, Wo, bo):
            Bq, Lq, Dm = q.shape
            dh = Dm // H
            qh = (q @ Wq + bq).reshape(Bq, Lq, H, dh)
            kh = (k @ Wk + bk).reshape(Bq, -1, H, dh)
            vh = (v @ Wv + bv).reshape(Bq, -1, H, dh)
            scores = jnp.einsum('bqhd,bkhd->bhqk', qh, kh) / jnp.asarray(np.sqrt(dh), q.dtype)
            attn = jax.nn.softmax(scores, axis=-1)
            out = jnp.einsum('bhqk,bkhd->bqhd', attn, vh).reshape(Bq, Lq, Dm)
            return out @ Wo + bo
        Bx = x.shape[0]
        q = jnp.broadcast_to(slot_query, (Bx, NS, D))
        o = q + _mha(q, x, x, d_Wq, d_bq, d_Wk, d_bk, d_Wv, d_bv, d_Wo, d_bo)
        os = o.reshape(Bx, E, S, D)
        h = _layernorm(os, e_ln_g[None, :, None, :], e_ln_b[None, :, None, :])
        u = jax.nn.silu(jnp.einsum('besd,edf->besf', h, e_W1) + e_b1[None, :, None, :])
        g = jax.nn.silu(jnp.einsum('besd,edf->besf', h, e_Wg) + e_bg[None, :, None, :])
        y = jnp.einsum('besf,efd->besd', u * g, e_W2) + e_b2[None, :, None, :]
        o = o + y.reshape(Bx, NS, D)
        out = _mha(x, o, o, c_Wq, c_bq, c_Wk, c_bk, c_Wv, c_bv, c_Wo, c_bo)
        return out
    x = L0_attn_x
    x = x + _layernorm(_L0_attn_ref(_layernorm(x, axis=-1), L0_attn_Wz, L0_attn_bz, L0_attn_Wh, L0_attn_bh), axis=-1)
    x = x + _layernorm(_L0_ffn_ref(_layernorm(x, axis=-1), L0_ffn_slot_query, L0_ffn_d_Wq, L0_ffn_d_Wk, L0_ffn_d_Wv, L0_ffn_d_Wo, L0_ffn_d_bq, L0_ffn_d_bk, L0_ffn_d_bv, L0_ffn_d_bo, L0_ffn_c_Wq, L0_ffn_c_Wk, L0_ffn_c_Wv, L0_ffn_c_Wo, L0_ffn_c_bq, L0_ffn_c_bk, L0_ffn_c_bv, L0_ffn_c_bo, L0_ffn_e_ln_g, L0_ffn_e_ln_b, L0_ffn_e_W1, L0_ffn_e_b1, L0_ffn_e_Wg, L0_ffn_e_bg, L0_ffn_e_W2, L0_ffn_e_b2), axis=-1)
    return x

_drawn_inputs = setup_inputs


def setup_inputs(seed=0):
    import zlib

    import numpy as np

    out = dict(_drawn_inputs(seed))
    spreads = {'L0_attn_bz': (0.0, 0.333),
     'L0_attn_bh': (0.0, 0.1),
     'L0_ffn_d_bq': (0.0, 0.8),
     'L0_ffn_d_bk': (0.0, 2.0),
     'L0_ffn_d_bv': (0.0, 0.369),
     'L0_ffn_d_bo': (0.0, 0.1),
     'L0_ffn_c_bq': (0.0, 0.8),
     'L0_ffn_c_bk': (0.0, 2.0),
     'L0_ffn_c_bv': (0.0, 0.8),
     'L0_ffn_c_bo': (0.0, 0.673),
     'L0_ffn_e_ln_g': (1.0, 0.6),
     'L0_ffn_e_ln_b': (0.0, 0.8),
     'L0_ffn_e_b1': (0.0, 0.8),
     'L0_ffn_e_bg': (0.0, 0.8),
     'L0_ffn_e_b2': (0.0, 0.621)}
    factors = {'L0_ffn_slot_query': 8.0,
     'L0_ffn_d_Wq': 8.0,
     'L0_ffn_d_Wk': 8.0,
     'L0_ffn_d_Wv': 8.0,
     'L0_ffn_d_Wo': 2.91,
     'L0_ffn_c_Wq': 8.0,
     'L0_ffn_c_Wk': 8.0,
     'L0_ffn_e_W1': 8.0,
     'L0_ffn_e_Wg': 8.0,
     'L0_ffn_e_W2': 8.0}
    for name, (base, spread) in spreads.items():
        noise = np.random.default_rng([zlib.crc32(name.encode()), seed]).standard_normal(out[name].shape)
        drawn = base * np.exp(spread * noise) if base else spread * noise
        out[name] = jnp.asarray(drawn.astype(out[name].dtype))
    for name, factor in factors.items():
        out[name] = (out[name] * factor).astype(out[name].dtype)
    return out
```

```python
from collections import namedtuple
from contextlib import ExitStack

import concourse.bass as bass
from concourse import mybir

F32 = mybir.dt.float32
F32R = mybir.dt.float32r
ALU = mybir.AluOpType
ACT = mybir.ActivationFunctionType
AX = mybir.AxisListType.X

P = 128
B, S, D = 16, 1024, 256
C = D // P
T = S // P
HT = T // 2
HS = S // 2
H, NQ = 16, 16
DH = D // H
HC = P // DH
HQ = H * NQ
E, F = 16, 1024
FK = F // P
EPS = 1e-5
KEY_SCALE = 0.25
SLOTS = 4
ROWS = 4

SEMAPHORES = """
sp_passed pool_passed dve_passed pe_passed
ident_built consts_built w_loaded sel_built x_loaded0 x_loaded1 split_w zeroed
sqT_done sqT_kept qT_done qT_kept wkT_done wkT_kept qb_built mk_done mk_hi mk_kept
x_stats x_mv x_var x_pow n_ready
tn_done tn_hi tn_lo
zh_done z_sig a_sig b_made h_scanned
th_done th_stats th_mv th_var th_pow th_norm y_ready x1_ready
x1_stored0 x1_stored1 st_stored x1_stats x1_mv x1_var x1_pow n2_ready
t2_done t2_hi t2_lo
s_done s_max mt_done mt_red mt_sum mt_kept mr_done mr_hi mr_kept ga_done p_ready
u_done u_rcp u_kept tu_done ut_kept
ew0 ew1 ew2 ew3 ew_used
slot_w slot_small wvp_built spread_made ao_done ao_kept o_done o_kept o_stats o_mv o_var o_pow
o_centred o_scaled o_ln b2t_done b2t_kept ot_done ot_kept
xe_made ug_done ug_silu hg_made hgt_done hgt_kept y_done y_kept yt_done o2_made
c_w c_rows0 c_rows1 c_rows2 c_rows3 kv_done kv_kept wqT_done wqT_kept bqp_made bo_made
n2c_ready kb_made mn_done m_hi m_kept n_kept cr_hi cr_kept
t3_done t3_hi t3_lo sc_done c_max c_sub c_exp c_sum c_rcp c_prob tp_done tp_kept
oc_done oc_stats oc_mv oc_var oc_pow oc_norm yc_ready oc_added oc_stored
"""


def live(b):
    return not isinstance(b, int) or 0 <= b < B


def after_first(b):
    return not isinstance(b, int) or b > 0


def row(ap, b):
    return ap[bass.ds(b, 1)].rearrange("o p n -> (o p) n")


def mixer_moe(nc, x, Wz, bz, Wh, bh, slot_query, d_Wq, d_Wk, d_Wv, d_Wo, d_bq, d_bk, d_bv, d_bo,
              c_Wq, c_Wk, c_Wv, c_Wo, c_bq, c_bk, c_bv, c_bo,
              e_ln_g, e_ln_b, e_W1, e_b1, e_Wg, e_bg, e_W2, e_b2, out):
    x1_dram = nc.dram_tensor("x1_rows", [B, P, T * D], F32, kind="Internal").ap()
    st_dram = nc.dram_tensor("x1_norms", [B, P, 2 * T], F32, kind="Internal").ap()
    with ExitStack() as ctx:
        names = SEMAPHORES.split()
        sem = namedtuple("Semaphores", names)(*[ctx.enter_context(nc.semaphore(n)) for n in names])
        ps = ctx.enter_context(nc.psum_tensor("ps", [P, 8, 512], F32))
        keep = tensors(nc, ctx, "keep", [
            ("ident", [P, P], F32), ("hmask", [P, HC, DH], F32), ("selrow", [P, P], F32R),
            ("zero", [P, D], F32), ("mhalf", [P, T], F32),
            ("UT", [P, C, HQ, B], F32),
            ("w1_0", [P, C, F], F32), ("wg_0", [P, C, F], F32), ("w2_0", [P, FK, D], F32),
        ])
        with ExitStack() as inner:
            dispatch_phase(nc, inner, sem, ps, keep, x, Wz, bz, Wh, bh, slot_query, d_Wq, d_Wk, d_bq, d_bk,
                           e_W1, e_Wg, e_W2, x1_dram, st_dram)
        with ExitStack() as inner:
            o2 = tensors(nc, inner, "slots", [("o2T", [P, C, NQ * B], F32)])
            with ExitStack() as innermost:
                expert_phase(nc, innermost, sem, ps, keep, o2, slot_query, d_Wv, d_Wo, d_bv, d_bo,
                             e_ln_g, e_ln_b, e_W1, e_b1, e_Wg, e_bg, e_W2, e_b2)
            with ExitStack() as innermost:
                combine_phase(nc, innermost, sem, ps, keep, o2, c_Wq, c_Wk, c_Wv, c_Wo, c_bq, c_bk, c_bv, c_bo,
                              x1_dram, st_dram, out)


def alone(e, passed):
    e.sem_inc(passed, 1)


def tensors(nc, ctx, phase, specs):
    got = [ctx.enter_context(nc.sbuf_tensor(f"{phase}_{n}", shape, dtype)) for n, shape, dtype in specs]
    return namedtuple("Tensors", [n for n, _, _ in specs])(*got)


def three_passes(nc, dst, w_hi, w_lo, a_hi, a_lo, first, last, skip=False):
    nc.tensor.matmul(dst, w_hi, a_hi, start=first, stop=False, skip_group_check=skip)
    nc.tensor.matmul(dst, w_hi, a_lo, start=False, stop=False, skip_group_check=skip)
    return nc.tensor.matmul(dst, w_lo, a_hi, start=False, stop=last, skip_group_check=skip)


def dispatch_phase(nc, ctx, sem, ps, keep, x, Wz, bz, Wh, bh, slot_query, d_Wq, d_Wk, d_bq, d_bk,
                   e_W1, e_Wg, e_W2, x1_dram, st_dram):
    t = tensors(nc, ctx, "dispatch", [
        ("xt", [P, 2, T, D], F32),
        ("n", [P, T, D], F32),
        ("nT_hi", [P, C, S], F32R), ("nT_lo", [P, C, S], F32R),
        ("z", [P, 2, HS], F32),
        ("a", [P, C, S], F32),
        ("hT", [P, C, S], F32),
        ("y", [P, HT, D], F32),
        ("n2", [P, 2, T, D + 4], F32),
        ("n2T_hi", [P, C, S], F32R), ("n2T_lo", [P, C, S], F32R),
        ("pT", [P, T, HQ], F32),
        ("u", [P, 2, D], F32),
        ("wz", [P, C, D], F32), ("wh", [P, C, D], F32),
        ("wz_hi", [P, C, D], F32R), ("wz_lo", [P, C, D], F32R),
        ("wh_hi", [P, C, D], F32R), ("wh_lo", [P, C, D], F32R),
        ("mk_hi", [P, C, HQ], F32R), ("mk_lo", [P, C, HQ], F32R),
        ("wkT", [P, C, D], F32),
        ("sq", [NQ, D], F32), ("sqT", [P, C, NQ], F32), ("qT", [P, C, NQ], F32),
        ("qb", [P, C, HC, NQ], F32),
        ("bz", [P, C], F32), ("nbz", [P, C], F32), ("bh", [P, C], F32),
        ("bq", [P, C], F32), ("bk", [P, C], F32),
        ("ccol", [P, 2], F32),
        ("sel32", [P, P], F32),
        ("x_st", [P, T, 6], F32), ("x_mv", [P, T, 2], F32), ("x_v", [P, 2, T], F32), ("x_r", [P, T], F32),
        ("h_st", [P, HT, 6], F32), ("h_mv", [P, HT, 2], F32), ("h_v", [P, 2, HT], F32),
        ("h_r", [P, 2, 2, HT], F32),
        ("x1_st", [P, T, 6], F32), ("x1_mv", [P, T, 2], F32), ("x1_v", [P, T], F32),
        ("x1_n", [P, 2, 2, T], F32),
        ("mx", [P, HQ], F32), ("mcol", [P, 2], F32), ("mcol2", [P, 2], F32), ("mcolp", [P, 2, 64], F32),
        ("grow", [P, HQ], F32R), ("grow_t", [64, HQ], F32R),
        ("rcp", [P, 2], F32),
    ])
    wq, wk = t.xt[:, 1, 0:2, :], t.xt[:, 1, 2:4, :]
    x_loaded, x1_stored = (sem.x_loaded0, sem.x_loaded1), (sem.x1_stored0, sem.x1_stored1)
    s_all = ps[:, 4:8, :].rearrange("p k n -> p (k n)")
    s_tile = s_all.rearrange("p (j q) -> p j q", q=HQ)
    G0, G1 = 0, 2

    def rows(e, body):
        for i in range(4):
            body(i, i % 2, i // 2)
        with e.Fori(2, B // 2 - 1) as k:
            body(2 * k, 0, k)
            body(2 * k + 1, 1, k)
        for i in range(B - 2, B + 3):
            body(i, i % 2, i // 2)

    with nc.Block() as block:

        @block.sync
        def _(sp):
            sp.dma_start(t.sq[:, :], slot_query.rearrange("o q d -> (o q) d")).then_inc(sem.w_loaded, 16)
            for dst, src in ((wq, d_Wq), (wk, d_Wk), (t.wz[:, :, :], Wz), (t.wh[:, :, :], Wh)):
                sp.dma_start(dst, src.rearrange("(c p) n -> p c n", p=P)).then_inc(sem.w_loaded, 16)
            for dst, src in ((t.bz, bz), (t.bh, bh), (t.bq, d_bq), (t.bk, d_bk)):
                sp.dma_start(dst[:, :], src.rearrange("(c p) -> p c", p=P), allow_slow_non_contiguous=True) \
                    .then_inc(sem.w_loaded, 16)
            sp.dma_start(t.xt[:, 0], x[0].rearrange("(j p) d -> p j d", p=P)).then_inc(x_loaded[0], 16)
            sp.wait_ge(sem.qT_kept, 1)
            sp.wait_ge(sem.wkT_kept, 1)
            sp.dma_start(t.xt[:, 1], x[1].rearrange("(j p) d -> p j d", p=P)).then_inc(x_loaded[1], 16)

            def body(i, s, k):
                o = 1 - s
                if live(i - 1):
                    sp.wait_ge(sem.x1_ready, 2 * i)
                    alone(sp, sem.sp_passed)
                    sp.dma_start(row(x1_dram, i - 1), t.xt[:, o].rearrange("p j d -> p (j d)")) \
                        .then_inc(x1_stored[o], 16)
                    sp.wait_ge(sem.n2_ready, i)
                    alone(sp, sem.sp_passed)
                    if after_first(i - 1):
                        sp.wait_ge(sem.st_stored, 16 * (i - 1))
                    alone(sp, sem.sp_passed)
                    sp.dma_start(row(st_dram, i - 1), t.x1_n[:, o].rearrange("p a j -> p (a j)")) \
                        .then_inc(sem.st_stored, 16)
                if live(i - 1) and live(i + 1):
                    sp.wait_ge(x1_stored[o], 16 * (k + s))
                    alone(sp, sem.sp_passed)
                    sp.dma_start(t.xt[:, o], x[bass.ds(i + 1, 1)].rearrange("o (j p) d -> p (o j) d", p=P)) \
                        .then_inc(x_loaded[o], 16)

            rows(sp, body)
            sp.dma_start(keep.w1_0[:, :, :], e_W1[0].rearrange("(c p) f -> p c f", p=P)).then_inc(sem.ew0, 16)
            sp.dma_start(keep.wg_0[:, :, :], e_Wg[0].rearrange("(c p) f -> p c f", p=P)).then_inc(sem.ew0, 16)
            sp.dma_start(keep.w2_0[:, :, :], e_W2[0].rearrange("(k p) d -> p k d", p=P)).then_inc(sem.ew0, 16)
            sp.wait_ge(x1_stored[0], 16 * (B // 2))
            sp.wait_ge(x1_stored[1], 16 * (B // 2))
            sp.wait_ge(sem.st_stored, 16 * B)

        @block.gpsimd
        def _(pool):
            g = nc.gpsimd
            g.memset(keep.ident[:, :], 0.0).then_inc(sem.ident_built, 1)
            g.memset(keep.hmask[:, :, :], 1.0).then_inc(sem.ident_built, 1)
            g.memset(keep.mhalf[:, :], -0.5)
            g.memset(keep.zero[:, :], 0.0)
            g.memset(t.mcolp[:, :, :], 0.0)
            g.memset(t.n2[:, 0, :, D:D + 4], 1.0)
            g.memset(t.n2[:, 1, :, D:D + 4], 1.0).then_inc(sem.zeroed, 1)
            pool.wait_ge(sem.ident_built, 2)
            g.affine_select(out=keep.ident[:, :], in_=keep.ident[:, :], compare_op=ALU.not_equal, fill=1.0,
                            base=0, pattern=[[-1, P]], channel_multiplier=1).then_inc(sem.ident_built, 1)
            g.affine_select(out=keep.hmask[:, :, :], in_=keep.hmask[:, :, :], compare_op=ALU.is_ge, fill=0.0,
                            base=0, pattern=[[-DH, HC], [0, DH]], channel_multiplier=1).then_inc(sem.ident_built, 1)
            pool.wait_ge(sem.ident_built, 4)
            g.affine_select(out=keep.hmask[:, :, :], in_=keep.hmask[:, :, :], compare_op=ALU.is_ge, fill=0.0,
                            base=DH - 1, pattern=[[DH, HC], [0, DH]], channel_multiplier=-1) \
                .then_inc(sem.consts_built, 1)

            def norm_x(b, s):
                pool.wait_ge(sem.x_var, b + 1)
                g.tensor_tensor(t.x_r[:, :], t.x_v[:, 0], keep.mhalf[:, :], ALU.pow).then_inc(sem.x_pow, 1)
                pool.wait_ge(sem.x_pow, b + 1)
                if after_first(b):
                    pool.wait_ge(sem.tn_done, 2 * b)
                alone(pool, sem.pool_passed)
                for j in range(T):
                    last = g.tensor_scalar(t.n[:, j], t.xt[:, s, j], t.x_v[:, 1, j:j + 1], t.x_r[:, j:j + 1],
                                           ALU.add, ALU.mult)
                    if j % HT == HT - 1:
                        last.then_inc(sem.n_ready, 1)

            def body(i, s, k):
                o = 1 - s
                if live(i - 1):
                    pool.wait_ge(sem.x1_var, i)
                    if live(i - 3) and after_first(i - 2):
                        pool.wait_ge(sem.st_stored, 16 * (i - 2))
                    g.tensor_tensor(t.x1_n[:, o, 0], t.x1_v[:, :], keep.mhalf[:, :], ALU.pow) \
                        .then_inc(sem.x1_pow, 1)
                    pool.wait_ge(sem.x1_pow, i)
                    if live(i - 3):
                        pool.wait_ge(sem.u_done, i - 2)
                    alone(pool, sem.pool_passed)
                    for j in range(T):
                        last = g.tensor_scalar(t.n2[:, o, j, 0:D], t.xt[:, o, j], t.x1_n[:, o, 1, j:j + 1],
                                               t.x1_n[:, o, 0, j:j + 1], ALU.add, ALU.mult)
                    last.then_inc(sem.n2_ready, 1)
                if live(i + 1):
                    norm_x(i + 1, o)
                if live(i):
                    for h in range(2):
                        pool.wait_ge(sem.th_var, 2 * i + h + 1)
                        g.tensor_tensor(t.h_r[:, h, 0], t.h_v[:, 0], keep.mhalf[:, 0:HT], ALU.pow) \
                            .then_inc(sem.th_pow, 1)
                        pool.wait_ge(sem.th_pow, 2 * i + h + 1)
                        g.tensor_tensor(t.h_r[:, h, 1], t.h_v[:, 1], t.h_r[:, h, 0], ALU.mult) \
                            .then_inc(sem.th_norm, 1)
                        pool.wait_ge(sem.y_ready, 2 * i + h + 1)
                        half = t.xt[:, s, h * HT:(h + 1) * HT]
                        g.tensor_tensor(half, half, t.y[:, :, :], ALU.add).then_inc(sem.x1_ready, 1)

            norm_x(0, 0)
            rows(pool, body)

        @block.scalar
        def _(act):
            a = nc.scalar
            act.wait_ge(sem.w_loaded, 16 * 9)
            a.activation(t.nbz[:, :], t.bz[:, :], ACT.Copy, scale=-1.0).then_inc(sem.split_w, 1)
            act.wait_ge(sem.mk_done, 1)
            a.activation(t.mk_hi[:, :, :], ps[:, 4, :].rearrange("p (c q) -> p c q", c=C), ACT.Copy) \
                .then_inc(sem.mk_hi, 1)
            act.wait_ge(sem.split_w, 1)

            def keep_hi(dst, group, h, done, n, out_sem):
                act.wait_ge(done, n)
                a.activation(dst[:, :, h * HS:(h + 1) * HS], ps[:, group:group + 2, :], ACT.Copy) \
                    .then_inc(out_sem, 1)

            def body(i, s, k):
                if live(i):
                    for h in range(2):
                        if h == 0 and after_first(i):
                            act.wait_ge(sem.zh_done, 4 * i)
                        keep_hi(t.nT_hi, (G0, G1)[h], h, sem.tn_done, 2 * i + h + 1, sem.tn_hi)
                if live(i - 3):
                    act.wait_ge(sem.tu_done, i - 2)
                    a.activation(keep.UT[:, :, :, bass.ds(i - 3, 1)],
                                 ps[:, 1, :].rearrange("p (c q o) -> p c q o", c=C, o=1), ACT.Copy) \
                        .then_inc(sem.ut_kept, 1)
                if live(i - 2):
                    act.wait_ge(sem.ga_done, i - 1)
                    if after_first(i - 2):
                        act.wait_ge(sem.u_done, i - 2)
                    a.activation(t.pT[:, :, :].rearrange("p j q -> p (j q)"), s_all, ACT.Exp).then_inc(sem.p_ready, 1)
                if live(i):
                    for m in range(4):
                        e, h = m % 2, m // 2
                        bank = (G1, G0)[m % 2]
                        act.wait_ge(sem.zh_done, 4 * i + m + 1)
                        if m >= 2 or after_first(i):
                            act.wait_ge(sem.b_made, 4 * i + m - 1)
                        a.activation(t.z[:, m % 2], ps[:, bank, :], ACT.Sigmoid, bias=t.bz[:, e:e + 1]) \
                            .then_inc(sem.z_sig, 1)
                        if m == 0 and after_first(i):
                            act.wait_ge(sem.h_scanned, 4 * i)
                        a.activation(t.a[:, e, h * HS:(h + 1) * HS], ps[:, bank, :], ACT.Sigmoid,
                                     bias=t.nbz[:, e:e + 1], scale=-1.0).then_inc(sem.a_sig, 1)
                if live(i - 2):
                    act.wait_ge(sem.u_rcp, i - 1)
                    if after_first(i - 2):
                        act.wait_ge(sem.tu_done, i - 2)
                    for m in range(2):
                        last = a.activation(t.u[:, m], ps[:, G1 + m, 0:D], ACT.Copy, scale=t.rcp[:, m:m + 1])
                    last.then_inc(sem.u_kept, 1)
                if live(i - 1):
                    for h in range(2):
                        if h == 0 and after_first(i - 1):
                            act.wait_ge(sem.s_done, i - 1)
                        keep_hi(t.n2T_hi, (G0, G1)[h], h, sem.t2_done, 2 * i + h - 1, sem.t2_hi)
                if live(i):
                    for h in range(2):
                        act.wait_ge(sem.th_norm, 2 * i + h + 1)
                        if h == 1 or after_first(i):
                            act.wait_ge(sem.x1_ready, 2 * i + h)
                        for j in range(HT):
                            last = a.activation(t.y[:, j],
                                                ps[:, (G0, G1)[h] + j // 2, (j % 2) * D:(j % 2 + 1) * D],
                                                ACT.Identity, scale=t.h_r[:, h, 0, j:j + 1],
                                                bias=t.h_r[:, h, 1, j:j + 1])
                        last.then_inc(sem.y_ready, 1)

            rows(act, body)

        @block.vector
        def _(dve):
            v = nc.vector
            dve.wait_ge(sem.w_loaded, 16 * 9)
            v.tensor_copy(t.wz_hi[:, :, :], t.wz[:, :, :])
            v.tensor_copy(t.wh_hi[:, :, :], t.wh[:, :, :]).then_inc(sem.split_w, 1)
            dve.wait_ge(sem.split_w, 2)
            v.tensor_tensor(t.wz_lo[:, :, :], t.wz[:, :, :], t.wz_hi[:, :, :], ALU.subtract)
            v.tensor_tensor(t.wh_lo[:, :, :], t.wh[:, :, :], t.wh_hi[:, :, :], ALU.subtract).then_inc(sem.split_w, 1)
            v.memset(t.sel32[:, :], 0.0).then_inc(sem.sel_built, 1)
            dve.wait_ge(sem.sel_built, 1)
            v.memset(t.sel32[0:1, :], 1.0)
            v.memset(t.sel32[32:33, :], 1.0).then_inc(sem.sel_built, 1)
            dve.wait_ge(sem.sel_built, 2)
            dve.wait_ge(sem.zeroed, 1)
            v.tensor_copy(keep.selrow[:, :], t.sel32[:, :])
            v.tensor_copy(t.grow[:, :], keep.zero[:, :]).then_inc(sem.split_w, 1)
            dve.wait_ge(sem.sqT_done, 1)
            v.tensor_copy(t.sqT[:, :, :], ps[:, 0, 0:C * NQ].rearrange("p (c q) -> p c q", c=C)).then_inc(sem.sqT_kept, 1)
            dve.wait_ge(sem.qT_done, 1)
            for c in range(C):
                last = v.tensor_scalar(t.qT[:, c], ps[:, 1, c * NQ:(c + 1) * NQ], t.bq[:, c:c + 1], KEY_SCALE,
                                       ALU.add, ALU.mult)
            last.then_inc(sem.qT_kept, 1)
            dve.wait_ge(sem.wkT_done, 1)
            v.tensor_copy(t.wkT[:, :, :], ps[:, 2:4, 0:D]).then_inc(sem.wkT_kept, 1)
            dve.wait_ge(sem.qT_kept, 1)
            dve.wait_ge(sem.consts_built, 1)
            for c in range(C):
                last = v.tensor_tensor(t.qb[:, c], t.qT[:, c].unsqueeze(1).to_broadcast([P, HC, NQ]),
                                       keep.hmask[:, :, :], ALU.mult)
            last.then_inc(sem.qb_built, 1)
            dve.wait_ge(sem.mk_done, 1)
            v.tensor_copy(t.ccol[:, :], ps[:, 5, 0:2])
            dve.wait_ge(sem.mk_hi, 1)
            v.tensor_tensor(t.mk_lo[:, :, :], ps[:, 4, :].rearrange("p (c q) -> p c q", c=C), t.mk_hi[:, :, :],
                            ALU.subtract).then_inc(sem.mk_kept, 1)
            dve.wait_ge(sem.mk_kept, 1)

            def stats_x(b, s, count):
                dve.wait_ge(x_loaded[s], 16 * count)
                for j in range(T):
                    last = v.bn_stats(t.x_st[:, j], t.xt[:, s, j])
                last.then_inc(sem.x_stats, 1)
                dve.wait_ge(sem.x_stats, b + 1)
                alone(dve, sem.dve_passed)
                for j in range(T):
                    last = v.bn_aggr(t.x_mv[:, j], t.x_st[:, j])
                last.then_inc(sem.x_mv, 1)
                dve.wait_ge(sem.x_mv, b + 1)
                if after_first(b):
                    dve.wait_ge(sem.n_ready, 2 * b)
                v.tensor_scalar(t.x_v[:, 0], t.x_mv[:, :, 1], EPS, None, ALU.add)
                v.tensor_scalar(t.x_v[:, 1], t.x_mv[:, :, 0], -1.0, None, ALU.mult).then_inc(sem.x_var, 1)

            def keep_lo(dst, hi, group, h, hi_sem, n, out_sem):
                dve.wait_ge(hi_sem, n)
                half = slice(h * HS, (h + 1) * HS)
                v.tensor_tensor(dst[:, :, half], ps[:, group:group + 2, :], hi[:, :, half], ALU.subtract) \
                    .then_inc(out_sem, 1)

            def body(i, s, k):
                o = 1 - s
                if live(i):
                    for h in range(2):
                        keep_lo(t.nT_lo, t.nT_hi, (G0, G1)[h], h, sem.tn_hi, 2 * i + h + 1, sem.tn_lo)
                if live(i - 2):
                    b = i - 2
                    dve.wait_ge(sem.mt_done, b + 1)
                    v.tensor_reduce(t.mcol[:, :], ps[:, 0, 0:2 * P].rearrange("p (c n) -> p c n", c=2), AX, ALU.max) \
                        .then_inc(sem.mt_red, 1)
                    dve.wait_ge(sem.mt_red, b + 1)
                    v.tensor_tensor(t.mcol2[:, :], t.mcol[:, :], t.ccol[:, :], ALU.add).then_inc(sem.mt_sum, 1)
                    dve.wait_ge(sem.mt_sum, b + 1)
                    v.tensor_tensor(t.mcolp[:, :, 0:64:32], t.ccol[:, :].unsqueeze(2).to_broadcast([P, 2, 2]),
                                    t.mcol2[:, :].unsqueeze(2).to_broadcast([P, 2, 2]), ALU.subtract) \
                        .then_inc(sem.mt_kept, 1)
                if live(i - 1):
                    for h in range(2):
                        if h == 1 and live(i - 2):
                            guard_row(i - 2)
                        dve.wait_ge(sem.x1_ready, 2 * i + h - 1)
                        for j in range(h * HT, (h + 1) * HT):
                            last = v.bn_stats(t.x1_st[:, j], t.xt[:, o, j])
                    last.then_inc(sem.x1_stats, 1)
                    dve.wait_ge(sem.x1_stats, i)
                    alone(dve, sem.dve_passed)
                    for j in range(T):
                        last = v.bn_aggr(t.x1_mv[:, j], t.x1_st[:, j])
                    last.then_inc(sem.x1_mv, 1)
                    dve.wait_ge(sem.x1_mv, i)
                    if live(i - 2) and after_first(i - 1):
                        dve.wait_ge(sem.n2_ready, i - 1)
                    if live(i - 3):
                        dve.wait_ge(sem.st_stored, 16 * (i - 2))
                    v.tensor_scalar(t.x1_v[:, :], t.x1_mv[:, :, 1], EPS, None, ALU.add)
                    v.tensor_scalar(t.x1_n[:, o, 1], t.x1_mv[:, :, 0], -1.0, None, ALU.mult).then_inc(sem.x1_var, 1)
                elif live(i - 2):
                    guard_row(i - 2)
                if live(i):
                    for m in range(4):
                        e, h = m % 2, m // 2
                        bank = (G1, G0)[m % 2]
                        half = slice(h * HS, (h + 1) * HS)
                        dve.wait_ge(sem.z_sig, 4 * i + m + 1)
                        v.scalar_tensor_tensor(t.hT[:, e, half], ps[:, bank + 1, :], t.bh[:, e:e + 1], t.z[:, m % 2],
                                               ALU.add, ALU.mult).then_inc(sem.b_made, 1)
                        dve.wait_ge(sem.b_made, 4 * i + m + 1)
                        dve.wait_ge(sem.a_sig, 4 * i + m + 1)
                        if h:
                            dve.wait_ge(sem.h_scanned, 4 * i + m - 1)
                        v.tensor_tensor_scan(t.hT[:, e, half], t.a[:, e, half], t.hT[:, e, half],
                                             t.hT[:, e, HS - 1:HS] if h else 0.0, ALU.mult, ALU.add) \
                            .then_inc(sem.h_scanned, 1)
                if live(i - 2):
                    dve.wait_ge(sem.u_done, i - 1)
                    if after_first(i - 2):
                        dve.wait_ge(sem.u_kept, i - 2)
                    v.reciprocal(t.rcp[:, :].unsqueeze(2), ps[:, G1:G1 + 2, D:D + 1]).then_inc(sem.u_rcp, 1)
                if live(i + 1):
                    stats_x(i + 1, o, k + s + 1)
                if live(i - 1):
                    for h in range(2):
                        keep_lo(t.n2T_lo, t.n2T_hi, (G0, G1)[h], h, sem.t2_hi, 2 * i + h - 1, sem.t2_lo)
                if live(i):
                    for h in range(2):
                        n = 2 * i + h
                        dve.wait_ge(sem.th_done, n + 1)
                        for j in range(HT):
                            last = v.bn_stats(t.h_st[:, j], ps[:, (G0, G1)[h] + j // 2, (j % 2) * D:(j % 2 + 1) * D])
                        last.then_inc(sem.th_stats, 1)
                        dve.wait_ge(sem.th_stats, n + 1)
                        alone(dve, sem.dve_passed)
                        for j in range(HT):
                            last = v.bn_aggr(t.h_mv[:, j], t.h_st[:, j])
                        last.then_inc(sem.th_mv, 1)
                        dve.wait_ge(sem.th_mv, n + 1)
                        if h == 1 or after_first(i):
                            dve.wait_ge(sem.th_norm, n)
                        v.tensor_scalar(t.h_v[:, 0], t.h_mv[:, :, 1], EPS, None, ALU.add)
                        v.tensor_scalar(t.h_v[:, 1], t.h_mv[:, :, 0], -1.0, None, ALU.mult).then_inc(sem.th_var, 1)
                if live(i - 1):
                    dve.wait_ge(sem.s_done, i)
                    v.tensor_reduce(t.mx[:, :], s_all.rearrange("p (j q) -> p q j", q=HQ), AX, ALU.max) \
                        .then_inc(sem.s_max, 1)

            def guard_row(b):
                dve.wait_ge(sem.mr_done, b + 1)
                if after_first(b):
                    dve.wait_ge(sem.ga_done, b)
                v.tensor_copy(t.grow_t[32:64, :], ps[32:64, 0, D:2 * D]).then_inc(sem.mr_hi, 1)
                v.tensor_copy(t.grow[0:32, :], ps[0:32, 0, D:2 * D])
                dve.wait_ge(sem.mr_hi, b + 1)
                v.tensor_tensor(t.grow[32:64, :], ps[32:64, 0, D:2 * D], t.grow_t[32:64, :], ALU.subtract) \
                    .then_inc(sem.mr_kept, 1)

            stats_x(0, 0, 1)
            rows(dve, body)

        @block.tensor
        def _(pe):
            mm, tr = nc.tensor.matmul, nc.tensor.transpose
            pe.wait_ge(sem.w_loaded, 16 * 9)
            pe.wait_ge(sem.ident_built, 4)
            for c in range(C):
                last = tr(ps[:, 0, c * NQ:(c + 1) * NQ], t.sq[:, c * P:(c + 1) * P], keep.ident[0:NQ, 0:NQ])
            last.then_inc(sem.sqT_done, 1)
            for f in range(C):
                for c in range(C):
                    last = tr(ps[:, 2 + f, c * P:(c + 1) * P], wk[:, c, f * P:(f + 1) * P], keep.ident[:, :])
            last.then_inc(sem.wkT_done, 1)
            pe.wait_ge(sem.sqT_kept, 1)
            for f in range(C):
                for c in range(C):
                    last = mm(ps[:, 1, f * NQ:(f + 1) * NQ], wq[:, c, f * P:(f + 1) * P], t.sqT[:, c],
                              start=(c == 0), stop=(c == C - 1))
            last.then_inc(sem.qT_done, 1)
            pe.wait_ge(sem.qb_built, 1)
            pe.wait_ge(sem.wkT_kept, 1)
            for f in range(C):
                qb = t.qb[:, f].rearrange("p h q -> p (h q)")
                for c in range(C):
                    mm(ps[:, 4, c * HQ + f * P:c * HQ + (f + 1) * P], t.wkT[:, f, c * P:(c + 1) * P], qb,
                       start=True, stop=True)
                last = mm(ps[:, 5, f:f + 1], qb, t.bk[:, f:f + 1], start=True, stop=True)
            last.then_inc(sem.mk_done, 1)
            pe.wait_ge(sem.split_w, 4)
            pe.wait_ge(sem.mk_kept, 1)

            def transposed(src, group, h):
                for j in range(HT):
                    for c in range(C):
                        last = tr(ps[:, group + c, j * P:(j + 1) * P], src[:, h * HT + j, c * P:(c + 1) * P],
                                  keep.ident[:, :])
                return last

            def projections(i, m):
                e, h = m % 2, m // 2
                bank = (G1, G0)[m % 2]
                half = slice(h * HS, (h + 1) * HS)
                for k, (hi, lo) in enumerate(((t.wz_hi, t.wz_lo), (t.wh_hi, t.wh_lo))):
                    for c in range(C):
                        last = three_passes(nc, ps[:, bank + k, :], hi[:, c, e * P:(e + 1) * P],
                                            lo[:, c, e * P:(e + 1) * P], t.nT_hi[:, c, half], t.nT_lo[:, c, half],
                                            c == 0, c == C - 1)
                last.then_inc(sem.zh_done, 1)

            def body(i, s, k):
                o = 1 - s
                if live(i):
                    for h in range(2):
                        pe.wait_ge(sem.n_ready, 2 * i + h + 1)
                        if after_first(i):
                            pe.wait_ge(sem.y_ready, 2 * i + h - 1)
                        transposed(t.n, (G0, G1)[h], h).then_inc(sem.tn_done, 1)
                    pe.wait_ge(sem.tn_lo, 2 * i + 1)
                elif live(i - 1):
                    pe.wait_ge(sem.y_ready, 2 * i)
                if live(i - 3):
                    pe.wait_ge(sem.u_kept, i - 2)
                    if after_first(i - 3):
                        pe.wait_ge(sem.ut_kept, i - 3)
                    for c in range(C):
                        for m in range(2):
                            last = tr(ps[:, 1, c * HQ + m * P:c * HQ + (m + 1) * P], t.u[:, m, c * P:(c + 1) * P],
                                      keep.ident[:, :])
                    last.then_inc(sem.tu_done, 1)
                if live(i - 2):
                    pe.wait_ge(sem.s_max, i - 1)
                    for c in range(2):
                        last = tr(ps[:, 0, c * P:(c + 1) * P], t.mx[:, c * P:(c + 1) * P], keep.ident[:, :])
                    last.then_inc(sem.mt_done, 1)
                if live(i):
                    pe.wait_ge(sem.tn_lo, 2 * i + 2)
                    projections(i, 0)
                if live(i - 2):
                    pe.wait_ge(sem.mt_kept, i - 1)
                    for c in range(2):
                        last = mm(ps[0:64, 0, D + c * P:D + (c + 1) * P], t.mcolp[:, c], keep.ident[:, :],
                                  start=True, stop=True)
                    last.then_inc(sem.mr_done, 1)
                    pe.wait_ge(sem.mr_kept, i - 1)
                    for k in range(4):
                        last = mm(ps[:, 4 + k, :], keep.selrow[:, :],
                                  t.grow[:, :].unsqueeze(1).to_broadcast([P, 2, HQ]),
                                  start=False, stop=True, skip_group_check=True)
                    last.then_inc(sem.ga_done, 1)
                if live(i):
                    if live(i - 3):
                        pe.wait_ge(sem.ut_kept, i - 2)
                    projections(i, 1)
                    for m in (2, 3):
                        pe.wait_ge(sem.b_made, 4 * i + m - 1)
                        pe.wait_ge(sem.a_sig, 4 * i + m - 1)
                        projections(i, m)
                if live(i - 2):
                    pe.wait_ge(sem.p_ready, i - 1)
                    if live(i):
                        pe.wait_ge(sem.b_made, 4 * i + 3)
                        pe.wait_ge(sem.a_sig, 4 * i + 3)
                    for m in range(2):
                        for j in range(T):
                            last = mm(ps[:, G1 + m, 0:D + 1], t.pT[:, j, m * P:(m + 1) * P], t.n2[:, s, j, 0:D + 1],
                                      start=(j == 0), stop=(j == T - 1))
                    last.then_inc(sem.u_done, 1)
                if live(i - 1):
                    pe.wait_ge(sem.n2_ready, i)
                    if live(i):
                        pe.wait_ge(sem.b_made, 4 * i + 4)
                        pe.wait_ge(sem.a_sig, 4 * i + 4)
                    elif live(i - 3):
                        pe.wait_ge(sem.ut_kept, i - 2)
                    transposed(t.n2[:, o], G0, 0).then_inc(sem.t2_done, 1)
                    if live(i - 2):
                        pe.wait_ge(sem.u_kept, i - 1)
                    transposed(t.n2[:, o], G1, 1).then_inc(sem.t2_done, 1)
                if live(i):
                    for h in range(2):
                        pe.wait_ge(sem.h_scanned, 4 * i + 2 * h + 2)
                        if live(i - 1):
                            pe.wait_ge(sem.t2_lo, 2 * i + h - 1)
                        else:
                            pe.wait_ge(sem.b_made, 4 * i + 4)
                            pe.wait_ge(sem.a_sig, 4 * i + 4)
                        for j in range(HT):
                            for c in range(C):
                                at = (j % 2) * D + c * P
                                last = tr(ps[:, (G0, G1)[h] + j // 2, at:at + P],
                                          t.hT[:, c, (h * HT + j) * P:(h * HT + j + 1) * P], keep.ident[:, :])
                        last.then_inc(sem.th_done, 1)
                if live(i - 1):
                    pe.wait_ge(sem.t2_lo, 2 * i)
                    if live(i - 2):
                        pe.wait_ge(sem.p_ready, i - 1)
                    for j in range(T):
                        for c in range(C):
                            last = three_passes(nc, s_tile[:, j], t.n2T_hi[:, c, j * P:(j + 1) * P],
                                                t.n2T_lo[:, c, j * P:(j + 1) * P], t.mk_hi[:, c], t.mk_lo[:, c],
                                                j % 2 == 0 and c == 0, c == C - 1, skip=True)
                    last.then_inc(sem.s_done, 1)

            rows(pe, body)


def expert_phase(nc, ctx, sem, ps, keep, o2, slot_query, d_Wv, d_Wo, d_bv, d_bo,
                 e_ln_g, e_ln_b, e_W1, e_b1, e_Wg, e_bg, e_W2, e_b2):
    TT = NQ * B // P
    QT = NQ // TT
    GH = 4
    NG = H // GH
    t = tensors(nc, ctx, "expert", [
        ("wv", [P, C, D], F32), ("wvp", [P, C, H, 32], F32),
        ("wop", [P, NG, D], F32), ("bvp", [P, NG], F32),
        ("ao", [P, NG, NQ * B], F32),
        ("sqb", [64, D], F32),
        ("ln_g", [NQ, D], F32), ("ln_b", [NQ, D], F32),
        ("spread", [64, NQ, B], F32),
        ("o", [P, TT, D], F32), ("oln", [P, TT, D], F32),
        ("o_st", [P, TT, 6], F32), ("o_mv", [P, TT, 2], F32), ("o_v", [P, 2, TT], F32), ("o_r", [P, TT], F32),
        ("hT", [P, C, NQ * B], F32), ("oT", [P, C, NQ * B], F32),
        ("b1", [P, F], F32), ("bg", [P, F], F32), ("eb2", [E, D], F32), ("b2T", [P, C, E], F32),
        ("xe", [P, 2, C, 32], F32), ("sel", [P, 2, 32], F32),
        ("sg", [P, 2, 512], F32), ("hg", [P, 2, D], F32), ("hgT", [P, 2, D], F32), ("ye", [32, 2, D], F32),
    ] + [(f"{w}_{k}", [P, a, n], F32) for k in range(1, SLOTS) for w, a, n in (("w1", C, F), ("wg", C, F), ("w2", FK, D))])
    w1 = [keep.w1_0, t.w1_1, t.w1_2, t.w1_3]
    wg = [keep.wg_0, t.wg_1, t.wg_2, t.wg_3]
    w2 = [keep.w2_0, t.w2_1, t.w2_2, t.w2_3]
    arrived = [sem.ew0, sem.ew1, sem.ew2, sem.ew3]

    def expert(ap, e, rule):
        return ap[bass.ds(e, 1)].rearrange(rule, p=P)

    with nc.Block() as block:

        @block.sync
        def _(sp):
            sp.wait_ge(sem.wvp_built, 1)
            sp.dma_start(t.wv[:, :, :], d_Wv.rearrange("(c p) n -> p c n", p=P)).then_inc(sem.slot_w, 16)
            for j in range(GH):
                lane = slice(32 * j, 32 * j + DH)
                sp.dma_start(t.wop[lane, :, :], d_Wo.rearrange("(g j k) n -> j k g n", j=GH, k=DH)[j]) \
                    .then_inc(sem.slot_small, 16)
                sp.dma_start(t.bvp[lane, :], d_bv.rearrange("(g j k) -> j k g", j=GH, k=DH)[j],
                             allow_slow_non_contiguous=True) \
                    .then_inc(sem.slot_small, 16)
            sp.dma_start(t.sqb[0:NQ, :], slot_query[0]).then_inc(sem.slot_small, 16)
            sp.dma_start(t.sqb[32:33, :], d_bo.unsqueeze(0)).then_inc(sem.slot_small, 16)
            sp.dma_start(t.ln_g[:, :], e_ln_g).then_inc(sem.slot_small, 16)
            sp.dma_start(t.ln_b[:, :], e_ln_b).then_inc(sem.slot_small, 16)
            for dst, src in ((t.b1, e_b1), (t.bg, e_bg), (t.eb2, e_b2)):
                sp.dma_start(dst[0:E, :], src).then_inc(sem.slot_small, 16)

            def load(e, k):
                sp.dma_start(w1[k][:, :, :], expert(e_W1, e, "o (c p) f -> p (o c) f")).then_inc(arrived[k], 16)
                sp.dma_start(wg[k][:, :, :], expert(e_Wg, e, "o (c p) f -> p (o c) f")).then_inc(arrived[k], 16)
                sp.dma_start(w2[k][:, :, :], expert(e_W2, e, "o (k p) d -> p (o k) d")).then_inc(arrived[k], 16)

            for k in range(1, SLOTS):
                load(k, k)
            with sp.Fori(1, E // SLOTS) as r:
                for k in range(SLOTS):
                    sp.wait_ge(sem.y_done, SLOTS * r - SLOTS + k + 1)
                    alone(sp, sem.sp_passed)
                    load(SLOTS * r + k, k)

        @block.gpsimd
        def _(pool):
            g = nc.gpsimd
            g.memset(t.wop[:, :, :], 0.0)
            g.memset(t.sqb[:, :], 0.0)
            g.memset(t.bvp[:, :], 0.0)
            g.memset(t.b1[:, :], 0.0)
            g.memset(t.bg[:, :], 0.0)
            g.memset(t.wvp[:, :, :, :], 0.0)
            g.memset(t.xe[:, :, :, :], 0.0)
            g.memset(t.sel[:, :, :], 0.0).then_inc(sem.wvp_built, 1)
            pool.wait_ge(sem.o_var, 1)
            g.tensor_tensor(t.o_r[:, :], t.o_v[:, 0], keep.mhalf[:, 0:TT], ALU.pow).then_inc(sem.o_pow, 1)

        @block.vector
        def _(dve):
            v = nc.vector
            v.memset(t.spread[:, :, :], 0.0).then_inc(sem.spread_made, 1)
            dve.wait_ge(sem.spread_made, 1)
            v.memset(t.spread[32:33, :, :], 1.0).then_inc(sem.spread_made, 1)
            v.tensor_copy(t.spread[0:NQ, :, :], keep.ident[0:NQ, 0:NQ].unsqueeze(2).to_broadcast([NQ, NQ, B])) \
                .then_inc(sem.spread_made, 1)
            dve.wait_ge(sem.slot_w, 16)
            v.tensor_copy(t.wvp[:, :, :, 0:DH], t.wv[:, :, :].rearrange("p c (h k) -> p c h k", k=DH)) \
                .then_inc(sem.wvp_built, 1)
            dve.wait_ge(sem.slot_small, 16 * 15)
            dve.wait_ge(sem.ao_done, 1)
            for g in range(NG):
                last = v.tensor_scalar(t.ao[:, g], ps[:, g // 2, (g % 2) * D:(g % 2 + 1) * D], t.bvp[:, g:g + 1],
                                       None, ALU.add)
            last.then_inc(sem.ao_kept, 1)
            dve.wait_ge(sem.b2t_done, 1)
            v.tensor_copy(t.b2T[:, :, :], ps[:, 6, 0:C * E].rearrange("p (c e) -> p c e", c=C)).then_inc(sem.b2t_kept, 1)
            dve.wait_ge(sem.o_done, 1)
            v.tensor_copy(t.o[:, :, :], ps[:, 4:4 + TT, 0:D]).then_inc(sem.o_kept, 1)
            dve.wait_ge(sem.o_kept, 1)
            for m in range(TT):
                last = v.bn_stats(t.o_st[:, m], t.o[:, m])
            last.then_inc(sem.o_stats, 1)
            dve.wait_ge(sem.o_stats, 1)
            alone(dve, sem.dve_passed)
            for m in range(TT):
                last = v.bn_aggr(t.o_mv[:, m], t.o_st[:, m])
            last.then_inc(sem.o_mv, 1)
            dve.wait_ge(sem.o_mv, 1)
            v.tensor_scalar(t.o_v[:, 0], t.o_mv[:, :, 1], EPS, None, ALU.add)
            v.tensor_scalar(t.o_v[:, 1], t.o_mv[:, :, 0], -1.0, None, ALU.mult).then_inc(sem.o_var, 1)
            dve.wait_ge(sem.o_pow, 1)
            dve.wait_ge(sem.o_var, 1)
            for m in range(TT):
                last = v.tensor_scalar(t.oln[:, m], t.o[:, m], t.o_v[:, 1, m:m + 1], t.o_r[:, m:m + 1],
                                       ALU.add, ALU.mult)
            last.then_inc(sem.o_centred, 1)
            dve.wait_ge(sem.o_centred, 1)
            v.tensor_tensor(t.oln[:, :, :], t.oln[:, :, :], ps[:, 2, :].rearrange("p (m d) -> p m d", d=D), ALU.mult).then_inc(sem.o_scaled, 1)
            dve.wait_ge(sem.o_scaled, 1)
            v.tensor_tensor(t.oln[:, :, :], t.oln[:, :, :], ps[:, 3, :].rearrange("p (m d) -> p m d", d=D), ALU.add).then_inc(sem.o_ln, 1)
            dve.wait_ge(sem.ot_done, 1)
            v.tensor_copy(t.hT[:, :, :], ps[:, 6, :].rearrange("p (c n) -> p c n", c=C))
            dve.wait_ge(sem.b2t_kept, 1)
            for c in range(C):
                last = v.tensor_tensor(t.oT[:, c].rearrange("p (q b) -> p q b", b=B),
                                       ps[:, 7, c * NQ * B:(c + 1) * NQ * B].rearrange("p (q b) -> p q b", b=B),
                                       t.b2T[:, c].unsqueeze(2).to_broadcast([P, NQ, B]), ALU.add)
            last.then_inc(sem.ot_kept, 1)
            dve.wait_ge(sem.ot_kept, 1)

            def finish_expert(r, k, fresh):
                e, q = SLOTS * r + k, k % 2
                if not fresh:
                    dve.wait_ge(sem.ug_done, e - 1)
                v.tensor_copy(t.xe[:, q, :, 0:B], t.hT[:, :, bass.ds(e * B, B)])
                v.tensor_copy(t.sel[0:E, q, 0:B], keep.ident[0:E, bass.ds(e, 1)].to_broadcast([E, B])) \
                    .then_inc(sem.xe_made, 1)
                dve.wait_ge(sem.ug_silu, e + 1)
                v.tensor_tensor(t.hg[:, q], t.sg[:, q, 0:D], t.sg[:, q, D:2 * D], ALU.mult).then_inc(sem.hg_made, 1)
                dve.wait_ge(sem.hgt_done, e + 1)
                if not fresh:
                    dve.wait_ge(sem.y_done, e - 1)
                v.tensor_copy(t.hgT[:, q], ps[:, 2 + q, 0:D]).then_inc(sem.hgt_kept, 1)
                dve.wait_ge(sem.y_done, e + 1)
                v.tensor_copy(t.ye[:, q], ps[0:32, 4 + q, 0:D]).then_inc(sem.y_kept, 1)
                dve.wait_ge(sem.yt_done, e + 1)
                v.tensor_tensor(o2.o2T[:, :, bass.ds(e * B, B)], t.oT[:, :, bass.ds(e * B, B)],
                                ps[:, 6 + q, 0:64].rearrange("p (c n) -> p c n", c=C)[:, :, 0:B], ALU.add) \
                    .then_inc(sem.o2_made, 1)

            for k in range(SLOTS):
                finish_expert(0, k, k < 2)
            with dve.Fori(1, E // SLOTS) as r:
                for k in range(SLOTS):
                    finish_expert(r, k, False)

        @block.scalar
        def _(act):
            a = nc.scalar

            def round_(r, first):
                for k in range(SLOTS):
                    e, q = SLOTS * r + k, k % 2
                    act.wait_ge(sem.ug_done, e + 1)
                    if not (first and k < 2):
                        act.wait_ge(sem.hg_made, e - 1)
                    a.activation(t.sg[:, q], ps[:, q, :], ACT.Silu).then_inc(sem.ug_silu, 1)

            round_(0, True)
            with act.Fori(1, E // SLOTS) as r:
                round_(r, False)

        @block.tensor
        def _(pe):
            mm, tr = nc.tensor.matmul, nc.tensor.transpose
            pe.wait_ge(sem.wvp_built, 2)
            for g in range(NG):
                for c in range(C):
                    for j in range(GH):
                        h = GH * g + j
                        last = mm(ps[32 * j:32 * j + 32, g // 2, (g % 2) * D:(g % 2 + 1) * D], t.wvp[:, c, h],
                                  keep.UT[:, c, h * NQ:(h + 1) * NQ, :].rearrange("p q b -> p (q b)"),
                                  start=(c == 0), stop=(c == C - 1), skip_group_check=True)
            last.then_inc(sem.ao_done, 1)
            pe.wait_ge(sem.slot_small, 16 * 15)
            for c in range(C):
                last = tr(ps[:, 6, c * E:(c + 1) * E], t.eb2[:, c * P:(c + 1) * P], keep.ident[0:E, 0:E])
            last.then_inc(sem.b2t_done, 1)
            pe.wait_ge(sem.spread_made, 3)
            for m in range(TT):
                spread = t.spread[:, m * QT:(m + 1) * QT, :].rearrange("q s b -> q (s b)")
                for bank, rows in ((2, t.ln_g), (3, t.ln_b)):
                    mm(ps[:, bank, m * D:(m + 1) * D], spread[0:NQ], rows[:, :], start=True, stop=True)
                mm(ps[:, 4 + m, 0:D], spread, t.sqb[:, :], start=True, stop=False)
            pe.wait_ge(sem.ao_kept, 1)
            for m in range(TT):
                for g in range(NG):
                    last = mm(ps[:, 4 + m, 0:D], t.ao[:, g, m * P:(m + 1) * P], t.wop[:, g],
                              start=False, stop=(g == NG - 1))
            last.then_inc(sem.o_done, 1)
            pe.wait_ge(sem.o_ln, 1)
            pe.wait_ge(sem.b2t_kept, 1)
            for m in range(TT):
                for c in range(C):
                    tr(ps[:, 6, c * NQ * B + m * P:c * NQ * B + (m + 1) * P], t.oln[:, m, c * P:(c + 1) * P],
                       keep.ident[:, :])
                    last = tr(ps[:, 7, c * NQ * B + m * P:c * NQ * B + (m + 1) * P], t.o[:, m, c * P:(c + 1) * P],
                              keep.ident[:, :])
            last.then_inc(sem.ot_done, 1)

            def up(e, k, r, fresh):
                q = k % 2
                pe.wait_ge(sem.xe_made, e + 1)
                pe.wait_ge(arrived[k], 48 * (r + 1))
                if not fresh:
                    pe.wait_ge(sem.ug_silu, e - 1)
                for n, (w, bias) in enumerate(((w1[k], t.b1), (wg[k], t.bg))):
                    for c in range(C + 1):
                        for j in range(4):
                            cols = slice(j * D, (j + 1) * D)
                            lhs = t.xe[:, q, c] if c < C else t.sel[:, q]
                            rhs = w[:, c, cols] if c < C else bias[:, cols]
                            last = mm(ps[32 * j:32 * j + 32, q, n * D:(n + 1) * D], lhs, rhs,
                                      start=(c == 0), stop=(c == C), skip_group_check=True)
                last.then_inc(sem.ug_done, 1)

            def down(e, k, fresh):
                q = k % 2
                pe.wait_ge(sem.hg_made, e + 1)
                if not fresh:
                    pe.wait_ge(sem.hgt_kept, e - 1)
                for n in range(2):
                    last = tr(ps[:, 2 + q, n * P:(n + 1) * P], t.hg[:, q, n * P:(n + 1) * P], keep.ident[:, :])
                last.then_inc(sem.hgt_done, 1)
                pe.wait_ge(sem.hgt_kept, e + 1)
                if not fresh:
                    pe.wait_ge(sem.y_kept, e - 1)
                for f in range(FK):
                    j, n = f // 2, f % 2
                    last = mm(ps[0:32, 4 + q, 0:D], t.hgT[:, q, n * P + 32 * j:n * P + 32 * j + 32], w2[k][:, f],
                              start=(f == 0), stop=(f == FK - 1))
                last.then_inc(sem.y_done, 1)
                pe.wait_ge(sem.y_kept, e + 1)
                if not fresh:
                    pe.wait_ge(sem.o2_made, e - 1)
                alone(pe, sem.pe_passed)
                for c in range(C):
                    last = tr(ps[:, 6 + q, 32 * c:32 * c + 32], t.ye[:, q, c * P:(c + 1) * P], keep.ident[0:32, 0:32])
                last.then_inc(sem.yt_done, 1)

            pe.wait_ge(sem.ot_kept, 1)
            for k in range(SLOTS):
                up(k, k, 0, k < 2)
                down(k, k, k < 2)
            with pe.Fori(1, E // SLOTS) as r:
                for k in range(SLOTS):
                    up(SLOTS * r + k, k, r, False)
                    down(SLOTS * r + k, k, False)


def combine_phase(nc, ctx, sem, ps, keep, o2, c_Wq, c_Wk, c_Wv, c_Wo, c_bq, c_bk, c_bv, c_bo,
                  x1_dram, st_dram, out):
    GA, GB, GC, GD = 0, 2, 4, 6
    TOK = NQ * B
    t = tensors(nc, ctx, "combine", [
        ("xc", [P, ROWS, T, D], F32), ("nrm", [P, ROWS, 2, T], F32),
        ("wq", [P, C, D], F32), ("wk", [P, C, D], F32), ("wv", [P, C, D], F32), ("wo", [P, C, D], F32),
        ("bq", [P, C], F32), ("bk", [P, C], F32), ("bv", [P, C], F32), ("bo_rep", [P, D], F32),
        ("khT", [P, C, TOK], F32), ("vhT", [P, C, TOK], F32), ("wqT", [P, C, D], F32),
        ("bqp", [P, C, 64], F32),
        ("kb", [P, C, HC, NQ], F32), ("vb", [P, C, HC, NQ], F32),
        ("m_hi", [P, C, HQ], F32R), ("m_lo", [P, C, HQ], F32R),
        ("nv", [P, 2, C, D], F32),
        ("crow", [P, HQ], F32R), ("crow_t", [64, HQ], F32R),
        ("n2", [P, T, D], F32), ("n2T_hi", [P, C, S], F32R), ("n2T_lo", [P, C, S], F32R),
        ("p", [P, 2, T * H, NQ], F32),
        ("mx", [P, 2, HT * H], F32), ("sm", [P, 2, HT * H], F32), ("rc", [P, 2, HT * H], F32),
        ("pT", [P, C, S], F32),
        ("o_st", [P, HT, 6], F32), ("o_mv", [P, HT, 2], F32), ("o_v", [P, 2, HT], F32), ("o_r", [P, 2, 2, HT], F32),
        ("y", [P, T, D], F32),
    ])
    rows_loaded = (sem.c_rows0, sem.c_rows1, sem.c_rows2, sem.c_rows3)

    def rows(e, body):
        for i in range(-1, 4):
            body(i, i % ROWS, i // ROWS)
        with e.Fori(1, B // ROWS - 1) as k:
            for s in range(ROWS):
                body(ROWS * k + s, s, k)
        for i in range(B - ROWS, B + 2):
            body(i, i % ROWS, i // ROWS)

    with nc.Block() as block:

        @block.sync
        def _(sp):
            for dst, src in ((t.wk, c_Wk), (t.wv, c_Wv), (t.wq, c_Wq), (t.wo, c_Wo)):
                sp.dma_start(dst[:, :, :], src.rearrange("(c p) n -> p c n", p=P)).then_inc(sem.c_w, 16)
            for dst, src in ((t.bq, c_bq), (t.bk, c_bk), (t.bv, c_bv)):
                sp.dma_start(dst[:, :], src.rearrange("(c p) -> p c", p=P), allow_slow_non_contiguous=True) \
                    .then_inc(sem.c_w, 16)
            sp.dma_start(t.bo_rep[:, :], c_bo.unsqueeze(0).to_broadcast([P, D])).then_inc(sem.c_w, 16)

            def load(b, s):
                sp.dma_start(t.xc[:, s].rearrange("p j d -> p (j d)"), row(x1_dram, b)).then_inc(rows_loaded[s], 16)
                sp.dma_start(t.nrm[:, s].rearrange("p a j -> p (a j)"), row(st_dram, b)).then_inc(rows_loaded[s], 16)

            load(0, 0)
            load(1, 1)

            def body(i, s, k):
                if live(i - 2):
                    sp.wait_ge(sem.oc_added, i - 1)
                    alone(sp, sem.sp_passed)
                    if after_first(i - 2):
                        sp.wait_ge(sem.oc_stored, 16 * (i - 2))
                    alone(sp, sem.sp_passed)
                    sp.dma_start(out[bass.ds(i - 2, 1)].rearrange("o (j p) d -> p (o j) d", p=P),
                                 t.xc[:, (s - 2) % ROWS]).then_inc(sem.oc_stored, 16)
                if live(i + 2) and not (isinstance(i, int) and i < 0):
                    if live(i - 2):
                        sp.wait_ge(sem.oc_stored, 16 * (i - 1))
                    alone(sp, sem.sp_passed)
                    load(i + 2, (s + 2) % ROWS)

            rows(sp, body)
            sp.wait_ge(sem.oc_stored, 16 * B)

        @block.gpsimd
        def _(pool):
            g = nc.gpsimd
            g.memset(t.bqp[:, :, :], 0.0).then_inc(sem.bqp_made, 1)
            pool.wait_ge(sem.kv_kept, 2)

            def body(i, s, k):
                if live(i + 1):
                    q = (s + 1) % ROWS
                    turn = (k if s < ROWS - 1 else k + 1) + 1
                    pool.wait_ge(rows_loaded[q], 32 * turn)
                    if not (isinstance(i, int) and i < 0):
                        pool.wait_ge(sem.t3_done, 2 * i + 2)
                    alone(pool, sem.pool_passed)
                    for j in range(T):
                        last = g.tensor_scalar(t.n2[:, j], t.xc[:, q, j], t.nrm[:, q, 1, j:j + 1],
                                               t.nrm[:, q, 0, j:j + 1], ALU.add, ALU.mult)
                    last.then_inc(sem.n2c_ready, 1)
                    if not (isinstance(i, int) and i < 0):
                        pool.wait_ge(sem.mn_done, i + 1)
                    for dst, src in ((t.kb, t.khT), (t.vb, t.vhT)):
                        for c in range(C):
                            cols = src[:, c].rearrange("p (k b) -> p b k", b=B)[:, bass.ds(i + 1, 1), :]
                            last = g.tensor_tensor(dst[:, c], cols.to_broadcast([P, HC, NQ]), keep.hmask[:, :, :],
                                                   ALU.mult)
                    last.then_inc(sem.kb_made, 1)
                if live(i - 2):
                    pool.wait_ge(sem.yc_ready, 2 * i - 2)
                    q = (s - 2) % ROWS
                    for h in range(2):
                        half = t.xc[:, q, h * HT:(h + 1) * HT]
                        last = g.tensor_tensor(half, half, t.y[:, h * HT:(h + 1) * HT], ALU.add)
                    last.then_inc(sem.oc_added, 1)
                if live(i):
                    for h in range(2):
                        pool.wait_ge(sem.c_rcp, 2 * i + h + 1)
                        half = t.p[:, s % 2, h * HT * H:(h + 1) * HT * H]
                        g.tensor_tensor(half, half, t.rc[:, h].unsqueeze(2).to_broadcast([P, HT * H, NQ]), ALU.mult) \
                            .then_inc(sem.c_prob, 1)
                if live(i - 1):
                    for h in range(2):
                        n = 2 * i - 2 + h
                        pool.wait_ge(sem.oc_var, n + 1)
                        g.tensor_tensor(t.o_r[:, h, 0], t.o_v[:, 0], keep.mhalf[:, 0:HT], ALU.pow).then_inc(sem.oc_pow, 1)
                        pool.wait_ge(sem.oc_pow, n + 1)
                        g.tensor_tensor(t.o_r[:, h, 1], t.o_v[:, 1], t.o_r[:, h, 0], ALU.mult).then_inc(sem.oc_norm, 1)

            rows(pool, body)

        @block.scalar
        def _(act):
            a = nc.scalar

            def body(i, s, k):
                if live(i):
                    for h, group in enumerate((GA, GB)):
                        act.wait_ge(sem.t3_done, 2 * i + h + 1)
                        if h == 0 and after_first(i):
                            act.wait_ge(sem.sc_done, 2 * i)
                        a.activation(t.n2T_hi[:, :, h * HS:(h + 1) * HS], ps[:, group:group + 2, :], ACT.Copy) \
                            .then_inc(sem.t3_hi, 1)
                if live(i):
                    exp(i, s, 0)
                if live(i - 1):
                    for h, group in enumerate((GA, GB)):
                        act.wait_ge(sem.tp_done, 2 * i - 1 + h)
                        if h == 0 and after_first(i - 1):
                            act.wait_ge(sem.oc_done, 2 * i - 2)
                        a.activation(t.pT[:, :, h * HS:(h + 1) * HS], ps[:, group:group + 2, :], ACT.Copy) \
                            .then_inc(sem.tp_kept, 1)
                if live(i):
                    exp(i, s, 1)
                if live(i - 1):
                    for h, group in enumerate((GA, GC)):
                        act.wait_ge(sem.oc_norm, 2 * i - 1 + h)
                        if h == 0 and after_first(i - 1):
                            act.wait_ge(sem.oc_added, i - 1)
                        for j in range(HT):
                            last = a.activation(t.y[:, h * HT + j], ps[:, group + j // 2, (j % 2) * D:(j % 2 + 1) * D],
                                                ACT.Identity, scale=t.o_r[:, h, 0, j:j + 1],
                                                bias=t.o_r[:, h, 1, j:j + 1])
                        last.then_inc(sem.yc_ready, 1)
                if live(i + 1):
                    act.wait_ge(sem.mn_done, i + 2)
                    a.activation(t.m_hi[:, :, :], ps[:, GB, :].rearrange("p (c q) -> p c q", c=C), ACT.Copy) \
                        .then_inc(sem.m_hi, 1)

            def exp(i, s, h):
                act.wait_ge(sem.c_sub, 2 * i + h + 1)
                half = t.p[:, s % 2, h * HT * H:(h + 1) * HT * H]
                a.activation(half, half, ACT.Exp).then_inc(sem.c_exp, 1)

            rows(act, body)

        @block.vector
        def _(dve):
            v = nc.vector
            dve.wait_ge(sem.c_w, 16 * 8)
            dve.wait_ge(sem.kv_done, 1)
            for bank, dst, bias in ((0, t.khT, t.bk), (1, t.vhT, t.bv)):
                for c in range(C):
                    last = v.tensor_scalar(dst[:, c], ps[:, bank, c * TOK:(c + 1) * TOK], bias[:, c:c + 1], None,
                                           ALU.add)
                last.then_inc(sem.kv_kept, 1)
            dve.wait_ge(sem.wqT_done, 1)
            v.tensor_scalar(t.wqT[:, :, :], ps[:, 4:6, 0:D], KEY_SCALE, None, ALU.mult).then_inc(sem.wqT_kept, 1)
            v.tensor_scalar(t.bo_rep[:, :], t.bo_rep[:, :], 1.0 / H, None, ALU.mult).then_inc(sem.bo_made, 1)
            dve.wait_ge(sem.bqp_made, 1)
            v.tensor_scalar(t.bqp[:, :, 0:64:32], t.bq[:, :].unsqueeze(2).to_broadcast([P, C, 2]), KEY_SCALE, None,
                            ALU.mult)
            v.tensor_copy(t.crow[:, :], keep.zero[:, :]).then_inc(sem.bqp_made, 1)
            dve.wait_ge(sem.bqp_made, 2)
            dve.wait_ge(sem.bo_made, 1)

            def body(i, s, k):
                if live(i):
                    for h, group in enumerate((GA, GB)):
                        dve.wait_ge(sem.t3_hi, 2 * i + h + 1)
                        half = slice(h * HS, (h + 1) * HS)
                        v.tensor_tensor(t.n2T_lo[:, :, half], ps[:, group:group + 2, :], t.n2T_hi[:, :, half],
                                        ALU.subtract).then_inc(sem.t3_lo, 1)
                    for h, group in enumerate((GC, GD)):
                        n = 2 * i + h
                        scores = ps[:, group:group + 2, :].rearrange("p b (g q) -> p (b g) q", q=NQ)
                        dve.wait_ge(sem.sc_done, n + 1)
                        v.tensor_reduce(t.mx[:, h], scores, AX, ALU.max).then_inc(sem.c_max, 1)
                        dve.wait_ge(sem.c_max, n + 1)
                        v.tensor_tensor(t.p[:, s % 2, h * HT * H:(h + 1) * HT * H], scores,
                                        t.mx[:, h].unsqueeze(2).to_broadcast([P, HT * H, NQ]), ALU.subtract) \
                            .then_inc(sem.c_sub, 1)
                    for h in range(2):
                        n = 2 * i + h
                        dve.wait_ge(sem.c_exp, n + 1)
                        v.tensor_reduce(t.sm[:, h], t.p[:, s % 2, h * HT * H:(h + 1) * HT * H], AX, ALU.add) \
                            .then_inc(sem.c_sum, 1)
                        dve.wait_ge(sem.c_sum, n + 1)
                        if after_first(i):
                            dve.wait_ge(sem.c_prob, n - 1)
                        v.reciprocal(t.rc[:, h], t.sm[:, h]).then_inc(sem.c_rcp, 1)
                if live(i - 1):
                    for h, group in enumerate((GA, GC)):
                        n = 2 * i - 2 + h
                        dve.wait_ge(sem.oc_done, n + 1)
                        for j in range(HT):
                            last = v.bn_stats(t.o_st[:, j], ps[:, group + j // 2, (j % 2) * D:(j % 2 + 1) * D])
                        last.then_inc(sem.oc_stats, 1)
                        dve.wait_ge(sem.oc_stats, n + 1)
                        alone(dve, sem.dve_passed)
                        for j in range(HT):
                            last = v.bn_aggr(t.o_mv[:, j], t.o_st[:, j])
                        last.then_inc(sem.oc_mv, 1)
                        dve.wait_ge(sem.oc_mv, n + 1)
                        if h == 1 or after_first(i - 1):
                            dve.wait_ge(sem.oc_norm, n)
                        v.tensor_scalar(t.o_v[:, 0], t.o_mv[:, :, 1], EPS, None, ALU.add)
                        v.tensor_scalar(t.o_v[:, 1], t.o_mv[:, :, 0], -1.0, None, ALU.mult).then_inc(sem.oc_var, 1)
                if live(i + 1):
                    dve.wait_ge(sem.mn_done, i + 2)
                    v.tensor_copy(t.crow_t[32:64, :], ps[32:64, GD, 0:HQ]).then_inc(sem.cr_hi, 1)
                    v.tensor_copy(t.crow[0:32, :], ps[0:32, GD, 0:HQ])
                    v.tensor_tensor(t.nv[:, (s + 1) % 2], ps[:, GB + 1, :].rearrange("p (c d) -> p c d", c=C),
                                    t.bo_rep[:, :].unsqueeze(1).to_broadcast([P, C, D]), ALU.add) \
                        .then_inc(sem.n_kept, 1)
                    dve.wait_ge(sem.cr_hi, i + 2)
                    v.tensor_tensor(t.crow[32:64, :], ps[32:64, GD, 0:HQ], t.crow_t[32:64, :], ALU.subtract) \
                        .then_inc(sem.cr_kept, 1)
                    dve.wait_ge(sem.m_hi, i + 2)
                    v.tensor_tensor(t.m_lo[:, :, :], ps[:, GB, :].rearrange("p (c q) -> p c q", c=C), t.m_hi[:, :, :],
                                    ALU.subtract).then_inc(sem.m_kept, 1)

            rows(dve, body)

        @block.tensor
        def _(pe):
            mm, tr = nc.tensor.matmul, nc.tensor.transpose
            pe.wait_ge(sem.c_w, 16 * 8)
            for bank, w in ((0, t.wk), (1, t.wv)):
                for f in range(C):
                    for c in range(C):
                        last = mm(ps[:, bank, f * TOK:(f + 1) * TOK], w[:, c, f * P:(f + 1) * P], o2.o2T[:, c],
                                  start=(c == 0), stop=(c == C - 1))
            last.then_inc(sem.kv_done, 1)
            for f in range(C):
                for c in range(C):
                    last = tr(ps[:, 4 + f, c * P:(c + 1) * P], t.wq[:, c, f * P:(f + 1) * P], keep.ident[:, :])
            last.then_inc(sem.wqT_done, 1)
            pe.wait_ge(sem.wqT_kept, 1)
            pe.wait_ge(sem.bqp_made, 2)

            def body(i, s, k):
                if live(i):
                    for h, group in enumerate((GA, GB)):
                        if h == 0:
                            pe.wait_ge(sem.n2c_ready, i + 1)
                            if live(i - 2):
                                pe.wait_ge(sem.yc_ready, 2 * i - 3)
                        else:
                            pe.wait_ge(sem.m_kept, i + 1)
                            pe.wait_ge(sem.n_kept, i + 1)
                        for j in range(HT):
                            for c in range(C):
                                last = tr(ps[:, group + c, j * P:(j + 1) * P],
                                          t.n2[:, h * HT + j, c * P:(c + 1) * P], keep.ident[:, :])
                        last.then_inc(sem.t3_done, 1)
                    for h, group in enumerate((GC, GD)):
                        pe.wait_ge(sem.t3_lo, 2 * i + h + 1)
                        if h == 0:
                            pe.wait_ge(sem.cr_kept, i + 1)
                            if live(i - 2):
                                pe.wait_ge(sem.yc_ready, 2 * i - 2)
                        for b in range(2):
                            mm(ps[:, group + b, :], keep.selrow[:, :],
                               t.crow[:, :].unsqueeze(1).to_broadcast([P, 2, HQ]), start=True, stop=False,
                               skip_group_check=True)
                            for jj in range(2):
                                at = slice((h * HT + 2 * b + jj) * P, (h * HT + 2 * b + jj + 1) * P)
                                for c in range(C):
                                    last = three_passes(nc, ps[:, group + b, jj * HQ:(jj + 1) * HQ],
                                                        t.n2T_hi[:, c, at], t.n2T_lo[:, c, at],
                                                        t.m_hi[:, c], t.m_lo[:, c], False, c == C - 1, skip=True)
                        last.then_inc(sem.sc_done, 1)
                if live(i - 1):
                    for h, group in enumerate((GA, GB)):
                        pe.wait_ge(sem.c_prob, 2 * i - 1 + h)
                        if not live(i) and h == 0 and live(i - 2):
                            pe.wait_ge(sem.yc_ready, 2 * i - 2)
                        for j in range(HT):
                            src = t.p[:, (s + 1) % 2, (h * HT + j) * H:(h * HT + j + 1) * H].rearrange("p g q -> p (g q)")
                            for c in range(C):
                                last = tr(ps[:, group + c, j * P:(j + 1) * P], src[:, c * P:(c + 1) * P],
                                          keep.ident[:, :])
                        last.then_inc(sem.tp_done, 1)
                    for h, group in enumerate((GA, GC)):
                        pe.wait_ge(sem.tp_kept, 2 * i - 1 + h)
                        if h == 1 and live(i):
                            pe.wait_ge(sem.c_sub, 2 * i + 1)
                        for j in range(HT):
                            for c in range(C):
                                last = mm(ps[:, group + j // 2, (j % 2) * D:(j % 2 + 1) * D],
                                          t.pT[:, c, (h * HT + j) * P:(h * HT + j + 1) * P],
                                          t.nv[:, (s + 1) % 2, c], start=(c == 0), stop=(c == C - 1))
                        last.then_inc(sem.oc_done, 1)
                if live(i + 1):
                    pe.wait_ge(sem.kb_made, i + 2)
                    if live(i - 1):
                        pe.wait_ge(sem.tp_kept, 2 * i)
                    elif live(i):
                        pe.wait_ge(sem.t3_lo, 2 * i + 2)
                    if live(i):
                        pe.wait_ge(sem.c_sub, 2 * i + 2)
                    for f in range(C):
                        kb = t.kb[:, f].rearrange("p h q -> p (h q)")
                        for c in range(C):
                            mm(ps[:, GB, c * HQ + f * P:c * HQ + (f + 1) * P], t.wqT[:, f, c * P:(c + 1) * P], kb,
                               start=True, stop=True)
                        mm(ps[:, GB + 1, f * D:(f + 1) * D], t.vb[:, f].rearrange("p h q -> p (h q)"), t.wo[:, f],
                           start=True, stop=True)
                        last = mm(ps[0:64, GD, f * P:(f + 1) * P], t.bqp[:, f], kb, start=True, stop=True)
                    last.then_inc(sem.mn_done, 1)

            rows(pe, body)


_INS = ['L0_attn_x', 'L0_attn_Wz', 'L0_attn_bz', 'L0_attn_Wh', 'L0_attn_bh', 'L0_ffn_slot_query',
        'L0_ffn_d_Wq', 'L0_ffn_d_Wk', 'L0_ffn_d_Wv', 'L0_ffn_d_Wo', 'L0_ffn_d_bq', 'L0_ffn_d_bk', 'L0_ffn_d_bv',
        'L0_ffn_d_bo', 'L0_ffn_c_Wq', 'L0_ffn_c_Wk', 'L0_ffn_c_Wv', 'L0_ffn_c_Wo', 'L0_ffn_c_bq', 'L0_ffn_c_bk',
        'L0_ffn_c_bv', 'L0_ffn_c_bo', 'L0_ffn_e_ln_g', 'L0_ffn_e_ln_b', 'L0_ffn_e_W1', 'L0_ffn_e_b1',
        'L0_ffn_e_Wg', 'L0_ffn_e_bg', 'L0_ffn_e_W2', 'L0_ffn_e_b2']


def kernel(**inputs):
    import numpy as _np
    import concourse.bacc as _bacc
    from concourse import mybir as _mybir
    from concourse.bass_utils import run_bass_kernel_spmd as _run

    nc = _bacc.Bacc("TRN2", target_bir_lowering=False, num_devices=1)
    arrays, args = {}, []
    for name in _INS:
        a = _np.ascontiguousarray(inputs[name])
        arrays[f"in_{name}_dram"] = a
        args.append(nc.dram_tensor(f"in_{name}_dram", a.shape, _mybir.dt.from_np(a.dtype), kind="ExternalInput").ap())
    out = nc.dram_tensor("out_0_dram", (B, S, D), _mybir.dt.float32, kind="ExternalOutput").ap()
    mixer_moe(nc, *args, out)
    r = _run(nc, [arrays], core_ids=[0])
    return r.results[0]["out_0_dram"]
```

```python
from collections import namedtuple
from contextlib import ExitStack

import concourse.bass as bass
from concourse import mybir

F32 = mybir.dt.float32
F32R = mybir.dt.float32r
ALU = mybir.AluOpType
ACT = mybir.ActivationFunctionType
AX = mybir.AxisListType.X

P = 128
B, S, D = 16, 1024, 256
C = D // P
T = S // P
HT = T // 2
HS = S // 2
H, NQ = 16, 16
DH = D // H
HC = P // DH
HQ = H * NQ
E, F = 16, 1024
FK = F // P
EPS = 1e-5
KEY_SCALE = 0.25
SLOTS = 4
ROWS = 4

SEMAPHORES = """
sp_passed pool_passed dve_passed
ident_built consts_built w_loaded sel_built x_loaded0 x_loaded1 split_w zeroed
sqT_done sqT_kept qT_done qT_kept wkT_done wkT_kept qb_built mk_done mk_hi mk_kept
x_stats x_mv x_var x_pow n_ready
tn_done tn_hi tn_lo
z_done hh_done z_sig a_sig b_made h_scanned
th_done th_stats th_mv th_var th_pow th_norm y_ready x1_ready
x1_stored0 x1_stored1 st_stored x1_stats x1_mv x1_var x1_pow n2_ready
t2_done t2_hi t2_lo
s_done s_max mt_done mt_red mt_sum mt_kept mr_done mr_hi mr_kept ga_done p_ready
u_done u_rcp u_kept tu_done ut_kept
ew0 ew1 ew2 ew3 ew_used
slot_w slot_small pads_zero wvp_built spread_made ao_done ao_kept o_done o_kept o_stats o_mv o_var o_pow
o_centred o_scaled o_ln b2t_done b2t_kept ot_done ot_kept
xe_made ug_done ug_silu hg_made hgt_done hgt_kept y_done y_kept yt_done y_summed o2_made
c_w c_rows0 c_rows1 c_rows2 c_rows3 kv_done kv_kept wqT_done wqT_kept bqp_made bo_made
n2c_ready kb_made mn_done m_hi m_kept n_kept cr_hi cr_kept
t3_done t3_hi t3_lo sc_done c_max c_sub c_exp c_sum c_rcp c_prob tp_done tp_kept
oc_done oc_stats oc_mv oc_var oc_pow oc_norm yc_ready oc_added oc_stored
"""


def live(b):
    return not isinstance(b, int) or 0 <= b < B


def after_first(b):
    return not isinstance(b, int) or b > 0


def row(ap, b):
    return ap[bass.ds(b, 1)].rearrange("o p n -> (o p) n")


def mixer_moe(nc, x, Wz, bz, Wh, bh, slot_query, d_Wq, d_Wk, d_Wv, d_Wo, d_bq, d_bk, d_bv, d_bo,
              c_Wq, c_Wk, c_Wv, c_Wo, c_bq, c_bk, c_bv, c_bo,
              e_ln_g, e_ln_b, e_W1, e_b1, e_Wg, e_bg, e_W2, e_b2, out):
    x1_dram = nc.dram_tensor("x1_rows", [B, P, T * D], F32, kind="Internal").ap()
    st_dram = nc.dram_tensor("x1_norms", [B, P, 2 * T], F32, kind="Internal").ap()
    with ExitStack() as ctx:
        names = SEMAPHORES.split()
        sem = namedtuple("Semaphores", names)(*[ctx.enter_context(nc.semaphore(n)) for n in names])
        ps = ctx.enter_context(nc.psum_tensor("ps", [P, 8, 512], F32))
        keep = tensors(nc, ctx, "keep", [
            ("ident", [P, P], F32), ("hmask", [P, HC, DH], F32), ("selrow", [P, P], F32R),
            ("zero", [P, D], F32), ("mhalf", [P, T], F32),
            ("UT", [P, C, HQ, B], F32),
            ("pT", [P, T, HQ], F32),
            ("nrm", [P, ROWS, 2, T], F32), ("cb", [P, 3, C], F32), ("bo_rep", [P, D], F32),
            ("w1_0", [P, C, F], F32), ("wg_0", [P, C, F], F32), ("w2_0", [P, FK, D], F32),
            ("o2T", [P, C, NQ * B], F32),
        ])
        with ExitStack() as inner:
            both = tensors(nc, inner, "both", [
                ("xt", [P, 2, T, D], F32),
                ("x1", [P, 2, T, D], F32),
                ("n", [P, T, D], F32),
                ("a", [P, C, S], F32),
                ("hT", [P, C, S], F32),
                ("y", [P, T, D], F32),
            ])
            ring = expert_slots(keep, both)
            with ExitStack() as innermost:
                dispatch_phase(nc, innermost, sem, ps, keep, both, ring, x, Wz, bz, Wh, bh, slot_query,
                               d_Wq, d_Wk, d_bq, d_bk, e_W1, e_Wg, e_W2, x1_dram, st_dram)
            with ExitStack() as innermost:
                expert_phase(nc, innermost, sem, ps, keep, ring, slot_query, d_Wv, d_Wo, d_bv, d_bo,
                             e_ln_g, e_ln_b, e_W1, e_b1, e_Wg, e_bg, e_W2, e_b2,
                             c_Wq, c_Wk, c_Wv, c_Wo, c_bq, c_bk, c_bv, c_bo, x1_dram, st_dram)
        with ExitStack() as inner:
            combine_phase(nc, inner, sem, ps, keep, x1_dram, st_dram, out)


def expert_slots(keep, both):
    def halves(ap):
        return ap.rearrange("p (c a) d -> p c (a d)", c=C)
    return [[keep.w1_0[:, :, :], keep.wg_0[:, :, :], keep.w2_0[:, :, :]],
            [halves(both.xt[:, 0]), halves(both.xt[:, 1]), both.n[:, :, :]],
            [both.a[:, :, :], both.hT[:, :, :], both.y[:, :, :]],
            [halves(both.x1[:, 0]), halves(both.x1[:, 1]), None]]


def load_expert(sp, sem, ring, k, e, e_W1, e_Wg, e_W2, parts=(0, 1, 2)):
    arrived = (sem.ew0, sem.ew1, sem.ew2, sem.ew3)[k]
    sources = ((e_W1, "o (c p) f -> p (o c) f"), (e_Wg, "o (c p) f -> p (o c) f"), (e_W2, "o (k p) d -> p (o k) d"))
    for n in parts:
        w, rule = sources[n]
        sp.dma_start(ring[k][n], w[bass.ds(e, 1)].rearrange(rule, p=P)).then_inc(arrived, 16)


def combine_rows(keep):
    return keep.UT[:, :, :, :].rearrange("p c q b -> p (c q b)").rearrange("p (s j d) -> p s j d", s=ROWS, d=D)


def load_row(sp, sem, keep, x1_dram, st_dram, b, s):
    loaded = (sem.c_rows0, sem.c_rows1, sem.c_rows2, sem.c_rows3)[s]
    sp.dma_start(combine_rows(keep)[:, s].rearrange("p j d -> p (j d)"), row(x1_dram, b)).then_inc(loaded, 16)
    sp.dma_start(keep.nrm[:, s].rearrange("p a j -> p (a j)"), row(st_dram, b)).then_inc(loaded, 16)


def alone(e, passed):
    e.sem_inc(passed, 1)


def tensors(nc, ctx, phase, specs):
    got = [ctx.enter_context(nc.sbuf_tensor(f"{phase}_{n}", shape, dtype)) for n, shape, dtype in specs]
    return namedtuple("Tensors", [n for n, _, _ in specs])(*got)


def three_passes(nc, dst, w_hi, w_lo, a_hi, a_lo, first, last, skip=False):
    nc.tensor.matmul(dst, w_hi, a_hi, start=first, stop=False, skip_group_check=skip)
    nc.tensor.matmul(dst, w_hi, a_lo, start=False, stop=False, skip_group_check=skip)
    return nc.tensor.matmul(dst, w_lo, a_hi, start=False, stop=last, skip_group_check=skip)


def dispatch_phase(nc, ctx, sem, ps, keep, both, ring, x, Wz, bz, Wh, bh, slot_query,
                   d_Wq, d_Wk, d_bq, d_bk, e_W1, e_Wg, e_W2, x1_dram, st_dram):
    t = tensors(nc, ctx, "dispatch", [
        ("nT_hi", [P, C, S], F32R), ("nT_lo", [P, C, S], F32R),
        ("z", [P, 2, HS], F32),
        ("n2", [P, 2, T, D + 4], F32),
        ("n2T_hi", [P, C, S], F32R), ("n2T_lo", [P, C, S], F32R),
        ("u", [P, 2, D], F32),
        ("wz_hi", [P, C, D], F32R), ("wz_lo", [P, C, D], F32R),
        ("wh_hi", [P, C, D], F32R), ("wh_lo", [P, C, D], F32R),
        ("mk_hi", [P, C, HQ], F32R), ("mk_lo", [P, C, HQ], F32R),
        ("sqT", [P, C, NQ], F32), ("qT", [P, C, NQ], F32),
        ("qb", [P, C, HC, NQ], F32),
        ("bz", [P, C], F32), ("nbz", [P, C], F32), ("bh", [P, C], F32),
        ("bq", [P, C], F32), ("bk", [P, C], F32),
        ("ccol", [P, 2], F32),
        ("x_st", [P, T, 6], F32), ("x_mv", [P, T, 2], F32), ("x_v", [P, 2, T], F32), ("x_r", [P, T], F32),
        ("h_st", [P, HT, 6], F32), ("h_mv", [P, HT, 2], F32), ("h_v", [P, 2, 2, HT], F32),
        ("h_r", [P, 2, 2, HT], F32),
        ("x1_st", [P, T, 6], F32), ("x1_mv", [P, T, 2], F32), ("x1_v", [P, T], F32),
        ("x1_n", [P, 2, 2, T], F32),
        ("mx", [P, 2, HQ], F32), ("mcol", [P, 2], F32), ("mcol2", [P, 2], F32), ("mcolp", [P, 2, 64], F32),
        ("grow", [P, HQ], F32R), ("grow_t", [64, HQ], F32R),
        ("rcp", [P, 2], F32),
    ])
    wq, wk = both.a[:, :, 0:D], both.a[:, :, D:2 * D]
    wz, wh, wkT = both.y[:, 0:2, :], both.y[:, 2:4, :], both.y[:, 4:6, :]
    sq, sel32 = both.y[0:NQ, 6, :], both.y[:, 7, 0:P]
    x_loaded, x1_stored = (sem.x_loaded0, sem.x_loaded1), (sem.x1_stored0, sem.x1_stored1)
    s_all = ps[:, 4:8, :].rearrange("p k n -> p (k n)")
    s_tile = s_all.rearrange("p (j q) -> p j q", q=HQ)
    BANK = (2, 0)

    def rows(e, body):
        for i in range(4):
            body(i, i % 2, i // 2)
        with e.Fori(2, B // 2 - 1) as k:
            body(2 * k, 0, k)
            body(2 * k + 1, 1, k)
        for i in range(B - 2, B + 2):
            body(i, i % 2, i // 2)

    with nc.Block() as block:

        @block.sync
        def _(sp):
            sp.dma_start(both.xt[:, 0], x[0].rearrange("(j p) d -> p j d", p=P)).then_inc(x_loaded[0], 16)
            sp.dma_start(sq, slot_query.rearrange("o q d -> (o q) d")).then_inc(sem.w_loaded, 16)
            for dst, src in ((wq, d_Wq), (wk, d_Wk), (wz, Wz), (wh, Wh)):
                sp.dma_start(dst, src.rearrange("(c p) n -> p c n", p=P)).then_inc(sem.w_loaded, 16)
            for dst, src in ((t.bz, bz), (t.bh, bh), (t.bq, d_bq), (t.bk, d_bk)):
                sp.dma_start(dst[:, :], src.rearrange("(c p) -> p c", p=P), allow_slow_non_contiguous=True) \
                    .then_inc(sem.w_loaded, 16)
            sp.dma_start(both.xt[:, 1], x[1].rearrange("(j p) d -> p j d", p=P)).then_inc(x_loaded[1], 16)

            def body(i, s, k):
                o = 1 - s
                if live(i - 1):
                    sp.wait_ge(sem.x1_ready, 2 * i)
                    alone(sp, sem.sp_passed)
                    if live(i + 1):
                        sp.dma_start(both.xt[:, o], x[bass.ds(i + 1, 1)].rearrange("o (j p) d -> p (o j) d", p=P)) \
                            .then_inc(x_loaded[o], 16)
                    sp.dma_start(row(x1_dram, i - 1), both.x1[:, o].rearrange("p j d -> p (j d)")) \
                        .then_inc(x1_stored[o], 16)
                    if isinstance(i, int) and i == 2:
                        load_expert(sp, sem, ring, 0, 0, e_W1, e_Wg, e_W2)
                    if isinstance(i, int) and i == B:
                        load_expert(sp, sem, ring, 1, 1, e_W1, e_Wg, e_W2)
                        load_expert(sp, sem, ring, 2, 2, e_W1, e_Wg, e_W2)
                    sp.wait_ge(sem.x1_pow, i)
                    alone(sp, sem.sp_passed)
                    if after_first(i - 1):
                        sp.wait_ge(sem.st_stored, 16 * (i - 1))
                    alone(sp, sem.sp_passed)
                    sp.dma_start(row(st_dram, i - 1), t.x1_n[:, o].rearrange("p a j -> p (a j)")) \
                        .then_inc(sem.st_stored, 16)
                    if isinstance(i, int) and i == B:
                        sp.wait_ge(sem.n2_ready, 2 * B - 2)
                        sp.wait_ge(x1_stored[s], 16 * (B // 2))
                        load_expert(sp, sem, ring, 3, 3, e_W1, e_Wg, e_W2, parts=(0,))

            rows(sp, body)
            sp.wait_ge(sem.n2_ready, 2 * B)
            sp.wait_ge(x1_stored[(B - 1) % 2], 16 * (B // 2))
            load_expert(sp, sem, ring, 3, 3, e_W1, e_Wg, e_W2, parts=(1,))
            sp.wait_ge(x1_stored[0], 16 * (B // 2))
            sp.wait_ge(x1_stored[1], 16 * (B // 2))
            sp.wait_ge(sem.st_stored, 16 * B)

        @block.gpsimd
        def _(pool):
            g = nc.gpsimd
            g.memset(keep.ident[:, :], 0.0).then_inc(sem.ident_built, 1)
            g.memset(keep.hmask[:, :, :], 1.0).then_inc(sem.ident_built, 1)
            g.memset(keep.mhalf[:, :], -0.5)
            g.memset(keep.zero[:, :], 0.0)
            g.memset(t.mcolp[:, :, :], 0.0)
            g.memset(t.n2[:, 0, :, D:D + 4], 1.0)
            g.memset(t.n2[:, 1, :, D:D + 4], 1.0).then_inc(sem.zeroed, 1)
            pool.wait_ge(sem.ident_built, 2)
            g.affine_select(out=keep.ident[:, :], in_=keep.ident[:, :], compare_op=ALU.not_equal, fill=1.0,
                            base=0, pattern=[[-1, P]], channel_multiplier=1).then_inc(sem.ident_built, 1)
            g.affine_select(out=keep.hmask[:, :, :], in_=keep.hmask[:, :, :], compare_op=ALU.is_ge, fill=0.0,
                            base=0, pattern=[[-DH, HC], [0, DH]], channel_multiplier=1).then_inc(sem.ident_built, 1)
            pool.wait_ge(sem.ident_built, 4)
            g.affine_select(out=keep.hmask[:, :, :], in_=keep.hmask[:, :, :], compare_op=ALU.is_ge, fill=0.0,
                            base=DH - 1, pattern=[[DH, HC], [0, DH]], channel_multiplier=-1) \
                .then_inc(sem.consts_built, 1)

            def norm_x(b, s, h):
                if h == 0:
                    pool.wait_ge(sem.x_var, b + 1)
                    g.tensor_tensor(t.x_r[:, :], t.x_v[:, 0], keep.mhalf[:, :], ALU.pow).then_inc(sem.x_pow, 1)
                    pool.wait_ge(sem.x_pow, b + 1)
                    if after_first(b):
                        pool.wait_ge(sem.tn_done, 2 * b)
                    alone(pool, sem.pool_passed)
                for j in range(h * HT, (h + 1) * HT):
                    last = g.tensor_scalar(both.n[:, j], both.xt[:, s, j], t.x_v[:, 1, j:j + 1], t.x_r[:, j:j + 1],
                                           ALU.add, ALU.mult)
                last.then_inc(sem.n_ready, 1)

            def norm_h(i, h):
                pool.wait_ge(sem.th_var, 2 * i + h + 1)
                g.tensor_tensor(t.h_r[:, h, 0], t.h_v[:, h, 0], keep.mhalf[:, 0:HT], ALU.pow) \
                    .then_inc(sem.th_pow, 1)
                pool.wait_ge(sem.th_pow, 2 * i + h + 1)
                g.tensor_tensor(t.h_r[:, h, 1], t.h_v[:, h, 1], t.h_r[:, h, 0], ALU.mult).then_inc(sem.th_norm, 1)

            def residual(i, s, k, h):
                if h == 0 and live(i - 2):
                    pool.wait_ge(x1_stored[s], 16 * k)
                    alone(pool, sem.pool_passed)
                pool.wait_ge(sem.y_ready, 2 * i + h + 1)
                half = slice(h * HT, (h + 1) * HT)
                g.tensor_tensor(both.x1[:, s, half], both.xt[:, s, half], both.y[:, half], ALU.add).then_inc(sem.x1_ready, 1)

            def body(i, s, k):
                o = 1 - s
                if live(i - 1):
                    pool.wait_ge(sem.x1_var, i)
                    if live(i - 3) and after_first(i - 2):
                        pool.wait_ge(sem.st_stored, 16 * (i - 2))
                    g.tensor_tensor(t.x1_n[:, o, 0], t.x1_v[:, :], keep.mhalf[:, :], ALU.pow) \
                        .then_inc(sem.x1_pow, 1)
                    pool.wait_ge(sem.x1_pow, i)
                    if live(i - 3):
                        pool.wait_ge(sem.u_done, i - 2)
                    alone(pool, sem.pool_passed)
                    for j in range(T):
                        last = g.tensor_scalar(t.n2[:, o, j, 0:D], both.x1[:, o, j], t.x1_n[:, o, 1, j:j + 1],
                                               t.x1_n[:, o, 0, j:j + 1], ALU.add, ALU.mult)
                        if j % HT == HT - 1:
                            last.then_inc(sem.n2_ready, 1)
                if live(i + 1):
                    norm_x(i + 1, o, 0)
                if live(i):
                    norm_h(i, 0)
                if live(i + 1):
                    norm_x(i + 1, o, 1)
                if live(i):
                    residual(i, s, k, 0)
                    norm_h(i, 1)
                    residual(i, s, k, 1)

            norm_x(0, 0, 0)
            norm_x(0, 0, 1)
            rows(pool, body)

        @block.scalar
        def _(act):
            a = nc.scalar
            act.wait_ge(sem.w_loaded, 16 * 9)
            a.activation(t.nbz[:, :], t.bz[:, :], ACT.Copy, scale=-1.0).then_inc(sem.split_w, 1)
            act.wait_ge(sem.mk_done, 1)
            a.activation(t.mk_hi[:, :, :], ps[:, 4, :].rearrange("p (c q) -> p c q", c=C), ACT.Copy) \
                .then_inc(sem.mk_hi, 1)
            act.wait_ge(sem.split_w, 1)

            def keep_hi(dst, bank, h, done, n, out_sem):
                act.wait_ge(done, n)
                a.activation(dst[:, :, h * HS:(h + 1) * HS], ps[:, bank:bank + 2, :], ACT.Copy) \
                    .then_inc(out_sem, 1)

            def gate(i, m):
                e, h, bank = m % 2, m // 2, BANK[m % 2]
                act.wait_ge(sem.z_done, 4 * i + m + 1)
                if m >= 2 or after_first(i):
                    act.wait_ge(sem.b_made, 4 * i + m - 1)
                a.activation(t.z[:, m % 2], ps[:, bank, :], ACT.Sigmoid, bias=t.bz[:, e:e + 1]) \
                    .then_inc(sem.z_sig, 1)
                if m == 0 and after_first(i):
                    act.wait_ge(sem.h_scanned, 4 * i)
                a.activation(both.a[:, e, h * HS:(h + 1) * HS], ps[:, bank, :], ACT.Sigmoid,
                             bias=t.nbz[:, e:e + 1], scale=-1.0).then_inc(sem.a_sig, 1)

            def centre_h(i, h):
                act.wait_ge(sem.th_norm, 2 * i + h + 1)
                if after_first(i):
                    act.wait_ge(sem.x1_ready, 2 * i + h - 1)
                for j in range(HT):
                    last = a.activation(both.y[:, h * HT + j],
                                        ps[:, BANK[h] + j // 2, (j % 2) * D:(j % 2 + 1) * D],
                                        ACT.Identity, scale=t.h_r[:, h, 0, j:j + 1], bias=t.h_r[:, h, 1, j:j + 1])
                last.then_inc(sem.y_ready, 1)

            def body(i, s, k):
                if live(i):
                    for h in range(2):
                        if h == 0 and after_first(i):
                            act.wait_ge(sem.hh_done, 4 * i)
                        keep_hi(t.nT_hi, BANK[h], h, sem.tn_done, 2 * i + h + 1, sem.tn_hi)
                    for m in range(3):
                        gate(i, m)
                if live(i - 2):
                    act.wait_ge(sem.ga_done, i - 1)
                    if after_first(i - 2):
                        act.wait_ge(sem.u_done, i - 2)
                    a.activation(keep.pT[:, :, :].rearrange("p j q -> p (j q)"), s_all, ACT.Exp).then_inc(sem.p_ready, 1)
                if live(i):
                    gate(i, 3)
                if live(i - 1):
                    if after_first(i - 1):
                        act.wait_ge(sem.s_done, 2 * i - 2)
                    keep_hi(t.n2T_hi, 6, 0, sem.t2_done, 2 * i - 1, sem.t2_hi)
                if live(i - 2):
                    act.wait_ge(sem.u_rcp, i - 1)
                    if after_first(i - 2):
                        act.wait_ge(sem.tu_done, i - 2)
                    for m in range(2):
                        last = a.activation(t.u[:, m], ps[:, 4 + m, 0:D], ACT.Copy, scale=t.rcp[:, m:m + 1])
                    last.then_inc(sem.u_kept, 1)
                if live(i - 1):
                    keep_hi(t.n2T_hi, 6, 1, sem.t2_done, 2 * i, sem.t2_hi)
                if live(i):
                    centre_h(i, 0)
                if live(i - 2):
                    act.wait_ge(sem.tu_done, i - 1)
                    a.activation(keep.UT[:, :, :, bass.ds(i - 2, 1)],
                                 ps[:, 7, :].rearrange("p (c q o) -> p c q o", c=C, o=1), ACT.Copy) \
                        .then_inc(sem.ut_kept, 1)
                if live(i):
                    centre_h(i, 1)

            rows(act, body)

        @block.vector
        def _(dve):
            v = nc.vector
            def stats_x(b, s, count):
                dve.wait_ge(x_loaded[s], 16 * count)
                for j in range(T):
                    last = v.bn_stats(t.x_st[:, j], both.xt[:, s, j])
                last.then_inc(sem.x_stats, 1)
                dve.wait_ge(sem.x_stats, b + 1)
                alone(dve, sem.dve_passed)
                for j in range(T):
                    last = v.bn_aggr(t.x_mv[:, j], t.x_st[:, j])
                last.then_inc(sem.x_mv, 1)
                dve.wait_ge(sem.x_mv, b + 1)
                if after_first(b):
                    dve.wait_ge(sem.n_ready, 2 * b)
                v.tensor_scalar(t.x_v[:, 0], t.x_mv[:, :, 1], EPS, None, ALU.add)
                v.tensor_scalar(t.x_v[:, 1], t.x_mv[:, :, 0], -1.0, None, ALU.mult).then_inc(sem.x_var, 1)

            stats_x(0, 0, 1)
            dve.wait_ge(sem.w_loaded, 16 * 9)
            v.tensor_copy(t.wz_hi[:, :, :], wz)
            v.tensor_copy(t.wh_hi[:, :, :], wh).then_inc(sem.split_w, 1)
            dve.wait_ge(sem.split_w, 2)
            v.tensor_tensor(t.wz_lo[:, :, :], wz, t.wz_hi[:, :, :], ALU.subtract)
            v.tensor_tensor(t.wh_lo[:, :, :], wh, t.wh_hi[:, :, :], ALU.subtract).then_inc(sem.split_w, 1)
            v.memset(sel32, 0.0).then_inc(sem.sel_built, 1)
            dve.wait_ge(sem.sel_built, 1)
            v.memset(sel32[0:1, :], 1.0)
            v.memset(sel32[32:33, :], 1.0).then_inc(sem.sel_built, 1)
            dve.wait_ge(sem.sel_built, 2)
            dve.wait_ge(sem.zeroed, 1)
            v.tensor_copy(keep.selrow[:, :], sel32)
            v.tensor_copy(t.grow[:, :], keep.zero[:, :]).then_inc(sem.split_w, 1)
            dve.wait_ge(sem.sqT_done, 1)
            v.tensor_copy(t.sqT[:, :, :], ps[:, 0, 0:C * NQ].rearrange("p (c q) -> p c q", c=C)).then_inc(sem.sqT_kept, 1)
            dve.wait_ge(sem.qT_done, 1)
            for c in range(C):
                last = v.tensor_scalar(t.qT[:, c], ps[:, 1, c * NQ:(c + 1) * NQ], t.bq[:, c:c + 1], KEY_SCALE,
                                       ALU.add, ALU.mult)
            last.then_inc(sem.qT_kept, 1)
            dve.wait_ge(sem.wkT_done, 1)
            v.tensor_copy(wkT, ps[:, 2:4, 0:D]).then_inc(sem.wkT_kept, 1)
            dve.wait_ge(sem.qT_kept, 1)
            dve.wait_ge(sem.consts_built, 1)
            for c in range(C):
                last = v.tensor_tensor(t.qb[:, c], t.qT[:, c].unsqueeze(1).to_broadcast([P, HC, NQ]),
                                       keep.hmask[:, :, :], ALU.mult)
            last.then_inc(sem.qb_built, 1)
            dve.wait_ge(sem.mk_done, 1)
            v.tensor_copy(t.ccol[:, :], ps[:, 5, 0:2])
            dve.wait_ge(sem.mk_hi, 1)
            v.tensor_tensor(t.mk_lo[:, :, :], ps[:, 4, :].rearrange("p (c q) -> p c q", c=C), t.mk_hi[:, :, :],
                            ALU.subtract).then_inc(sem.mk_kept, 1)
            dve.wait_ge(sem.mk_kept, 1)

            def keep_lo(dst, hi, bank, h, hi_sem, n, out_sem):
                dve.wait_ge(hi_sem, n)
                half = slice(h * HS, (h + 1) * HS)
                v.tensor_tensor(dst[:, :, half], ps[:, bank:bank + 2, :], hi[:, :, half], ALU.subtract) \
                    .then_inc(out_sem, 1)

            def inputs_of_scan(i, m):
                e, half = m % 2, slice(m // 2 * HS, (m // 2 + 1) * HS)
                dve.wait_ge(sem.z_sig, 4 * i + m + 1)
                dve.wait_ge(sem.hh_done, 4 * i + m + 1)
                if m == 0 and after_first(i):
                    dve.wait_ge(sem.th_done, 2 * i)
                alone(dve, sem.dve_passed)
                v.scalar_tensor_tensor(both.hT[:, e, half], ps[:, BANK[m % 2] + 1, :], t.bh[:, e:e + 1], t.z[:, m % 2],
                                       ALU.add, ALU.mult).then_inc(sem.b_made, 1)

            def scan(i, m):
                e, h = m % 2, m // 2
                half = slice(h * HS, (h + 1) * HS)
                dve.wait_ge(sem.b_made, 4 * i + m + 1)
                dve.wait_ge(sem.a_sig, 4 * i + m + 1)
                if h:
                    dve.wait_ge(sem.h_scanned, 4 * i + m - 1)
                v.tensor_tensor_scan(both.hT[:, e, half], both.a[:, e, half], both.hT[:, e, half],
                                     both.hT[:, e, HS - 1:HS] if h else 0.0, ALU.mult, ALU.add) \
                    .then_inc(sem.h_scanned, 1)

            def largest(b, h):
                dve.wait_ge(sem.s_done, 2 * b + h + 1)
                if h == 0 and after_first(b):
                    dve.wait_ge(sem.mt_done, b)
                v.tensor_reduce(t.mx[:, h], ps[:, 4 + 2 * h:6 + 2 * h, :].rearrange("p k (j q) -> p q (k j)", q=HQ),
                                AX, ALU.max).then_inc(sem.s_max, 1)

            def stats_h(i, h):
                n = 2 * i + h
                dve.wait_ge(sem.th_done, n + 1)
                for j in range(HT):
                    last = v.bn_stats(t.h_st[:, j], ps[:, BANK[h] + j // 2, (j % 2) * D:(j % 2 + 1) * D])
                last.then_inc(sem.th_stats, 1)
                dve.wait_ge(sem.th_stats, n + 1)
                alone(dve, sem.dve_passed)
                for j in range(HT):
                    last = v.bn_aggr(t.h_mv[:, j], t.h_st[:, j])
                last.then_inc(sem.th_mv, 1)
                dve.wait_ge(sem.th_mv, n + 1)
                if after_first(i):
                    dve.wait_ge(sem.th_norm, n - 1)
                v.tensor_scalar(t.h_v[:, h, 0], t.h_mv[:, :, 1], EPS, None, ALU.add)
                v.tensor_scalar(t.h_v[:, h, 1], t.h_mv[:, :, 0], -1.0, None, ALU.mult).then_inc(sem.th_var, 1)

            def body(i, s, k):
                o = 1 - s
                if live(i):
                    keep_lo(t.nT_lo, t.nT_hi, BANK[0], 0, sem.tn_hi, 2 * i + 1, sem.tn_lo)
                if live(i - 2):
                    largest(i - 2, 1)
                if live(i):
                    keep_lo(t.nT_lo, t.nT_hi, BANK[1], 1, sem.tn_hi, 2 * i + 2, sem.tn_lo)
                    inputs_of_scan(i, 0)
                if live(i - 2):
                    b = i - 2
                    dve.wait_ge(sem.mt_done, b + 1)
                    v.tensor_reduce(t.mcol[:, :], ps[:, 1, :].rearrange("p (c n) -> p c n", c=2), AX, ALU.max) \
                        .then_inc(sem.mt_red, 1)
                    dve.wait_ge(sem.mt_red, b + 1)
                    v.tensor_tensor(t.mcol2[:, :], t.mcol[:, :], t.ccol[:, :], ALU.add).then_inc(sem.mt_sum, 1)
                    dve.wait_ge(sem.mt_sum, b + 1)
                    v.tensor_tensor(t.mcolp[:, :, 0:64:32], t.ccol[:, :].unsqueeze(2).to_broadcast([P, 2, 2]),
                                    t.mcol2[:, :].unsqueeze(2).to_broadcast([P, 2, 2]), ALU.subtract) \
                        .then_inc(sem.mt_kept, 1)
                if live(i):
                    scan(i, 0)
                if live(i - 2):
                    guard_row(i - 2)
                if live(i - 1):
                    for h in range(2):
                        dve.wait_ge(sem.x1_ready, 2 * i + h - 1)
                        for j in range(h * HT, (h + 1) * HT):
                            last = v.bn_stats(t.x1_st[:, j], both.x1[:, o, j])
                    last.then_inc(sem.x1_stats, 1)
                if live(i):
                    inputs_of_scan(i, 1)
                if live(i - 1):
                    dve.wait_ge(sem.x1_stats, i)
                    alone(dve, sem.dve_passed)
                    for j in range(T):
                        last = v.bn_aggr(t.x1_mv[:, j], t.x1_st[:, j])
                    last.then_inc(sem.x1_mv, 1)
                    dve.wait_ge(sem.x1_mv, i)
                    if live(i - 2) and after_first(i - 1):
                        dve.wait_ge(sem.n2_ready, 2 * i - 2)
                    if live(i - 3):
                        dve.wait_ge(sem.st_stored, 16 * (i - 2))
                    v.tensor_scalar(t.x1_v[:, :], t.x1_mv[:, :, 1], EPS, None, ALU.add)
                    v.tensor_scalar(t.x1_n[:, o, 1], t.x1_mv[:, :, 0], -1.0, None, ALU.mult).then_inc(sem.x1_var, 1)
                if live(i):
                    scan(i, 1)
                    inputs_of_scan(i, 2)
                    scan(i, 2)
                if live(i + 1):
                    stats_x(i + 1, o, k + s + 1)
                if live(i):
                    inputs_of_scan(i, 3)
                    scan(i, 3)
                    stats_h(i, 0)
                if live(i - 1):
                    keep_lo(t.n2T_lo, t.n2T_hi, 6, 0, sem.t2_hi, 2 * i - 1, sem.t2_lo)
                if live(i - 2):
                    dve.wait_ge(sem.u_done, i - 1)
                    if after_first(i - 2):
                        dve.wait_ge(sem.u_kept, i - 2)
                    v.reciprocal(t.rcp[:, :].unsqueeze(2), ps[:, 4:6, D:D + 1]).then_inc(sem.u_rcp, 1)
                if live(i - 1):
                    keep_lo(t.n2T_lo, t.n2T_hi, 6, 1, sem.t2_hi, 2 * i, sem.t2_lo)
                if live(i):
                    stats_h(i, 1)
                if live(i - 1):
                    largest(i - 1, 0)

            def guard_row(b):
                dve.wait_ge(sem.mr_done, b + 1)
                if after_first(b):
                    dve.wait_ge(sem.ga_done, b)
                v.tensor_copy(t.grow_t[32:64, :], ps[32:64, 1, 0:D]).then_inc(sem.mr_hi, 1)
                v.tensor_copy(t.grow[0:32, :], ps[0:32, 1, 0:D])
                dve.wait_ge(sem.mr_hi, b + 1)
                v.tensor_tensor(t.grow[32:64, :], ps[32:64, 1, 0:D], t.grow_t[32:64, :], ALU.subtract) \
                    .then_inc(sem.mr_kept, 1)

            rows(dve, body)

        @block.tensor
        def _(pe):
            mm, tr = nc.tensor.matmul, nc.tensor.transpose
            pe.wait_ge(sem.w_loaded, 16 * 9)
            pe.wait_ge(sem.ident_built, 4)
            for c in range(C):
                last = tr(ps[:, 0, c * NQ:(c + 1) * NQ], sq[:, c * P:(c + 1) * P], keep.ident[0:NQ, 0:NQ])
            last.then_inc(sem.sqT_done, 1)
            for f in range(C):
                for c in range(C):
                    last = tr(ps[:, 2 + f, c * P:(c + 1) * P], wk[:, c, f * P:(f + 1) * P], keep.ident[:, :])
            last.then_inc(sem.wkT_done, 1)
            pe.wait_ge(sem.sqT_kept, 1)
            for f in range(C):
                for c in range(C):
                    last = mm(ps[:, 1, f * NQ:(f + 1) * NQ], wq[:, c, f * P:(f + 1) * P], t.sqT[:, c],
                              start=(c == 0), stop=(c == C - 1))
            last.then_inc(sem.qT_done, 1)
            pe.wait_ge(sem.qb_built, 1)
            pe.wait_ge(sem.wkT_kept, 1)
            for f in range(C):
                qb = t.qb[:, f].rearrange("p h q -> p (h q)")
                for c in range(C):
                    mm(ps[:, 4, c * HQ + f * P:c * HQ + (f + 1) * P], wkT[:, f, c * P:(c + 1) * P], qb,
                       start=True, stop=True)
                last = mm(ps[:, 5, f:f + 1], qb, t.bk[:, f:f + 1], start=True, stop=True)
            last.then_inc(sem.mk_done, 1)
            pe.wait_ge(sem.split_w, 4)
            pe.wait_ge(sem.mk_kept, 1)

            def transposed(src, bank, h):
                for j in range(HT):
                    for c in range(C):
                        last = tr(ps[:, bank + c, j * P:(j + 1) * P], src[:, h * HT + j, c * P:(c + 1) * P],
                                  keep.ident[:, :])
                return last

            def projection(m, bank, w_hi, w_lo):
                e, half = m % 2, slice(m // 2 * HS, (m // 2 + 1) * HS)
                for c in range(C):
                    last = three_passes(nc, ps[:, bank, :], w_hi[:, c, e * P:(e + 1) * P], w_lo[:, c, e * P:(e + 1) * P],
                                        t.nT_hi[:, c, half], t.nT_lo[:, c, half], c == 0, c == C - 1)
                return last

            def z_pre(m):
                projection(m, BANK[m % 2], t.wz_hi, t.wz_lo).then_inc(sem.z_done, 1)

            def h_tilde(m):
                projection(m, BANK[m % 2] + 1, t.wh_hi, t.wh_lo).then_inc(sem.hh_done, 1)

            def tokens_of_h(h):
                for j in range(HT):
                    for c in range(C):
                        at = (j % 2) * D + c * P
                        last = tr(ps[:, BANK[h] + j // 2, at:at + P],
                                  both.hT[:, c, (h * HT + j) * P:(h * HT + j + 1) * P], keep.ident[:, :])
                last.then_inc(sem.th_done, 1)

            def scores(tiles):
                for j in tiles:
                    for c in range(C):
                        last = three_passes(nc, s_tile[:, j], t.n2T_hi[:, c, j * P:(j + 1) * P],
                                            t.n2T_lo[:, c, j * P:(j + 1) * P], t.mk_hi[:, c], t.mk_lo[:, c],
                                            j % 2 == 0 and c == 0, c == C - 1, skip=True)
                return last

            def weighted_sums(s, m):
                for j in range(T):
                    last = mm(ps[:, 4 + m, 0:D + 1], keep.pT[:, j, m * P:(m + 1) * P], t.n2[:, s, j, 0:D + 1],
                              start=(j == 0), stop=(j == T - 1))
                return last

            def body(i, s, k):
                o = 1 - s
                if live(i - 2):
                    if live(i - 3):
                        pe.wait_ge(sem.ut_kept, i - 2)
                    scores([6])
                if live(i):
                    pe.wait_ge(sem.n_ready, 2 * i + 1)
                    if after_first(i):
                        pe.wait_ge(sem.y_ready, 2 * i - 1)
                    transposed(both.n, BANK[0], 0).then_inc(sem.tn_done, 1)
                if live(i - 2):
                    scores([7]).then_inc(sem.s_done, 1)
                if live(i):
                    pe.wait_ge(sem.n_ready, 2 * i + 2)
                    if after_first(i):
                        pe.wait_ge(sem.y_ready, 2 * i)
                    transposed(both.n, BANK[1], 1).then_inc(sem.tn_done, 1)
                    pe.wait_ge(sem.tn_lo, 2 * i + 1)
                    z_pre(0)
                    h_tilde(0)
                    pe.wait_ge(sem.tn_lo, 2 * i + 2)
                elif live(i - 1):
                    pe.wait_ge(sem.y_ready, 2 * i)
                if live(i - 2):
                    pe.wait_ge(sem.s_max, 2 * i - 2)
                    for c in range(2):
                        for h in range(2):
                            last = tr(ps[:, 1, (2 * c + h) * P:(2 * c + h + 1) * P], t.mx[:, h, c * P:(c + 1) * P],
                                      keep.ident[:, :])
                    last.then_inc(sem.mt_done, 1)
                if live(i):
                    z_pre(1)
                if live(i - 2):
                    pe.wait_ge(sem.mt_kept, i - 1)
                    for c in range(2):
                        last = mm(ps[0:64, 1, c * P:(c + 1) * P], t.mcolp[:, c], keep.ident[:, :],
                                  start=True, stop=True)
                    last.then_inc(sem.mr_done, 1)
                if live(i):
                    pe.wait_ge(sem.a_sig, 4 * i + 1)
                    z_pre(2)
                if live(i - 2):
                    pe.wait_ge(sem.mr_kept, i - 1)
                    for k in range(4):
                        last = mm(ps[:, 4 + k, :], keep.selrow[:, :],
                                  t.grow[:, :].unsqueeze(1).to_broadcast([P, 2, HQ]),
                                  start=False, stop=True, skip_group_check=True)
                    last.then_inc(sem.ga_done, 1)
                if live(i):
                    h_tilde(1)
                    pe.wait_ge(sem.b_made, 4 * i + 1)
                    h_tilde(2)
                    pe.wait_ge(sem.a_sig, 4 * i + 2)
                    z_pre(3)
                    pe.wait_ge(sem.b_made, 4 * i + 2)
                    h_tilde(3)
                if live(i - 2):
                    pe.wait_ge(sem.p_ready, i - 1)
                    weighted_sums(s, 0)
                if live(i):
                    pe.wait_ge(sem.h_scanned, 4 * i + 2)
                    pe.wait_ge(sem.b_made, 4 * i + 3)
                    pe.wait_ge(sem.a_sig, 4 * i + 3)
                    tokens_of_h(0)
                if live(i - 1):
                    pe.wait_ge(sem.n2_ready, 2 * i - 1)
                    transposed(t.n2[:, o], 6, 0).then_inc(sem.t2_done, 1)
                if live(i - 2):
                    weighted_sums(s, 1).then_inc(sem.u_done, 1)
                if live(i - 1):
                    pe.wait_ge(sem.n2_ready, 2 * i)
                    pe.wait_ge(sem.t2_lo, 2 * i - 1)
                    transposed(t.n2[:, o], 6, 1).then_inc(sem.t2_done, 1)
                if live(i):
                    pe.wait_ge(sem.h_scanned, 4 * i + 4)
                    tokens_of_h(1)
                if live(i - 2):
                    pe.wait_ge(sem.u_kept, i - 1)
                if live(i - 1):
                    scores([0])
                    pe.wait_ge(sem.t2_lo, 2 * i)
                if live(i - 2):
                    for c in range(C):
                        for m in range(2):
                            last = tr(ps[:, 7, c * HQ + m * P:c * HQ + (m + 1) * P], t.u[:, m, c * P:(c + 1) * P],
                                      keep.ident[:, :])
                    last.then_inc(sem.tu_done, 1)
                if live(i - 1):
                    scores([1, 2, 3]).then_inc(sem.s_done, 1)
                    scores([4, 5])

            rows(pe, body)


def expert_phase(nc, ctx, sem, ps, keep, ring, slot_query, d_Wv, d_Wo, d_bv, d_bo,
                 e_ln_g, e_ln_b, e_W1, e_b1, e_Wg, e_bg, e_W2, e_b2,
                 c_Wq, c_Wk, c_Wv, c_Wo, c_bq, c_bk, c_bv, c_bo, x1_dram, st_dram):
    TT = NQ * B // P
    QT = NQ // TT
    GH = 4
    NG = H // GH
    t = tensors(nc, ctx, "expert", [
        ("wv", [P, C, D], F32), ("wvp", [P, C, H, 32], F32),
        ("wop", [P, NG, D], F32), ("bvp", [P, NG], F32),
        ("ao", [P, NG, NQ * B], F32),
        ("sqb", [64, D], F32),
        ("ln_g", [NQ, D], F32), ("ln_b", [NQ, D], F32),
        ("spread", [64, NQ, B], F32),
        ("o", [P, TT, D], F32), ("oln", [P, TT, D], F32),
        ("o_st", [P, TT, 6], F32), ("o_mv", [P, TT, 2], F32), ("o_v", [P, 2, TT], F32), ("o_r", [P, TT], F32),
        ("hT", [P, C, NQ * B], F32), ("oT", [P, C, NQ * B], F32),
        ("b1", [P, F], F32), ("bg", [P, F], F32), ("eb2", [E, D], F32), ("b2T", [P, C, E], F32),
        ("xe", [P, 2, C, 32], F32), ("sel", [P, 2, 32], F32),
        ("sg", [P, 2, 512], F32), ("hg", [P, 2, D], F32), ("hgT", [P, 2, D], F32), ("ye", [P, 2, D], F32),
        ("ysum", [P, 2, C, B], F32),
        ("w2_3", [P, FK, D], F32),
    ])
    ring = ring[:3] + [ring[3][:2] + [t.w2_3[:, :, :]]]
    w1, wg, w2 = [[slot[n] for slot in ring] for n in range(3)]
    arrived = [sem.ew0, sem.ew1, sem.ew2, sem.ew3]

    with nc.Block() as block:

        @block.sync
        def _(sp):
            sp.dma_start(t.wv[:, :, :], d_Wv.rearrange("(c p) n -> p c n", p=P)).then_inc(sem.slot_w, 16)
            sp.wait_ge(sem.pads_zero, 1)
            for j in range(GH):
                lane = slice(32 * j, 32 * j + DH)
                sp.dma_start(t.wop[lane, :, :], d_Wo.rearrange("(g j k) n -> j k g n", j=GH, k=DH)[j]) \
                    .then_inc(sem.slot_small, 16)
                sp.dma_start(t.bvp[lane, :], d_bv.rearrange("(g j k) -> j k g", j=GH, k=DH)[j],
                             allow_slow_non_contiguous=True) \
                    .then_inc(sem.slot_small, 16)
            sp.dma_start(t.sqb[0:NQ, :], slot_query[0]).then_inc(sem.slot_small, 16)
            sp.dma_start(t.sqb[32:33, :], d_bo.unsqueeze(0)).then_inc(sem.slot_small, 16)
            sp.dma_start(t.ln_g[:, :], e_ln_g).then_inc(sem.slot_small, 16)
            sp.dma_start(t.ln_b[:, :], e_ln_b).then_inc(sem.slot_small, 16)
            for dst, src in ((t.b1, e_b1), (t.bg, e_bg), (t.eb2, e_b2)):
                sp.dma_start(dst[0:E, :], src).then_inc(sem.slot_small, 16)

            load_expert(sp, sem, ring, 3, 3, e_W1, e_Wg, e_W2, parts=(2,))
            for n, w in enumerate((c_Wk, c_Wv, c_Wq, c_Wo)):
                sp.dma_start(keep.pT[:, n * C:(n + 1) * C, :], w.rearrange("(c p) n -> p c n", p=P)) \
                    .then_inc(sem.c_w, 16)
            for n, w in enumerate((c_bq, c_bk, c_bv)):
                sp.dma_start(keep.cb[:, n], w.rearrange("(c p) -> p c", p=P), allow_slow_non_contiguous=True) \
                    .then_inc(sem.c_w, 16)
            sp.dma_start(keep.bo_rep[:, :], c_bo.unsqueeze(0).to_broadcast([P, D])).then_inc(sem.c_w, 16)
            sp.wait_ge(sem.ao_done, 1)
            for b in range(2):
                load_row(sp, sem, keep, x1_dram, st_dram, b, b)

            with sp.Fori(1, E // SLOTS) as r:
                for k in range(SLOTS):
                    sp.wait_ge(sem.y_done, SLOTS * r - SLOTS + k + 1)
                    alone(sp, sem.sp_passed)
                    load_expert(sp, sem, ring, k, SLOTS * r + k, e_W1, e_Wg, e_W2)

        @block.gpsimd
        def _(pool):
            g = nc.gpsimd
            g.memset(t.wop[:, :, :], 0.0)
            g.memset(t.sqb[:, :], 0.0)
            g.memset(t.bvp[:, :], 0.0)
            g.memset(t.b1[:, :], 0.0)
            g.memset(t.bg[:, :], 0.0).then_inc(sem.pads_zero, 1)
            g.memset(t.xe[:, :, :, :], 0.0)
            g.memset(t.sel[:, :, :], 0.0).then_inc(sem.pads_zero, 1)
            pool.wait_ge(sem.o_var, 1)
            g.tensor_tensor(t.o_r[:, :], t.o_v[:, 0], keep.mhalf[:, 0:TT], ALU.pow).then_inc(sem.o_pow, 1)

        @block.vector
        def _(dve):
            v = nc.vector
            v.memset(t.wvp[:, :, :, :], 0.0).then_inc(sem.wvp_built, 1)
            v.memset(t.spread[:, :, :], 0.0).then_inc(sem.spread_made, 1)
            dve.wait_ge(sem.spread_made, 1)
            v.memset(t.spread[32:33, :, :], 1.0).then_inc(sem.spread_made, 1)
            v.tensor_copy(t.spread[0:NQ, :, :], keep.ident[0:NQ, 0:NQ].unsqueeze(2).to_broadcast([NQ, NQ, B])) \
                .then_inc(sem.spread_made, 1)
            dve.wait_ge(sem.slot_w, 16)
            dve.wait_ge(sem.wvp_built, 1)
            v.tensor_copy(t.wvp[:, :, :, 0:DH], t.wv[:, :, :].rearrange("p c (h k) -> p c h k", k=DH)) \
                .then_inc(sem.wvp_built, 1)
            dve.wait_ge(sem.slot_small, 16 * 15)
            dve.wait_ge(sem.ao_done, 1)
            for g in range(NG):
                last = v.tensor_scalar(t.ao[:, g], ps[:, g // 2, (g % 2) * D:(g % 2 + 1) * D], t.bvp[:, g:g + 1],
                                       None, ALU.add)
            last.then_inc(sem.ao_kept, 1)
            dve.wait_ge(sem.b2t_done, 1)
            v.tensor_copy(t.b2T[:, :, :], ps[:, 6, 0:C * E].rearrange("p (c e) -> p c e", c=C)).then_inc(sem.b2t_kept, 1)
            dve.wait_ge(sem.o_done, 1)
            v.tensor_copy(t.o[:, :, :], ps[:, 4:4 + TT, 0:D]).then_inc(sem.o_kept, 1)
            dve.wait_ge(sem.o_kept, 1)
            for m in range(TT):
                last = v.bn_stats(t.o_st[:, m], t.o[:, m])
            last.then_inc(sem.o_stats, 1)
            dve.wait_ge(sem.o_stats, 1)
            alone(dve, sem.dve_passed)
            for m in range(TT):
                last = v.bn_aggr(t.o_mv[:, m], t.o_st[:, m])
            last.then_inc(sem.o_mv, 1)
            dve.wait_ge(sem.o_mv, 1)
            v.tensor_scalar(t.o_v[:, 0], t.o_mv[:, :, 1], EPS, None, ALU.add)
            v.tensor_scalar(t.o_v[:, 1], t.o_mv[:, :, 0], -1.0, None, ALU.mult).then_inc(sem.o_var, 1)
            dve.wait_ge(sem.o_pow, 1)
            dve.wait_ge(sem.o_var, 1)
            for m in range(TT):
                last = v.tensor_scalar(t.oln[:, m], t.o[:, m], t.o_v[:, 1, m:m + 1], t.o_r[:, m:m + 1],
                                       ALU.add, ALU.mult)
            last.then_inc(sem.o_centred, 1)
            dve.wait_ge(sem.o_centred, 1)
            v.tensor_tensor(t.oln[:, :, :], t.oln[:, :, :], ps[:, 2, :].rearrange("p (m d) -> p m d", d=D), ALU.mult).then_inc(sem.o_scaled, 1)
            dve.wait_ge(sem.o_scaled, 1)
            v.tensor_tensor(t.oln[:, :, :], t.oln[:, :, :], ps[:, 3, :].rearrange("p (m d) -> p m d", d=D), ALU.add).then_inc(sem.o_ln, 1)
            dve.wait_ge(sem.ot_done, 1)
            v.tensor_copy(t.hT[:, :, :], ps[:, 6, :].rearrange("p (c n) -> p c n", c=C))
            dve.wait_ge(sem.b2t_kept, 1)
            for c in range(C):
                last = v.tensor_tensor(t.oT[:, c].rearrange("p (q b) -> p q b", b=B),
                                       ps[:, 7, c * NQ * B:(c + 1) * NQ * B].rearrange("p (q b) -> p q b", b=B),
                                       t.b2T[:, c].unsqueeze(2).to_broadcast([P, NQ, B]), ALU.add)
            last.then_inc(sem.ot_kept, 1)
            dve.wait_ge(sem.ot_kept, 1)

            def prepare(e, q):
                v.tensor_copy(t.xe[:, q, :, 0:B], t.hT[:, :, bass.ds(e * B, B)])
                v.tensor_copy(t.sel[0:E, q, 0:B], keep.ident[0:E, bass.ds(e, 1)].to_broadcast([E, B])) \
                    .then_inc(sem.xe_made, 1)

            def result(e, q):
                dve.wait_ge(sem.yt_done, e + 1)
                parts = ps[:, 6 + q, 0:C * P].rearrange("p (c j n) -> p c n j", c=C, j=4)[:, :, 0:B, :]
                v.tensor_reduce(t.ysum[:, q], parts, AX, ALU.add).then_inc(sem.y_summed, 1)
                dve.wait_ge(sem.y_summed, e + 1)
                v.tensor_tensor(keep.o2T[:, :, bass.ds(e * B, B)], t.oT[:, :, bass.ds(e * B, B)], t.ysum[:, q],
                                ALU.add).then_inc(sem.o2_made, 1)

            def finish_expert(r, k):
                e, q = SLOTS * r + k, k % 2
                fresh = isinstance(r, int) and e < 2
                dve.wait_ge(sem.ug_silu, e + 1)
                v.tensor_tensor(t.hg[:, q], t.sg[:, q, 0:D], t.sg[:, q, D:2 * D], ALU.mult).then_inc(sem.hg_made, 1)
                dve.wait_ge(sem.hgt_done, e + 1)
                if not fresh:
                    dve.wait_ge(sem.y_done, e - 1)
                v.tensor_copy(t.hgT[:, q], ps[:, 2 + q, 0:D]).then_inc(sem.hgt_kept, 1)
                if not (isinstance(r, int) and e == E - 1):
                    if not (isinstance(r, int) and e == 0):
                        dve.wait_ge(sem.ug_done, e)
                    prepare(e + 1, 1 - q)
                dve.wait_ge(sem.y_done, e + 1)
                if not fresh:
                    dve.wait_ge(sem.yt_done, e - 1)
                v.tensor_copy(t.ye[:, q], ps[:, 4 + q, 0:D]).then_inc(sem.y_kept, 1)
                if not (isinstance(r, int) and e == 0):
                    result(e - 1, 1 - q)

            dve.wait_ge(sem.pads_zero, 2)
            prepare(0, 0)
            for k in range(SLOTS):
                finish_expert(0, k)
            with dve.Fori(1, E // SLOTS - 1) as r:
                for k in range(SLOTS):
                    finish_expert(r, k)
            for k in range(SLOTS):
                finish_expert(E // SLOTS - 1, k)
            result(E - 1, (E - 1) % 2)

        @block.scalar
        def _(act):
            a = nc.scalar

            def round_(r, first):
                for k in range(SLOTS):
                    e, q = SLOTS * r + k, k % 2
                    act.wait_ge(sem.ug_done, e + 1)
                    if not (first and k < 2):
                        act.wait_ge(sem.hg_made, e - 1)
                    a.activation(t.sg[:, q], ps[:, q, :], ACT.Silu).then_inc(sem.ug_silu, 1)

            round_(0, True)
            with act.Fori(1, E // SLOTS) as r:
                round_(r, False)

        @block.tensor
        def _(pe):
            mm, tr = nc.tensor.matmul, nc.tensor.transpose
            pe.wait_ge(sem.wvp_built, 2)
            for g in range(NG):
                for c in range(C):
                    for j in range(GH):
                        h = GH * g + j
                        last = mm(ps[32 * j:32 * j + 32, g // 2, (g % 2) * D:(g % 2 + 1) * D], t.wvp[:, c, h],
                                  keep.UT[:, c, h * NQ:(h + 1) * NQ, :].rearrange("p q b -> p (q b)"),
                                  start=(c == 0), stop=(c == C - 1), skip_group_check=True)
            last.then_inc(sem.ao_done, 1)
            pe.wait_ge(sem.slot_small, 16 * 15)
            for c in range(C):
                last = tr(ps[:, 6, c * E:(c + 1) * E], t.eb2[:, c * P:(c + 1) * P], keep.ident[0:E, 0:E])
            last.then_inc(sem.b2t_done, 1)
            pe.wait_ge(sem.spread_made, 3)
            for m in range(TT):
                spread = t.spread[:, m * QT:(m + 1) * QT, :].rearrange("q s b -> q (s b)")
                for bank, rows in ((2, t.ln_g), (3, t.ln_b)):
                    mm(ps[:, bank, m * D:(m + 1) * D], spread[0:NQ], rows[:, :], start=True, stop=True)
                mm(ps[:, 4 + m, 0:D], spread, t.sqb[:, :], start=True, stop=False)
            pe.wait_ge(sem.ao_kept, 1)
            for m in range(TT):
                for g in range(NG):
                    last = mm(ps[:, 4 + m, 0:D], t.ao[:, g, m * P:(m + 1) * P], t.wop[:, g],
                              start=False, stop=(g == NG - 1))
            last.then_inc(sem.o_done, 1)
            pe.wait_ge(sem.o_ln, 1)
            pe.wait_ge(sem.b2t_kept, 1)
            for m in range(TT):
                for c in range(C):
                    tr(ps[:, 6, c * NQ * B + m * P:c * NQ * B + (m + 1) * P], t.oln[:, m, c * P:(c + 1) * P],
                       keep.ident[:, :])
                    last = tr(ps[:, 7, c * NQ * B + m * P:c * NQ * B + (m + 1) * P], t.o[:, m, c * P:(c + 1) * P],
                              keep.ident[:, :])
            last.then_inc(sem.ot_done, 1)

            def up(e, k, r, fresh):
                q = k % 2
                pe.wait_ge(sem.xe_made, e + 1)
                pe.wait_ge(arrived[k], 48 * (r + 1))
                if not fresh:
                    pe.wait_ge(sem.ug_silu, e - 1)
                for n, (w, bias) in enumerate(((w1[k], t.b1), (wg[k], t.bg))):
                    for c in range(C + 1):
                        for j in range(4):
                            cols = slice(j * D, (j + 1) * D)
                            lhs = t.xe[:, q, c] if c < C else t.sel[:, q]
                            rhs = w[:, c, cols] if c < C else bias[:, cols]
                            last = mm(ps[32 * j:32 * j + 32, q, n * D:(n + 1) * D], lhs, rhs,
                                      start=(c == 0), stop=(c == C), skip_group_check=True)
                last.then_inc(sem.ug_done, 1)

            def down(e, k, fresh):
                q = k % 2
                pe.wait_ge(sem.hg_made, e + 1)
                if not fresh:
                    pe.wait_ge(sem.hgt_kept, e - 1)
                for n in range(2):
                    last = tr(ps[:, 2 + q, n * P:(n + 1) * P], t.hg[:, q, n * P:(n + 1) * P], keep.ident[:, :])
                last.then_inc(sem.hgt_done, 1)
                pe.wait_ge(sem.hgt_kept, e + 1)
                if not fresh:
                    pe.wait_ge(sem.y_kept, e - 1)
                for n in range(2):
                    for j in range(4):
                        last = mm(ps[32 * j:32 * j + 32, 4 + q, 0:D], t.hgT[:, q, n * P + 32 * j:n * P + 32 * j + 32],
                                  w2[k][:, 2 * j + n], start=(n == 0), stop=(n == 1), skip_group_check=True)
                last.then_inc(sem.y_done, 1)

            def down_transposed(e, q, fresh):
                pe.wait_ge(sem.y_kept, e + 1)
                if not fresh:
                    pe.wait_ge(sem.o2_made, e - 1)
                for c in range(C):
                    last = tr(ps[:, 6 + q, c * P:(c + 1) * P], t.ye[:, q, c * P:(c + 1) * P], keep.ident[:, :])
                last.then_inc(sem.yt_done, 1)

            pe.wait_ge(sem.ot_kept, 1)
            for k in range(SLOTS):
                up(k, k, 0, k < 2)
                if k > 0:
                    down_transposed(k - 1, (k - 1) % 2, k < 3)
                down(k, k, k < 2)
            with pe.Fori(1, E // SLOTS) as r:
                for k in range(SLOTS):
                    up(SLOTS * r + k, k, r, False)
                    down_transposed(SLOTS * r + k - 1, (k - 1) % 2, False)
                    down(SLOTS * r + k, k, False)
            down_transposed(E - 1, (E - 1) % 2, False)


def combine_phase(nc, ctx, sem, ps, keep, x1_dram, st_dram, out):
    GA, GB, GC, GD = 0, 2, 4, 6
    TOK = NQ * B
    t = tensors(nc, ctx, "combine", [
        ("khT", [P, C, TOK], F32), ("vhT", [P, C, TOK], F32), ("wqT", [P, C, D], F32),
        ("bqp", [P, C, 64], F32),
        ("kb", [P, C, HC, NQ], F32), ("vb", [P, C, HC, NQ], F32),
        ("m_hi", [P, C, HQ], F32R), ("m_lo", [P, C, HQ], F32R),
        ("nv", [P, 2, C, D], F32),
        ("crow", [P, HQ], F32R), ("crow_t", [64, HQ], F32R),
        ("n2", [P, T, D], F32), ("n2T_hi", [P, C, S], F32R), ("n2T_lo", [P, C, S], F32R),
        ("p", [P, 2, T * H, NQ], F32),
        ("mx", [P, 2, HT * H], F32), ("sm", [P, 2, HT * H], F32), ("rc", [P, 2, HT * H], F32),
        ("pT", [P, C, S], F32),
        ("o_st", [P, HT, 6], F32), ("o_mv", [P, HT, 2], F32), ("o_v", [P, 2, HT], F32), ("o_r", [P, 2, 2, HT], F32),
        ("y", [P, T, D], F32),
    ])
    xc = combine_rows(keep)
    wk, wv, wq, wo = [keep.pT[:, n * C:(n + 1) * C, :] for n in range(4)]
    bq, bk, bv = [keep.cb[:, n] for n in range(3)]
    rows_loaded = (sem.c_rows0, sem.c_rows1, sem.c_rows2, sem.c_rows3)

    def rows(e, body):
        for i in range(-1, 4):
            body(i, i % ROWS, i // ROWS)
        with e.Fori(1, B // ROWS - 1) as k:
            for s in range(ROWS):
                body(ROWS * k + s, s, k)
        for i in range(B - ROWS, B + 2):
            body(i, i % ROWS, i // ROWS)

    with nc.Block() as block:

        @block.sync
        def _(sp):
            def body(i, s, k):
                if live(i - 2):
                    sp.wait_ge(sem.oc_added, i - 1)
                    alone(sp, sem.sp_passed)
                    if after_first(i - 2):
                        sp.wait_ge(sem.oc_stored, 16 * (i - 2))
                    alone(sp, sem.sp_passed)
                    sp.dma_start(out[bass.ds(i - 2, 1)].rearrange("o (j p) d -> p (o j) d", p=P),
                                 xc[:, (s - 2) % ROWS]).then_inc(sem.oc_stored, 16)
                if live(i + 2) and not (isinstance(i, int) and i < 0):
                    if live(i - 2):
                        sp.wait_ge(sem.oc_stored, 16 * (i - 1))
                    alone(sp, sem.sp_passed)
                    load_row(sp, sem, keep, x1_dram, st_dram, i + 2, (s + 2) % ROWS)

            rows(sp, body)
            sp.wait_ge(sem.oc_stored, 16 * B)

        @block.gpsimd
        def _(pool):
            g = nc.gpsimd
            g.memset(t.bqp[:, :, :], 0.0).then_inc(sem.bqp_made, 1)
            pool.wait_ge(sem.kv_kept, 2)

            def body(i, s, k):
                if live(i + 1):
                    q = (s + 1) % ROWS
                    turn = (k if s < ROWS - 1 else k + 1) + 1
                    pool.wait_ge(rows_loaded[q], 32 * turn)
                    if not (isinstance(i, int) and i < 0):
                        pool.wait_ge(sem.t3_done, 2 * i + 2)
                    alone(pool, sem.pool_passed)
                    for j in range(T):
                        last = g.tensor_scalar(t.n2[:, j], xc[:, q, j], keep.nrm[:, q, 1, j:j + 1],
                                               keep.nrm[:, q, 0, j:j + 1], ALU.add, ALU.mult)
                    last.then_inc(sem.n2c_ready, 1)
                    if not (isinstance(i, int) and i < 0):
                        pool.wait_ge(sem.mn_done, i + 1)
                    for dst, src in ((t.kb, t.khT), (t.vb, t.vhT)):
                        for c in range(C):
                            cols = src[:, c].rearrange("p (k b) -> p b k", b=B)[:, bass.ds(i + 1, 1), :]
                            last = g.tensor_tensor(dst[:, c], cols.to_broadcast([P, HC, NQ]), keep.hmask[:, :, :],
                                                   ALU.mult)
                    last.then_inc(sem.kb_made, 1)
                if live(i - 2):
                    pool.wait_ge(sem.yc_ready, 2 * i - 2)
                    q = (s - 2) % ROWS
                    for h in range(2):
                        half = xc[:, q, h * HT:(h + 1) * HT]
                        last = g.tensor_tensor(half, half, t.y[:, h * HT:(h + 1) * HT], ALU.add)
                    last.then_inc(sem.oc_added, 1)
                if live(i):
                    for h in range(2):
                        pool.wait_ge(sem.c_rcp, 2 * i + h + 1)
                        half = t.p[:, s % 2, h * HT * H:(h + 1) * HT * H]
                        g.tensor_tensor(half, half, t.rc[:, h].unsqueeze(2).to_broadcast([P, HT * H, NQ]), ALU.mult) \
                            .then_inc(sem.c_prob, 1)
                if live(i - 1):
                    for h in range(2):
                        n = 2 * i - 2 + h
                        pool.wait_ge(sem.oc_var, n + 1)
                        g.tensor_tensor(t.o_r[:, h, 0], t.o_v[:, 0], keep.mhalf[:, 0:HT], ALU.pow).then_inc(sem.oc_pow, 1)
                        pool.wait_ge(sem.oc_pow, n + 1)
                        g.tensor_tensor(t.o_r[:, h, 1], t.o_v[:, 1], t.o_r[:, h, 0], ALU.mult).then_inc(sem.oc_norm, 1)

            rows(pool, body)

        @block.scalar
        def _(act):
            a = nc.scalar

            def body(i, s, k):
                if live(i):
                    for h, group in enumerate((GA, GB)):
                        act.wait_ge(sem.t3_done, 2 * i + h + 1)
                        if h == 0 and after_first(i):
                            act.wait_ge(sem.sc_done, 2 * i)
                        a.activation(t.n2T_hi[:, :, h * HS:(h + 1) * HS], ps[:, group:group + 2, :], ACT.Copy) \
                            .then_inc(sem.t3_hi, 1)
                if live(i):
                    exp(i, s, 0)
                if live(i - 1):
                    for h, group in enumerate((GA, GB)):
                        act.wait_ge(sem.tp_done, 2 * i - 1 + h)
                        if h == 0 and after_first(i - 1):
                            act.wait_ge(sem.oc_done, 2 * i - 2)
                        a.activation(t.pT[:, :, h * HS:(h + 1) * HS], ps[:, group:group + 2, :], ACT.Copy) \
                            .then_inc(sem.tp_kept, 1)
                if live(i):
                    exp(i, s, 1)
                if live(i - 1):
                    for h, group in enumerate((GA, GC)):
                        act.wait_ge(sem.oc_norm, 2 * i - 1 + h)
                        if h == 0 and after_first(i - 1):
                            act.wait_ge(sem.oc_added, i - 1)
                        for j in range(HT):
                            last = a.activation(t.y[:, h * HT + j], ps[:, group + j // 2, (j % 2) * D:(j % 2 + 1) * D],
                                                ACT.Identity, scale=t.o_r[:, h, 0, j:j + 1],
                                                bias=t.o_r[:, h, 1, j:j + 1])
                        last.then_inc(sem.yc_ready, 1)
                if live(i + 1):
                    act.wait_ge(sem.mn_done, i + 2)
                    a.activation(t.m_hi[:, :, :], ps[:, GB, :].rearrange("p (c q) -> p c q", c=C), ACT.Copy) \
                        .then_inc(sem.m_hi, 1)

            def exp(i, s, h):
                act.wait_ge(sem.c_sub, 2 * i + h + 1)
                half = t.p[:, s % 2, h * HT * H:(h + 1) * HT * H]
                a.activation(half, half, ACT.Exp).then_inc(sem.c_exp, 1)

            rows(act, body)

        @block.vector
        def _(dve):
            v = nc.vector
            dve.wait_ge(sem.c_w, 16 * 8)
            dve.wait_ge(sem.kv_done, 1)
            for bank, dst, bias in ((0, t.khT, bk), (1, t.vhT, bv)):
                for c in range(C):
                    last = v.tensor_scalar(dst[:, c], ps[:, bank, c * TOK:(c + 1) * TOK], bias[:, c:c + 1], None,
                                           ALU.add)
                last.then_inc(sem.kv_kept, 1)
            dve.wait_ge(sem.wqT_done, 1)
            v.tensor_scalar(t.wqT[:, :, :], ps[:, 4:6, 0:D], KEY_SCALE, None, ALU.mult).then_inc(sem.wqT_kept, 1)
            v.tensor_scalar(keep.bo_rep[:, :], keep.bo_rep[:, :], 1.0 / H, None, ALU.mult).then_inc(sem.bo_made, 1)
            dve.wait_ge(sem.bqp_made, 1)
            v.tensor_scalar(t.bqp[:, :, 0:64:32], bq.unsqueeze(2).to_broadcast([P, C, 2]), KEY_SCALE, None,
                            ALU.mult)
            v.tensor_copy(t.crow[:, :], keep.zero[:, :]).then_inc(sem.bqp_made, 1)
            dve.wait_ge(sem.bqp_made, 2)
            dve.wait_ge(sem.bo_made, 1)

            def body(i, s, k):
                if live(i):
                    for h, group in enumerate((GA, GB)):
                        dve.wait_ge(sem.t3_hi, 2 * i + h + 1)
                        half = slice(h * HS, (h + 1) * HS)
                        v.tensor_tensor(t.n2T_lo[:, :, half], ps[:, group:group + 2, :], t.n2T_hi[:, :, half],
                                        ALU.subtract).then_inc(sem.t3_lo, 1)
                    for h, group in enumerate((GC, GD)):
                        n = 2 * i + h
                        scores = ps[:, group:group + 2, :].rearrange("p b (g q) -> p (b g) q", q=NQ)
                        dve.wait_ge(sem.sc_done, n + 1)
                        v.tensor_reduce(t.mx[:, h], scores, AX, ALU.max).then_inc(sem.c_max, 1)
                        dve.wait_ge(sem.c_max, n + 1)
                        v.tensor_tensor(t.p[:, s % 2, h * HT * H:(h + 1) * HT * H], scores,
                                        t.mx[:, h].unsqueeze(2).to_broadcast([P, HT * H, NQ]), ALU.subtract) \
                            .then_inc(sem.c_sub, 1)
                    for h in range(2):
                        n = 2 * i + h
                        dve.wait_ge(sem.c_exp, n + 1)
                        v.tensor_reduce(t.sm[:, h], t.p[:, s % 2, h * HT * H:(h + 1) * HT * H], AX, ALU.add) \
                            .then_inc(sem.c_sum, 1)
                        dve.wait_ge(sem.c_sum, n + 1)
                        if after_first(i):
                            dve.wait_ge(sem.c_prob, n - 1)
                        v.reciprocal(t.rc[:, h], t.sm[:, h]).then_inc(sem.c_rcp, 1)
                if live(i - 1):
                    for h, group in enumerate((GA, GC)):
                        n = 2 * i - 2 + h
                        dve.wait_ge(sem.oc_done, n + 1)
                        for j in range(HT):
                            last = v.bn_stats(t.o_st[:, j], ps[:, group + j // 2, (j % 2) * D:(j % 2 + 1) * D])
                        last.then_inc(sem.oc_stats, 1)
                        dve.wait_ge(sem.oc_stats, n + 1)
                        alone(dve, sem.dve_passed)
                        for j in range(HT):
                            last = v.bn_aggr(t.o_mv[:, j], t.o_st[:, j])
                        last.then_inc(sem.oc_mv, 1)
                        dve.wait_ge(sem.oc_mv, n + 1)
                        if h == 1 or after_first(i - 1):
                            dve.wait_ge(sem.oc_norm, n)
                        v.tensor_scalar(t.o_v[:, 0], t.o_mv[:, :, 1], EPS, None, ALU.add)
                        v.tensor_scalar(t.o_v[:, 1], t.o_mv[:, :, 0], -1.0, None, ALU.mult).then_inc(sem.oc_var, 1)
                if live(i + 1):
                    dve.wait_ge(sem.mn_done, i + 2)
                    v.tensor_copy(t.crow_t[32:64, :], ps[32:64, GD, 0:HQ]).then_inc(sem.cr_hi, 1)
                    v.tensor_copy(t.crow[0:32, :], ps[0:32, GD, 0:HQ])
                    v.tensor_tensor(t.nv[:, (s + 1) % 2], ps[:, GB + 1, :].rearrange("p (c d) -> p c d", c=C),
                                    keep.bo_rep[:, :].unsqueeze(1).to_broadcast([P, C, D]), ALU.add) \
                        .then_inc(sem.n_kept, 1)
                    dve.wait_ge(sem.cr_hi, i + 2)
                    v.tensor_tensor(t.crow[32:64, :], ps[32:64, GD, 0:HQ], t.crow_t[32:64, :], ALU.subtract) \
                        .then_inc(sem.cr_kept, 1)
                    dve.wait_ge(sem.m_hi, i + 2)
                    v.tensor_tensor(t.m_lo[:, :, :], ps[:, GB, :].rearrange("p (c q) -> p c q", c=C), t.m_hi[:, :, :],
                                    ALU.subtract).then_inc(sem.m_kept, 1)

            rows(dve, body)

        @block.tensor
        def _(pe):
            mm, tr = nc.tensor.matmul, nc.tensor.transpose
            pe.wait_ge(sem.c_w, 16 * 8)
            for bank, w in ((0, wk), (1, wv)):
                for f in range(C):
                    for c in range(C):
                        last = mm(ps[:, bank, f * TOK:(f + 1) * TOK], w[:, c, f * P:(f + 1) * P], keep.o2T[:, c],
                                  start=(c == 0), stop=(c == C - 1))
            last.then_inc(sem.kv_done, 1)
            for f in range(C):
                for c in range(C):
                    last = tr(ps[:, 4 + f, c * P:(c + 1) * P], wq[:, c, f * P:(f + 1) * P], keep.ident[:, :])
            last.then_inc(sem.wqT_done, 1)
            pe.wait_ge(sem.wqT_kept, 1)
            pe.wait_ge(sem.bqp_made, 2)

            def body(i, s, k):
                if live(i):
                    for h, group in enumerate((GA, GB)):
                        if h == 0:
                            pe.wait_ge(sem.n2c_ready, i + 1)
                            if live(i - 2):
                                pe.wait_ge(sem.yc_ready, 2 * i - 3)
                        else:
                            pe.wait_ge(sem.m_kept, i + 1)
                            pe.wait_ge(sem.n_kept, i + 1)
                        for j in range(HT):
                            for c in range(C):
                                last = tr(ps[:, group + c, j * P:(j + 1) * P],
                                          t.n2[:, h * HT + j, c * P:(c + 1) * P], keep.ident[:, :])
                        last.then_inc(sem.t3_done, 1)
                    for h, group in enumerate((GC, GD)):
                        pe.wait_ge(sem.t3_lo, 2 * i + h + 1)
                        if h == 0:
                            pe.wait_ge(sem.cr_kept, i + 1)
                            if live(i - 2):
                                pe.wait_ge(sem.yc_ready, 2 * i - 2)
                        for b in range(2):
                            mm(ps[:, group + b, :], keep.selrow[:, :],
                               t.crow[:, :].unsqueeze(1).to_broadcast([P, 2, HQ]), start=True, stop=False,
                               skip_group_check=True)
                            for jj in range(2):
                                at = slice((h * HT + 2 * b + jj) * P, (h * HT + 2 * b + jj + 1) * P)
                                for c in range(C):
                                    last = three_passes(nc, ps[:, group + b, jj * HQ:(jj + 1) * HQ],
                                                        t.n2T_hi[:, c, at], t.n2T_lo[:, c, at],
                                                        t.m_hi[:, c], t.m_lo[:, c], False, c == C - 1, skip=True)
                        last.then_inc(sem.sc_done, 1)
                if live(i - 1):
                    for h, group in enumerate((GA, GB)):
                        pe.wait_ge(sem.c_prob, 2 * i - 1 + h)
                        if not live(i) and h == 0 and live(i - 2):
                            pe.wait_ge(sem.yc_ready, 2 * i - 2)
                        for j in range(HT):
                            src = t.p[:, (s + 1) % 2, (h * HT + j) * H:(h * HT + j + 1) * H].rearrange("p g q -> p (g q)")
                            for c in range(C):
                                last = tr(ps[:, group + c, j * P:(j + 1) * P], src[:, c * P:(c + 1) * P],
                                          keep.ident[:, :])
                        last.then_inc(sem.tp_done, 1)
                    for h, group in enumerate((GA, GC)):
                        pe.wait_ge(sem.tp_kept, 2 * i - 1 + h)
                        if h == 1 and live(i):
                            pe.wait_ge(sem.c_sub, 2 * i + 1)
                        for j in range(HT):
                            for c in range(C):
                                last = mm(ps[:, group + j // 2, (j % 2) * D:(j % 2 + 1) * D],
                                          t.pT[:, c, (h * HT + j) * P:(h * HT + j + 1) * P],
                                          t.nv[:, (s + 1) % 2, c], start=(c == 0), stop=(c == C - 1))
                        last.then_inc(sem.oc_done, 1)
                if live(i + 1):
                    pe.wait_ge(sem.kb_made, i + 2)
                    if live(i - 1):
                        pe.wait_ge(sem.tp_kept, 2 * i)
                    elif live(i):
                        pe.wait_ge(sem.t3_lo, 2 * i + 2)
                    if live(i):
                        pe.wait_ge(sem.c_sub, 2 * i + 2)
                    for f in range(C):
                        kb = t.kb[:, f].rearrange("p h q -> p (h q)")
                        for c in range(C):
                            mm(ps[:, GB, c * HQ + f * P:c * HQ + (f + 1) * P], t.wqT[:, f, c * P:(c + 1) * P], kb,
                               start=True, stop=True)
                        mm(ps[:, GB + 1, f * D:(f + 1) * D], t.vb[:, f].rearrange("p h q -> p (h q)"), wo[:, f],
                           start=True, stop=True)
                        last = mm(ps[0:64, GD, f * P:(f + 1) * P], t.bqp[:, f], kb, start=True, stop=True)
                    last.then_inc(sem.mn_done, 1)

            rows(pe, body)


_INS = ['L0_attn_x', 'L0_attn_Wz', 'L0_attn_bz', 'L0_attn_Wh', 'L0_attn_bh', 'L0_ffn_slot_query',
        'L0_ffn_d_Wq', 'L0_ffn_d_Wk', 'L0_ffn_d_Wv', 'L0_ffn_d_Wo', 'L0_ffn_d_bq', 'L0_ffn_d_bk', 'L0_ffn_d_bv',
        'L0_ffn_d_bo', 'L0_ffn_c_Wq', 'L0_ffn_c_Wk', 'L0_ffn_c_Wv', 'L0_ffn_c_Wo', 'L0_ffn_c_bq', 'L0_ffn_c_bk',
        'L0_ffn_c_bv', 'L0_ffn_c_bo', 'L0_ffn_e_ln_g', 'L0_ffn_e_ln_b', 'L0_ffn_e_W1', 'L0_ffn_e_b1',
        'L0_ffn_e_Wg', 'L0_ffn_e_bg', 'L0_ffn_e_W2', 'L0_ffn_e_b2']


def kernel(**inputs):
    import numpy as _np
    import concourse.bacc as _bacc
    from concourse import mybir as _mybir
    from concourse.bass_utils import run_bass_kernel_spmd as _run

    nc = _bacc.Bacc("TRN2", target_bir_lowering=False, num_devices=1)
    arrays, args = {}, []
    for name in _INS:
        a = _np.ascontiguousarray(inputs[name])
        arrays[f"in_{name}_dram"] = a
        args.append(nc.dram_tensor(f"in_{name}_dram", a.shape, _mybir.dt.from_np(a.dtype), kind="ExternalInput").ap())
    out = nc.dram_tensor("out_0_dram", (B, S, D), _mybir.dt.float32, kind="ExternalOutput").ap()
    mixer_moe(nc, *args, out)
    r = _run(nc, [arrays], core_ids=[0])
    return r.results[0]["out_0_dram"]
```

```python
from collections import namedtuple
from contextlib import ExitStack

import concourse.bass as bass
from concourse import mybir

F32 = mybir.dt.float32
F32R = mybir.dt.float32r
ALU = mybir.AluOpType
ACT = mybir.ActivationFunctionType
AX = mybir.AxisListType.X

P = 128
B, S, D = 16, 1024, 256
C = D // P
T = S // P
HT = T // 2
HS = S // 2
H, NQ = 16, 16
DH = D // H
HC = P // DH
HQ = H * NQ
E, F = 16, 1024
FK = F // P
EPS = 1e-5
KEY_SCALE = 0.25
SLOTS = 4
ROWS = 4

SEMAPHORES = """
sp_passed pool_passed dve_passed
ident_built consts_built w_loaded sel_built x_loaded0 x_loaded1 split_w zeroed
sqT_done sqT_kept qT_done qT_kept wkT_done wkT_kept qb_built mk_done mk_hi mk_kept
x_stats x_mv x_var x_pow n_ready
tn_done tn_hi tn_lo
z_done hh_done z_sig a_sig b_made h_scanned
th_done th_stats th_mv th_var th_pow th_norm y_ready x1_ready
x1_stored0 x1_stored1 st_stored x1_stats x1_mv x1_var x1_pow n2_ready
t2_done t2_hi t2_lo
s_done s_max mt_done mt_red mt_sum mt_kept mr_done mr_hi mr_kept ga_done p_ready
u_done u_rcp u_kept tu_done ut_kept
ew0 ew1 ew2 ew3 ew4 ew5 last_w1 last_wg last_w2
slot_w slot_bv slot_small slot_bias pads_zero banks_zero spread_made ln_spread ao_done ao_kept o_done o_kept o_stats o_mv o_var o_pow
o_centred o_scaled o_ln b2t_done b2t_kept ot_done ot_kept
xe_made ug_done ug_silu hg_made hgt_done hgt_kept y_done y_kept yt_done y_summed o2_made
c_w c_rows0 c_rows1 c_rows2 c_rows3 kv_done kv_kept wqT_done wqT_kept bqp_made bo_made
n2c_ready kb_made mn_done cr_done m_hi m_kept n_kept cr_hi cr_kept
t3_done t3_hi t3_lo sc_done c_max c_sub c_exp c_sum c_rcp c_prob tp_done tp_kept
oc_done oc_stats oc_mv oc_var oc_pow oc_norm yc_ready oc_added oc_stored last_prob last_added
"""


def live(b):
    return not isinstance(b, int) or 0 <= b < B


def after_first(b):
    return not isinstance(b, int) or b > 0


def last_row(b):
    return isinstance(b, int) and b == B - 1


def row(ap, b):
    return ap[bass.ds(b, 1)].rearrange("o p n -> (o p) n")


def mixer_moe(nc, x, Wz, bz, Wh, bh, slot_query, d_Wq, d_Wk, d_Wv, d_Wo, d_bq, d_bk, d_bv, d_bo,
              c_Wq, c_Wk, c_Wv, c_Wo, c_bq, c_bk, c_bv, c_bo,
              e_ln_g, e_ln_b, e_W1, e_b1, e_Wg, e_bg, e_W2, e_b2, out):
    x1_dram = nc.dram_tensor("x1_rows", [B, P, T * D], F32, kind="Internal").ap()
    st_dram = nc.dram_tensor("x1_norms", [B, P, 2 * T], F32, kind="Internal").ap()
    with ExitStack() as ctx:
        names = SEMAPHORES.split()
        sem = namedtuple("Semaphores", names)(*[ctx.enter_context(nc.semaphore(n)) for n in names])
        ps = ctx.enter_context(nc.psum_tensor("ps", [P, 8, 512], F32))
        keep = tensors(nc, ctx, "keep", [
            ("ident", [P, P], F32), ("hmask", [P, HC, DH], F32), ("selrow", [P, P], F32R),
            ("zero", [P, D], F32), ("mhalf", [P, T], F32),
            ("UT", [P, C, HQ, B], F32),
            ("pT", [P, T, HQ], F32),
            ("nrm", [P, ROWS, 2, T], F32), ("cb", [P, 3, C], F32), ("bo_rep", [P, D], F32),
            ("w1_0", [P, C, F], F32), ("wg_0", [P, C, F], F32), ("w2_0", [P, FK, D], F32),
            ("o2T", [P, C, NQ * B], F32),
        ])
        with ExitStack() as inner:
            both = tensors(nc, inner, "both", [
                ("xt", [P, 2, T, D], F32),
                ("x1", [P, 2, T, D], F32),
                ("n", [P, T, D], F32),
                ("a", [P, C, S], F32),
                ("hT", [P, C, S], F32),
                ("y", [P, T, D], F32),
                ("z", [P, 2, HS], F32),
            ])
            ring = expert_slots(keep, both)
            with ExitStack() as innermost:
                dispatch_phase(nc, innermost, sem, ps, keep, both, ring, x, Wz, bz, Wh, bh, slot_query,
                               d_Wq, d_Wk, d_Wv, d_bq, d_bk, e_W1, e_Wg, e_W2, x1_dram, st_dram)
            with ExitStack() as innermost:
                expert_phase(nc, innermost, sem, ps, keep, both, ring, slot_query, d_Wo, d_bv, d_bo,
                             e_ln_g, e_ln_b, e_W1, e_b1, e_Wg, e_bg, e_W2, e_b2,
                             c_Wq, c_Wk, c_Wv, c_Wo, c_bq, c_bk, c_bv, c_bo, x1_dram, st_dram)
        with ExitStack() as inner:
            combine_phase(nc, inner, sem, ps, keep, x1_dram, st_dram, out)


def expert_slots(keep, both):
    def halves(ap):
        return ap.rearrange("p (c a) d -> p c (a d)", c=C)
    return [[keep.w1_0[:, :, :], keep.wg_0[:, :, :], keep.w2_0[:, :, :]],
            [halves(both.xt[:, 0]), halves(both.xt[:, 1]), both.n[:, :, :]],
            [both.a[:, :, :], both.hT[:, :, :], both.y[:, :, :]],
            [halves(both.x1[:, 0]), halves(both.x1[:, 1]), None]]


def wv_place(both):
    return both.z[:, 0, :].rearrange("p (c n) -> p c n", n=D)


def load_expert(sp, sem, ring, k, e, e_W1, e_Wg, e_W2, parts=(0, 1, 2)):
    slot = (sem.ew0, sem.ew1, sem.ew2, sem.ew3, sem.ew4, sem.ew5)[k]
    arrived = (sem.last_w1, sem.last_wg, sem.last_w2) if isinstance(e, int) and e == E - 1 else (slot,) * 3
    sources = ((e_W1, "o (c p) f -> p (o c) f"), (e_Wg, "o (c p) f -> p (o c) f"), (e_W2, "o (k p) d -> p (o k) d"))
    for n in parts:
        w, rule = sources[n]
        sp.dma_start(ring[k][n], w[bass.ds(e, 1)].rearrange(rule, p=P)).then_inc(arrived[n], 16)


def combine_rows(keep):
    return keep.UT[:, :, :, :].rearrange("p c q b -> p (c q b)").rearrange("p (s j d) -> p s j d", s=ROWS, d=D)


def load_row(sp, sem, keep, x1_dram, st_dram, b, s):
    loaded = (sem.c_rows0, sem.c_rows1, sem.c_rows2, sem.c_rows3)[s]
    sp.dma_start(combine_rows(keep)[:, s].rearrange("p j d -> p (j d)"), row(x1_dram, b)).then_inc(loaded, 16)
    sp.dma_start(keep.nrm[:, s].rearrange("p a j -> p (a j)"), row(st_dram, b)).then_inc(loaded, 16)


def alone(e, passed):
    e.sem_inc(passed, 1)


def tensors(nc, ctx, phase, specs):
    got = [ctx.enter_context(nc.sbuf_tensor(f"{phase}_{n}", shape, dtype)) for n, shape, dtype in specs]
    return namedtuple("Tensors", [n for n, _, _ in specs])(*got)


def three_passes(nc, dst, w_hi, w_lo, a_hi, a_lo, first, last, skip=False):
    nc.tensor.matmul(dst, w_hi, a_hi, start=first, stop=False, skip_group_check=skip)
    nc.tensor.matmul(dst, w_hi, a_lo, start=False, stop=False, skip_group_check=skip)
    return nc.tensor.matmul(dst, w_lo, a_hi, start=False, stop=last, skip_group_check=skip)


def dispatch_phase(nc, ctx, sem, ps, keep, both, ring, x, Wz, bz, Wh, bh, slot_query,
                   d_Wq, d_Wk, d_Wv, d_bq, d_bk, e_W1, e_Wg, e_W2, x1_dram, st_dram):
    t = tensors(nc, ctx, "dispatch", [
        ("nT_hi", [P, C, S], F32R), ("nT_lo", [P, C, S], F32R),
        ("n2", [P, 2, T, D + 4], F32),
        ("n2T_hi", [P, C, S], F32R), ("n2T_lo", [P, C, S], F32R),
        ("u", [P, 2, D], F32),
        ("wz_hi", [P, C, D], F32R), ("wz_lo", [P, C, D], F32R),
        ("wh_hi", [P, C, D], F32R), ("wh_lo", [P, C, D], F32R),
        ("mk_hi", [P, C, HQ], F32R), ("mk_lo", [P, C, HQ], F32R),
        ("sqT", [P, C, NQ], F32), ("qT", [P, C, NQ], F32),
        ("qb", [P, C, HC, NQ], F32),
        ("bz", [P, C], F32), ("nbz", [P, C], F32), ("bh", [P, C], F32),
        ("bq", [P, C], F32), ("bk", [P, C], F32),
        ("ccol", [P, 2], F32),
        ("x_st", [P, T, 6], F32), ("x_mv", [P, T, 2], F32), ("x_v", [P, 2, T], F32), ("x_r", [P, T], F32),
        ("h_st", [P, HT, 6], F32), ("h_mv", [P, HT, 2], F32), ("h_v", [P, 2, 2, HT], F32),
        ("h_r", [P, 2, 2, HT], F32),
        ("x1_st", [P, T, 6], F32), ("x1_mv", [P, T, 2], F32), ("x1_v", [P, T], F32),
        ("x1_n", [P, 2, 2, T], F32),
        ("mx", [P, 2, HQ], F32), ("mcol", [P, 2], F32), ("mcol2", [P, 2], F32), ("mcolp", [P, 2, 64], F32),
        ("grow", [P, HQ], F32R), ("grow_t", [64, HQ], F32R),
        ("rcp", [P, 2], F32),
    ])
    wq, wk = both.a[:, :, 0:D], both.a[:, :, D:2 * D]
    wz, wh, wkT = both.y[:, 0:2, :], both.y[:, 2:4, :], both.y[:, 4:6, :]
    sq, sel32 = both.y[0:NQ, 6, :], both.y[:, 7, 0:P]
    x_loaded, x1_stored = (sem.x_loaded0, sem.x_loaded1), (sem.x1_stored0, sem.x1_stored1)
    s_all = ps[:, 4:8, :].rearrange("p k n -> p (k n)")
    s_tile = s_all.rearrange("p (j q) -> p j q", q=HQ)
    BANK = (2, 0)

    def rows(e, body, closing=None):
        for i in range(4):
            body(i, i % 2, i // 2)
        with e.Fori(2, B // 2 - 1) as k:
            body(2 * k, 0, k)
            body(2 * k + 1, 1, k)
        for i in range(B - 2, B if closing else B + 2):
            body(i, i % 2, i // 2)
        if closing:
            closing(B - 2, B - 1)

    with nc.Block() as block:

        @block.sync
        def _(sp):
            sp.dma_start(both.xt[:, 0], x[0].rearrange("(j p) d -> p j d", p=P)).then_inc(x_loaded[0], 16)
            sp.dma_start(sq, slot_query.rearrange("o q d -> (o q) d")).then_inc(sem.w_loaded, 16)
            for dst, src in ((wq, d_Wq), (wk, d_Wk), (wz, Wz), (wh, Wh)):
                sp.dma_start(dst, src.rearrange("(c p) n -> p c n", p=P)).then_inc(sem.w_loaded, 16)
            for dst, src in ((t.bz, bz), (t.bh, bh), (t.bq, d_bq), (t.bk, d_bk)):
                sp.dma_start(dst[:, :], src.rearrange("(c p) -> p c", p=P), allow_slow_non_contiguous=True) \
                    .then_inc(sem.w_loaded, 16)
            sp.dma_start(both.xt[:, 1], x[1].rearrange("(j p) d -> p j d", p=P)).then_inc(x_loaded[1], 16)

            def body(i, s, k):
                o = 1 - s
                if live(i - 1):
                    sp.wait_ge(sem.x1_ready, 2 * i)
                    alone(sp, sem.sp_passed)
                    if live(i + 1):
                        sp.dma_start(both.xt[:, o], x[bass.ds(i + 1, 1)].rearrange("o (j p) d -> p (o j) d", p=P)) \
                            .then_inc(x_loaded[o], 16)
                    sp.dma_start(row(x1_dram, i - 1), both.x1[:, o].rearrange("p j d -> p (j d)")) \
                        .then_inc(x1_stored[o], 16)
                    if isinstance(i, int) and i == 2:
                        load_expert(sp, sem, ring, 0, 0, e_W1, e_Wg, e_W2)
                    if isinstance(i, int) and i == B:
                        sp.dma_start(wv_place(both), d_Wv.rearrange("(c p) n -> p c n", p=P)).then_inc(sem.slot_w, 16)
                        load_expert(sp, sem, ring, 1, 1, e_W1, e_Wg, e_W2)
                        load_expert(sp, sem, ring, 2, 2, e_W1, e_Wg, e_W2)
                    sp.wait_ge(sem.x1_pow, i)
                    alone(sp, sem.sp_passed)
                    if after_first(i - 1):
                        sp.wait_ge(sem.st_stored, 16 * (i - 1))
                    alone(sp, sem.sp_passed)
                    sp.dma_start(row(st_dram, i - 1), t.x1_n[:, o].rearrange("p a j -> p (a j)")) \
                        .then_inc(sem.st_stored, 16)
                    if isinstance(i, int) and i == B:
                        sp.wait_ge(sem.n2_ready, 2 * B - 2)
                        sp.wait_ge(x1_stored[s], 16 * (B // 2))
                        load_expert(sp, sem, ring, 3, 3, e_W1, e_Wg, e_W2, parts=(0,))

            rows(sp, body)
            sp.wait_ge(sem.n2_ready, 2 * B)
            sp.wait_ge(x1_stored[(B - 1) % 2], 16 * (B // 2))
            load_expert(sp, sem, ring, 3, 3, e_W1, e_Wg, e_W2, parts=(1,))
            sp.wait_ge(x1_stored[0], 16 * (B // 2))
            sp.wait_ge(x1_stored[1], 16 * (B // 2))
            sp.wait_ge(sem.st_stored, 16 * B)

        @block.gpsimd
        def _(pool):
            g = nc.gpsimd
            g.memset(keep.ident[:, :], 0.0).then_inc(sem.ident_built, 1)
            g.memset(keep.hmask[:, :, :], 1.0).then_inc(sem.ident_built, 1)
            g.memset(keep.mhalf[:, :], -0.5)
            g.memset(keep.zero[:, :], 0.0)
            g.memset(t.mcolp[:, :, :], 0.0)
            g.memset(t.n2[:, 0, :, D:D + 4], 1.0)
            g.memset(t.n2[:, 1, :, D:D + 4], 1.0).then_inc(sem.zeroed, 1)
            pool.wait_ge(sem.ident_built, 2)
            g.affine_select(out=keep.ident[:, :], in_=keep.ident[:, :], compare_op=ALU.not_equal, fill=1.0,
                            base=0, pattern=[[-1, P]], channel_multiplier=1).then_inc(sem.ident_built, 1)
            g.affine_select(out=keep.hmask[:, :, :], in_=keep.hmask[:, :, :], compare_op=ALU.is_ge, fill=0.0,
                            base=0, pattern=[[-DH, HC], [0, DH]], channel_multiplier=1).then_inc(sem.ident_built, 1)
            pool.wait_ge(sem.ident_built, 4)
            g.affine_select(out=keep.hmask[:, :, :], in_=keep.hmask[:, :, :], compare_op=ALU.is_ge, fill=0.0,
                            base=DH - 1, pattern=[[DH, HC], [0, DH]], channel_multiplier=-1) \
                .then_inc(sem.consts_built, 1)

            def norm_x(b, s, h):
                if h == 0:
                    pool.wait_ge(sem.x_var, b + 1)
                    g.tensor_tensor(t.x_r[:, :], t.x_v[:, 0], keep.mhalf[:, :], ALU.pow).then_inc(sem.x_pow, 1)
                    pool.wait_ge(sem.x_pow, b + 1)
                    if after_first(b):
                        pool.wait_ge(sem.tn_done, 2 * b)
                    alone(pool, sem.pool_passed)
                for j in range(h * HT, (h + 1) * HT):
                    last = g.tensor_scalar(both.n[:, j], both.xt[:, s, j], t.x_v[:, 1, j:j + 1], t.x_r[:, j:j + 1],
                                           ALU.add, ALU.mult)
                last.then_inc(sem.n_ready, 1)

            def norm_h(i, h):
                pool.wait_ge(sem.th_var, 2 * i + h + 1)
                g.tensor_tensor(t.h_r[:, h, 0], t.h_v[:, h, 0], keep.mhalf[:, 0:HT], ALU.pow) \
                    .then_inc(sem.th_pow, 1)
                pool.wait_ge(sem.th_pow, 2 * i + h + 1)
                g.tensor_tensor(t.h_r[:, h, 1], t.h_v[:, h, 1], t.h_r[:, h, 0], ALU.mult).then_inc(sem.th_norm, 1)

            def residual(i, s, k, h):
                if h == 0 and live(i - 2):
                    pool.wait_ge(x1_stored[s], 16 * k)
                    alone(pool, sem.pool_passed)
                pool.wait_ge(sem.y_ready, 2 * i + h + 1)
                half = slice(h * HT, (h + 1) * HT)
                g.tensor_tensor(both.x1[:, s, half], both.xt[:, s, half], both.y[:, half], ALU.add).then_inc(sem.x1_ready, 1)

            def body(i, s, k):
                o = 1 - s
                if live(i - 1):
                    pool.wait_ge(sem.x1_var, i)
                    if live(i - 3) and after_first(i - 2):
                        pool.wait_ge(sem.st_stored, 16 * (i - 2))
                    g.tensor_tensor(t.x1_n[:, o, 0], t.x1_v[:, :], keep.mhalf[:, :], ALU.pow) \
                        .then_inc(sem.x1_pow, 1)
                    pool.wait_ge(sem.x1_pow, i)
                    if live(i - 3):
                        pool.wait_ge(sem.u_done, 2 * i - 4)
                    alone(pool, sem.pool_passed)
                    for j in range(T):
                        last = g.tensor_scalar(t.n2[:, o, j, 0:D], both.x1[:, o, j], t.x1_n[:, o, 1, j:j + 1],
                                               t.x1_n[:, o, 0, j:j + 1], ALU.add, ALU.mult)
                        if j % HT == HT - 1:
                            last.then_inc(sem.n2_ready, 1)
                if live(i + 1):
                    norm_x(i + 1, o, 0)
                if live(i):
                    norm_h(i, 0)
                if live(i + 1):
                    norm_x(i + 1, o, 1)
                if live(i):
                    norm_h(i, 1)
                    residual(i, s, k, 0)
                    residual(i, s, k, 1)

            norm_x(0, 0, 0)
            norm_x(0, 0, 1)
            rows(pool, body)

        @block.scalar
        def _(act):
            a = nc.scalar
            act.wait_ge(sem.w_loaded, 16 * 9)
            a.activation(t.nbz[:, :], t.bz[:, :], ACT.Copy, scale=-1.0).then_inc(sem.split_w, 1)
            act.wait_ge(sem.split_w, 1)

            def keep_hi(dst, bank, h, done, n, out_sem):
                act.wait_ge(done, n)
                a.activation(dst[:, :, h * HS:(h + 1) * HS], ps[:, bank:bank + 2, :], ACT.Copy) \
                    .then_inc(out_sem, 1)

            def keep_u(b, m, bank=4):
                act.wait_ge(sem.u_rcp, 2 * b + m + 1)
                if after_first(b):
                    act.wait_ge(sem.tu_done, b)
                a.activation(t.u[:, m], ps[:, bank + m, 0:D], ACT.Copy, scale=t.rcp[:, m:m + 1]).then_inc(sem.u_kept, 1)

            def exponentials(b):
                act.wait_ge(sem.ga_done, b + 1)
                if after_first(b):
                    act.wait_ge(sem.u_done, 2 * b)
                a.activation(keep.pT[:, :, :].rearrange("p j q -> p (j q)"), s_all, ACT.Exp).then_inc(sem.p_ready, 1)

            def gate(i, m):
                e, h, bank = m % 2, m // 2, BANK[m % 2]
                act.wait_ge(sem.z_done, 4 * i + m + 1)
                if m >= 2 or after_first(i):
                    act.wait_ge(sem.b_made, 4 * i + m - 1)
                a.activation(both.z[:, m % 2], ps[:, bank, :], ACT.Sigmoid, bias=t.bz[:, e:e + 1]) \
                    .then_inc(sem.z_sig, 1)
                if m == 0 and after_first(i):
                    act.wait_ge(sem.h_scanned, 4 * i)
                a.activation(both.a[:, e, h * HS:(h + 1) * HS], ps[:, bank, :], ACT.Sigmoid,
                             bias=t.nbz[:, e:e + 1], scale=-1.0).then_inc(sem.a_sig, 1)

            def centre_h(i, h):
                act.wait_ge(sem.th_norm, 2 * i + h + 1)
                if after_first(i):
                    act.wait_ge(sem.x1_ready, 2 * i + h - 1)
                for j in range(HT):
                    last = a.activation(both.y[:, h * HT + j],
                                        ps[:, BANK[h] + j // 2, (j % 2) * D:(j % 2 + 1) * D],
                                        ACT.Identity, scale=t.h_r[:, h, 0, j:j + 1], bias=t.h_r[:, h, 1, j:j + 1])
                last.then_inc(sem.y_ready, 1)

            def body(i, s, k):
                if live(i):
                    for h in range(2):
                        if h == 0 and after_first(i):
                            act.wait_ge(sem.hh_done, 4 * i)
                        keep_hi(t.nT_hi, BANK[h], h, sem.tn_done, 2 * i + h + 1, sem.tn_hi)
                    if isinstance(i, int) and i == 0:
                        act.wait_ge(sem.mk_done, 1)
                        a.activation(t.mk_hi[:, :, :], ps[:, 4, :].rearrange("p (c q) -> p c q", c=C), ACT.Copy) \
                            .then_inc(sem.mk_hi, 1)
                    for m in range(3):
                        gate(i, m)
                if live(i - 2):
                    exponentials(i - 2)
                if live(i):
                    gate(i, 3)
                if live(i - 2):
                    keep_u(i - 2, 0)
                if live(i - 1):
                    if after_first(i - 1):
                        act.wait_ge(sem.s_done, 2 * i - 2)
                    keep_hi(t.n2T_hi, 6, 0, sem.t2_done, 2 * i - 1, sem.t2_hi)
                if live(i - 2):
                    keep_u(i - 2, 1)
                if live(i - 1):
                    keep_hi(t.n2T_hi, 6, 1, sem.t2_done, 2 * i, sem.t2_hi)
                if live(i):
                    centre_h(i, 0)
                if live(i):
                    centre_h(i, 1)

            def closing(b, last):
                exponentials(b)
                act.wait_ge(sem.s_done, 2 * b + 2)
                keep_hi(t.n2T_hi, 0, 0, sem.t2_done, 2 * last + 1, sem.t2_hi)
                keep_hi(t.n2T_hi, 6, 1, sem.t2_done, 2 * last + 2, sem.t2_hi)
                keep_u(b, 0, bank=2)
                keep_u(b, 1, bank=2)
                exponentials(last)
                keep_u(last, 0)
                keep_u(last, 1)

            rows(act, body, closing)

        @block.vector
        def _(dve):
            v = nc.vector
            def stats_x(b, s, count):
                dve.wait_ge(x_loaded[s], 16 * count)
                for j in range(T):
                    last = v.bn_stats(t.x_st[:, j], both.xt[:, s, j])
                last.then_inc(sem.x_stats, 1)
                dve.wait_ge(sem.x_stats, b + 1)
                alone(dve, sem.dve_passed)
                for j in range(T):
                    last = v.bn_aggr(t.x_mv[:, j], t.x_st[:, j])
                last.then_inc(sem.x_mv, 1)
                dve.wait_ge(sem.x_mv, b + 1)
                if after_first(b):
                    dve.wait_ge(sem.n_ready, 2 * b)
                v.tensor_scalar(t.x_v[:, 0], t.x_mv[:, :, 1], EPS, None, ALU.add)
                v.tensor_scalar(t.x_v[:, 1], t.x_mv[:, :, 0], -1.0, None, ALU.mult).then_inc(sem.x_var, 1)

            stats_x(0, 0, 1)
            dve.wait_ge(sem.w_loaded, 16 * 9)
            v.tensor_copy(t.wz_hi[:, :, :], wz)
            v.tensor_copy(t.wh_hi[:, :, :], wh).then_inc(sem.split_w, 1)
            dve.wait_ge(sem.split_w, 2)
            v.tensor_tensor(t.wz_lo[:, :, :], wz, t.wz_hi[:, :, :], ALU.subtract)
            v.tensor_tensor(t.wh_lo[:, :, :], wh, t.wh_hi[:, :, :], ALU.subtract).then_inc(sem.split_w, 1)
            v.memset(sel32, 0.0).then_inc(sem.sel_built, 1)
            dve.wait_ge(sem.sel_built, 1)
            v.memset(sel32[0:1, :], 1.0)
            v.memset(sel32[32:33, :], 1.0).then_inc(sem.sel_built, 1)
            dve.wait_ge(sem.sel_built, 2)
            dve.wait_ge(sem.zeroed, 1)
            v.tensor_copy(keep.selrow[:, :], sel32)
            v.tensor_copy(t.grow[:, :], keep.zero[:, :]).then_inc(sem.split_w, 1)
            dve.wait_ge(sem.sqT_done, 1)
            v.tensor_copy(t.sqT[:, :, :], ps[:, 0, 0:C * NQ].rearrange("p (c q) -> p c q", c=C)).then_inc(sem.sqT_kept, 1)
            dve.wait_ge(sem.qT_done, 1)
            for c in range(C):
                last = v.tensor_scalar(t.qT[:, c], ps[:, 1, c * NQ:(c + 1) * NQ], t.bq[:, c:c + 1], KEY_SCALE,
                                       ALU.add, ALU.mult)
            last.then_inc(sem.qT_kept, 1)
            dve.wait_ge(sem.wkT_done, 1)
            v.tensor_copy(wkT, ps[:, 2:4, 0:D]).then_inc(sem.wkT_kept, 1)
            dve.wait_ge(sem.qT_kept, 1)
            dve.wait_ge(sem.consts_built, 1)
            for c in range(C):
                last = v.tensor_tensor(t.qb[:, c], t.qT[:, c].unsqueeze(1).to_broadcast([P, HC, NQ]),
                                       keep.hmask[:, :, :], ALU.mult)
            last.then_inc(sem.qb_built, 1)
            def keep_lo(dst, hi, bank, h, hi_sem, n, out_sem):
                dve.wait_ge(hi_sem, n)
                half = slice(h * HS, (h + 1) * HS)
                v.tensor_tensor(dst[:, :, half], ps[:, bank:bank + 2, :], hi[:, :, half], ALU.subtract) \
                    .then_inc(out_sem, 1)

            def inputs_of_scan(i, m):
                e, half = m % 2, slice(m // 2 * HS, (m // 2 + 1) * HS)
                dve.wait_ge(sem.z_sig, 4 * i + m + 1)
                dve.wait_ge(sem.hh_done, 4 * i + (1, 3, 3, 4)[m])
                if m == 0 and after_first(i):
                    dve.wait_ge(sem.th_done, 2 * i)
                alone(dve, sem.dve_passed)
                v.scalar_tensor_tensor(both.hT[:, e, half], ps[:, BANK[m % 2] + 1, :], t.bh[:, e:e + 1], both.z[:, m % 2],
                                       ALU.add, ALU.mult).then_inc(sem.b_made, 1)

            def scan(i, m):
                e, h = m % 2, m // 2
                half = slice(h * HS, (h + 1) * HS)
                dve.wait_ge(sem.b_made, 4 * i + m + 1)
                dve.wait_ge(sem.a_sig, 4 * i + m + 1)
                if h:
                    dve.wait_ge(sem.h_scanned, 4 * i + m - 1)
                v.tensor_tensor_scan(both.hT[:, e, half], both.a[:, e, half], both.hT[:, e, half],
                                     both.hT[:, e, HS - 1:HS] if h else 0.0, ALU.mult, ALU.add) \
                    .then_inc(sem.h_scanned, 1)

            def largest(b, h):
                dve.wait_ge(sem.s_done, 2 * b + h + 1)
                if h == 0 and after_first(b):
                    dve.wait_ge(sem.mt_done, b)
                v.tensor_reduce(t.mx[:, h], ps[:, 4 + 2 * h:6 + 2 * h, :].rearrange("p k (j q) -> p q (k j)", q=HQ),
                                AX, ALU.max).then_inc(sem.s_max, 1)

            def stats_x1(i, o, tiles):
                dve.wait_ge(sem.x1_ready, 2 * i - 1 + tiles[-1] // HT)
                for j in tiles:
                    last = v.bn_stats(t.x1_st[:, j], both.x1[:, o, j])
                if tiles[-1] == T - 1:
                    last.then_inc(sem.x1_stats, 1)

            def guard_column(b):
                dve.wait_ge(sem.mt_done, b + 1)
                v.tensor_reduce(t.mcol[:, :], ps[:, 1, :].rearrange("p (c n) -> p c n", c=2), AX, ALU.max) \
                    .then_inc(sem.mt_red, 1)
                dve.wait_ge(sem.mt_red, b + 1)
                v.tensor_tensor(t.mcol2[:, :], t.mcol[:, :], t.ccol[:, :], ALU.add).then_inc(sem.mt_sum, 1)
                dve.wait_ge(sem.mt_sum, b + 1)
                v.tensor_tensor(t.mcolp[:, :, 0:64:32], t.ccol[:, :].unsqueeze(2).to_broadcast([P, 2, 2]),
                                t.mcol2[:, :].unsqueeze(2).to_broadcast([P, 2, 2]), ALU.subtract) \
                    .then_inc(sem.mt_kept, 1)

            def mean_x1(i, o):
                dve.wait_ge(sem.x1_stats, i)
                alone(dve, sem.dve_passed)
                for j in range(T):
                    last = v.bn_aggr(t.x1_mv[:, j], t.x1_st[:, j])
                last.then_inc(sem.x1_mv, 1)
                dve.wait_ge(sem.x1_mv, i)
                if live(i - 2) and after_first(i - 1):
                    dve.wait_ge(sem.n2_ready, 2 * i - 2)
                if live(i - 3):
                    dve.wait_ge(sem.st_stored, 16 * (i - 2))
                v.tensor_scalar(t.x1_v[:, :], t.x1_mv[:, :, 1], EPS, None, ALU.add)
                v.tensor_scalar(t.x1_n[:, o, 1], t.x1_mv[:, :, 0], -1.0, None, ALU.mult).then_inc(sem.x1_var, 1)

            def keep_ut(b):
                dve.wait_ge(sem.tu_done, b + 1)
                v.tensor_copy(keep.UT[:, :, :, bass.ds(b, 1)],
                              ps[:, 7, :].rearrange("p (c q o) -> p c q o", c=C, o=1)).then_inc(sem.ut_kept, 1)

            def sum_reciprocal(b, m, bank=4):
                dve.wait_ge(sem.u_done, 2 * b + m + 1)
                if after_first(b):
                    dve.wait_ge(sem.u_kept, 2 * b + m - 1)
                v.reciprocal(t.rcp[:, m:m + 1], ps[:, bank + m, D:D + 1]).then_inc(sem.u_rcp, 1)

            def stats_h(i, h):
                dve.wait_ge(sem.th_done, 2 * i + h + 1)
                for j in range(HT):
                    last = v.bn_stats(t.h_st[:, j], ps[:, BANK[h] + j // 2, (j % 2) * D:(j % 2 + 1) * D])
                last.then_inc(sem.th_stats, 1)

            def mean_h(i, h):
                n = 2 * i + h
                dve.wait_ge(sem.th_stats, n + 1)
                alone(dve, sem.dve_passed)
                for j in range(HT):
                    last = v.bn_aggr(t.h_mv[:, j], t.h_st[:, j])
                last.then_inc(sem.th_mv, 1)
                dve.wait_ge(sem.th_mv, n + 1)
                if after_first(i):
                    dve.wait_ge(sem.th_norm, n - 1)
                v.tensor_scalar(t.h_v[:, h, 0], t.h_mv[:, :, 1], EPS, None, ALU.add)
                v.tensor_scalar(t.h_v[:, h, 1], t.h_mv[:, :, 0], -1.0, None, ALU.mult).then_inc(sem.th_var, 1)

            def body(i, s, k):
                o = 1 - s
                first = isinstance(i, int) and i == 0
                if first:
                    stats_x(i + 1, o, k + s + 1)
                if live(i):
                    keep_lo(t.nT_lo, t.nT_hi, BANK[0], 0, sem.tn_hi, 2 * i + 1, sem.tn_lo)
                if live(i - 2):
                    largest(i - 2, 1)
                if live(i):
                    keep_lo(t.nT_lo, t.nT_hi, BANK[1], 1, sem.tn_hi, 2 * i + 2, sem.tn_lo)
                if first:
                    dve.wait_ge(sem.mk_done, 1)
                    v.tensor_copy(t.ccol[:, :], ps[:, 5, 0:2])
                    dve.wait_ge(sem.mk_hi, 1)
                    v.tensor_tensor(t.mk_lo[:, :, :], ps[:, 4, :].rearrange("p (c q) -> p c q", c=C), t.mk_hi[:, :, :],
                                    ALU.subtract).then_inc(sem.mk_kept, 1)
                    dve.wait_ge(sem.mk_kept, 1)
                if live(i - 1):
                    stats_x1(i, o, range(2))
                if live(i - 2):
                    guard_column(i - 2)
                if live(i):
                    inputs_of_scan(i, 0)
                if live(i - 1):
                    stats_x1(i, o, range(2, 6))
                if live(i - 2):
                    guard_row(i - 2)
                if live(i - 1):
                    stats_x1(i, o, range(6, T))
                    mean_x1(i, o)
                if live(i):
                    scan(i, 0)
                    inputs_of_scan(i, 1)
                if live(i):
                    scan(i, 1)
                    inputs_of_scan(i, 2)
                    scan(i, 2)
                if live(i + 1) and not first:
                    stats_x(i + 1, o, k + s + 1)
                if live(i - 2):
                    sum_reciprocal(i - 2, 0)
                if live(i):
                    inputs_of_scan(i, 3)
                    scan(i, 3)
                if live(i):
                    stats_h(i, 0)
                if live(i - 1):
                    keep_lo(t.n2T_lo, t.n2T_hi, 6, 0, sem.t2_hi, 2 * i - 1, sem.t2_lo)
                if live(i):
                    mean_h(i, 0)
                if live(i - 2):
                    sum_reciprocal(i - 2, 1)
                if live(i):
                    stats_h(i, 1)
                    mean_h(i, 1)
                if live(i - 1):
                    keep_lo(t.n2T_lo, t.n2T_hi, 6, 1, sem.t2_hi, 2 * i, sem.t2_lo)
                if live(i - 1):
                    largest(i - 1, 0)
                if live(i - 2):
                    keep_ut(i - 2)

            def guard_row(b):
                dve.wait_ge(sem.mr_done, b + 1)
                if after_first(b):
                    dve.wait_ge(sem.ga_done, b)
                v.tensor_copy(t.grow_t[32:64, :], ps[32:64, 1, 0:D]).then_inc(sem.mr_hi, 1)
                v.tensor_copy(t.grow[0:32, :], ps[0:32, 1, 0:D])
                dve.wait_ge(sem.mr_hi, b + 1)
                v.tensor_tensor(t.grow[32:64, :], ps[32:64, 1, 0:D], t.grow_t[32:64, :], ALU.subtract) \
                    .then_inc(sem.mr_kept, 1)

            def closing(b, last):
                largest(b, 1)
                stats_x1(last + 1, last % 2, range(HT))
                guard_column(b)
                stats_x1(last + 1, last % 2, range(HT, T))
                guard_row(b)
                mean_x1(last + 1, last % 2)
                keep_lo(t.n2T_lo, t.n2T_hi, 0, 0, sem.t2_hi, 2 * last + 1, sem.t2_lo)
                keep_lo(t.n2T_lo, t.n2T_hi, 6, 1, sem.t2_hi, 2 * last + 2, sem.t2_lo)
                sum_reciprocal(b, 0, bank=2)
                largest(last, 0)
                largest(last, 1)
                guard_column(last)
                sum_reciprocal(b, 1, bank=2)
                guard_row(last)
                keep_ut(b)
                sum_reciprocal(last, 0)
                sum_reciprocal(last, 1)
                keep_ut(last)

            rows(dve, body, closing)

        @block.tensor
        def _(pe):
            mm, tr = nc.tensor.matmul, nc.tensor.transpose
            pe.wait_ge(sem.w_loaded, 16 * 9)
            pe.wait_ge(sem.ident_built, 4)
            for c in range(C):
                last = tr(ps[:, 0, c * NQ:(c + 1) * NQ], sq[:, c * P:(c + 1) * P], keep.ident[0:NQ, 0:NQ])
            last.then_inc(sem.sqT_done, 1)
            for f in range(C):
                for c in range(C):
                    last = tr(ps[:, 2 + f, c * P:(c + 1) * P], wk[:, c, f * P:(f + 1) * P], keep.ident[:, :])
            last.then_inc(sem.wkT_done, 1)
            pe.wait_ge(sem.sqT_kept, 1)
            for f in range(C):
                for c in range(C):
                    last = mm(ps[:, 1, f * NQ:(f + 1) * NQ], wq[:, c, f * P:(f + 1) * P], t.sqT[:, c],
                              start=(c == 0), stop=(c == C - 1))
            last.then_inc(sem.qT_done, 1)
            pe.wait_ge(sem.split_w, 4)
            pe.wait_ge(sem.qT_kept, 1)
            pe.wait_ge(sem.wkT_kept, 1)

            def folded_queries():
                pe.wait_ge(sem.qb_built, 1)
                for f in range(C):
                    qb = t.qb[:, f].rearrange("p h q -> p (h q)")
                    for c in range(C):
                        mm(ps[:, 4, c * HQ + f * P:c * HQ + (f + 1) * P], wkT[:, f, c * P:(c + 1) * P], qb,
                           start=True, stop=True)
                    last = mm(ps[:, 5, f:f + 1], qb, t.bk[:, f:f + 1], start=True, stop=True)
                last.then_inc(sem.mk_done, 1)

            def transposed(src, bank, h):
                for j in range(HT):
                    for c in range(C):
                        last = tr(ps[:, bank + c, j * P:(j + 1) * P], src[:, h * HT + j, c * P:(c + 1) * P],
                                  keep.ident[:, :])
                return last

            def projection(m, bank, w_hi, w_lo):
                e, half = m % 2, slice(m // 2 * HS, (m // 2 + 1) * HS)
                for c in range(C):
                    last = three_passes(nc, ps[:, bank, :], w_hi[:, c, e * P:(e + 1) * P], w_lo[:, c, e * P:(e + 1) * P],
                                        t.nT_hi[:, c, half], t.nT_lo[:, c, half], c == 0, c == C - 1)
                return last

            def z_pre(m):
                projection(m, BANK[m % 2], t.wz_hi, t.wz_lo).then_inc(sem.z_done, 1)

            def h_tilde(m):
                projection(m, BANK[m % 2] + 1, t.wh_hi, t.wh_lo).then_inc(sem.hh_done, 1)

            def tokens_of_h(h):
                for j in range(HT):
                    for c in range(C):
                        at = (j % 2) * D + c * P
                        last = tr(ps[:, BANK[h] + j // 2, at:at + P],
                                  both.hT[:, c, (h * HT + j) * P:(h * HT + j + 1) * P], keep.ident[:, :])
                last.then_inc(sem.th_done, 1)

            def scores(tiles):
                for j in tiles:
                    for c in range(C):
                        last = three_passes(nc, s_tile[:, j], t.n2T_hi[:, c, j * P:(j + 1) * P],
                                            t.n2T_lo[:, c, j * P:(j + 1) * P], t.mk_hi[:, c], t.mk_lo[:, c],
                                            j % 2 == 0 and c == 0, c == C - 1, skip=True)
                return last

            def largest_transposed(b):
                pe.wait_ge(sem.s_max, 2 * b + 2)
                for c in range(2):
                    for h in range(2):
                        last = tr(ps[:, 1, (2 * c + h) * P:(2 * c + h + 1) * P], t.mx[:, h, c * P:(c + 1) * P],
                                  keep.ident[:, :])
                last.then_inc(sem.mt_done, 1)

            def guard_transposed(b):
                pe.wait_ge(sem.mt_kept, b + 1)
                for c in range(2):
                    last = mm(ps[0:64, 1, c * P:(c + 1) * P], t.mcolp[:, c], keep.ident[:, :], start=True, stop=True)
                last.then_inc(sem.mr_done, 1)

            def add_guard(b):
                pe.wait_ge(sem.mr_kept, b + 1)
                for k in range(4):
                    last = mm(ps[:, 4 + k, :], keep.selrow[:, :], t.grow[:, :].unsqueeze(1).to_broadcast([P, 2, HQ]),
                              start=False, stop=True, skip_group_check=True)
                last.then_inc(sem.ga_done, 1)

            def sums_transposed():
                for c in range(C):
                    for m in range(2):
                        last = tr(ps[:, 7, c * HQ + m * P:c * HQ + (m + 1) * P], t.u[:, m, c * P:(c + 1) * P],
                                  keep.ident[:, :])
                last.then_inc(sem.tu_done, 1)

            def weighted_sums(s, m, tiles=range(T), bank=4):
                for j in tiles:
                    last = mm(ps[:, bank + m, 0:D + 1], keep.pT[:, j, m * P:(m + 1) * P], t.n2[:, s, j, 0:D + 1],
                              start=(j == 0), stop=(j == T - 1))
                return last

            def body(i, s, k):
                o = 1 - s
                if live(i):
                    pe.wait_ge(sem.n_ready, 2 * i + 1)
                    if after_first(i):
                        pe.wait_ge(sem.y_ready, 2 * i - 1)
                    transposed(both.n, BANK[0], 0).then_inc(sem.tn_done, 1)
                if live(i - 2):
                    scores([5])
                    if live(i - 3):
                        pe.wait_ge(sem.ut_kept, i - 2)
                    scores([6])
                if live(i):
                    pe.wait_ge(sem.n_ready, 2 * i + 2)
                    if after_first(i):
                        pe.wait_ge(sem.y_ready, 2 * i)
                    transposed(both.n, BANK[1], 1).then_inc(sem.tn_done, 1)
                if live(i - 2):
                    scores([7]).then_inc(sem.s_done, 1)
                if isinstance(i, int) and i == 0:
                    folded_queries()
                if live(i):
                    pe.wait_ge(sem.tn_lo, 2 * i + 1)
                    z_pre(0)
                    h_tilde(0)
                    pe.wait_ge(sem.tn_lo, 2 * i + 2)
                elif live(i - 1):
                    pe.wait_ge(sem.y_ready, 2 * i)
                if live(i - 2):
                    largest_transposed(i - 2)
                if live(i):
                    z_pre(1)
                if live(i - 2):
                    guard_transposed(i - 2)
                if live(i):
                    pe.wait_ge(sem.a_sig, 4 * i + 1)
                    z_pre(2)
                    pe.wait_ge(sem.b_made, 4 * i + 1)
                    h_tilde(2)
                if live(i - 2):
                    add_guard(i - 2)
                if live(i):
                    h_tilde(1)
                    pe.wait_ge(sem.a_sig, 4 * i + 2)
                    z_pre(3)
                    pe.wait_ge(sem.b_made, 4 * i + 2)
                    h_tilde(3)
                if live(i - 2):
                    pe.wait_ge(sem.p_ready, i - 1)
                    weighted_sums(s, 0).then_inc(sem.u_done, 1)
                if live(i):
                    pe.wait_ge(sem.h_scanned, 4 * i + 2)
                    pe.wait_ge(sem.b_made, 4 * i + 3)
                    pe.wait_ge(sem.a_sig, 4 * i + 3)
                    tokens_of_h(0)
                if live(i - 1):
                    pe.wait_ge(sem.n2_ready, 2 * i - 1)
                    transposed(t.n2[:, o], 6, 0).then_inc(sem.t2_done, 1)
                if live(i - 2):
                    weighted_sums(s, 1, range(HT))
                if live(i):
                    pe.wait_ge(sem.h_scanned, 4 * i + 4)
                    tokens_of_h(1)
                if live(i - 2):
                    weighted_sums(s, 1, range(HT, T)).then_inc(sem.u_done, 1)
                if live(i - 1):
                    pe.wait_ge(sem.n2_ready, 2 * i)
                    pe.wait_ge(sem.t2_lo, 2 * i - 1)
                    transposed(t.n2[:, o], 6, 1).then_inc(sem.t2_done, 1)
                if live(i - 2):
                    pe.wait_ge(sem.u_kept, 2 * i - 3)
                if live(i - 1):
                    if live(i) and not live(i - 2):
                        pe.wait_ge(sem.mk_kept, 1)
                    scores([0, 1])
                if live(i - 2):
                    pe.wait_ge(sem.u_kept, 2 * i - 2)
                if live(i - 1):
                    scores([2])
                    scores([3]).then_inc(sem.s_done, 1)
                    pe.wait_ge(sem.t2_lo, 2 * i)
                if live(i - 2):
                    sums_transposed()
                if live(i - 1):
                    scores([4])

            def closing(b, last):
                scores([5])
                pe.wait_ge(sem.ut_kept, b)
                scores([6, 7]).then_inc(sem.s_done, 1)
                pe.wait_ge(sem.y_ready, 2 * last + 2)
                largest_transposed(b)
                guard_transposed(b)
                add_guard(b)
                pe.wait_ge(sem.n2_ready, 2 * last + 1)
                transposed(t.n2[:, last % 2], 0, 0).then_inc(sem.t2_done, 1)
                pe.wait_ge(sem.p_ready, b + 1)
                weighted_sums(b % 2, 0, range(HT), bank=2)
                pe.wait_ge(sem.n2_ready, 2 * last + 2)
                transposed(t.n2[:, last % 2], 6, 1).then_inc(sem.t2_done, 1)
                weighted_sums(b % 2, 0, range(HT, T), bank=2).then_inc(sem.u_done, 1)
                pe.wait_ge(sem.t2_lo, 2 * last + 1)
                scores([0, 1, 2, 3]).then_inc(sem.s_done, 1)
                pe.wait_ge(sem.t2_lo, 2 * last + 2)
                scores([4, 5, 6, 7]).then_inc(sem.s_done, 1)
                weighted_sums(b % 2, 1, bank=2).then_inc(sem.u_done, 1)
                largest_transposed(last)
                guard_transposed(last)
                add_guard(last)
                pe.wait_ge(sem.p_ready, last + 1)
                pe.wait_ge(sem.u_kept, 2 * b + 2)
                sums_transposed()
                weighted_sums(last % 2, 0).then_inc(sem.u_done, 1)
                weighted_sums(last % 2, 1).then_inc(sem.u_done, 1)
                pe.wait_ge(sem.u_kept, 2 * last + 2)
                pe.wait_ge(sem.ut_kept, last)
                sums_transposed()

            rows(pe, body, closing)


def expert_phase(nc, ctx, sem, ps, keep, both, ring, slot_query, d_Wo, d_bv, d_bo,
                 e_ln_g, e_ln_b, e_W1, e_b1, e_Wg, e_bg, e_W2, e_b2,
                 c_Wq, c_Wk, c_Wv, c_Wo, c_bq, c_bk, c_bv, c_bo, x1_dram, st_dram):
    TT = NQ * B // P
    QT = NQ // TT
    GH = 4
    NG = H // GH
    t = tensors(nc, ctx, "expert", [
        ("wop", [P, NG, D], F32), ("bvp", [P, NG], F32),
        ("ao", [P, NG, NQ * B], F32),
        ("sqb", [64, D], F32),
        ("ln_g", [NQ, D], F32), ("ln_b", [NQ, D], F32),
        ("spread", [64, NQ, B], F32),
        ("o", [P, TT, D], F32),
        ("o_st", [P, TT, 6], F32), ("o_mv", [P, TT, 2], F32), ("o_v", [P, 2, TT], F32), ("o_r", [P, TT], F32),
        ("oT", [P, C, NQ * B], F32),
        ("b1", [P, F], F32), ("bg", [P, F], F32), ("eb2", [E, D], F32), ("b2T", [P, C, E], F32),
        ("xe", [P, 2, C, 32], F32), ("sel", [P, 2, 32], F32),
        ("sg", [P, 2, 512], F32), ("hg", [P, 2, D], F32), ("hgT", [P, 2, D], F32), ("ye", [P, 2, D], F32),
        ("ysum", [P, 2, C, B], F32),
        ("w2_3", [P, FK, D], F32),
        ("w1_4", [P, C, F], F32), ("wg_4", [P, C, F], F32), ("w2_4", [P, FK, D], F32),
    ])
    wv = wv_place(both)
    oln = both.z[:, 1, :].rearrange("p (m d) -> p m d", d=D)
    hT = t.ao[:, 0:C]
    ut = keep.UT[:, :, :, :].rearrange("p c q b -> p (c q b)")
    ring = ring[:3] + [ring[3][:2] + [t.w2_3[:, :, :]], [t.w1_4[:, :, :], t.wg_4[:, :, :], t.w2_4[:, :, :]],
                       [ut[:, 0:C * F].rearrange("p (c f) -> p c f", f=F),
                        ut[:, C * F:2 * C * F].rearrange("p (c f) -> p c f", f=F),
                        ut[:, 2 * C * F:2 * C * F + FK * D].rearrange("p (k d) -> p k d", d=D)]]
    w1, wg, w2 = [[slot[n] for slot in ring] for n in range(3)]
    arrived = [sem.ew0, sem.ew1, sem.ew2, sem.ew3, sem.ew4, sem.ew5]

    def pairs(e_, body):
        for e in range(2):
            body(e, e)
        with e_.Fori(1, E // 2 - 1) as r:
            for q in range(2):
                body(2 * r + q, q)
        for e in range(E - 2, E):
            body(e, e % 2)

    def experts(e_, body):
        for e in range(SLOTS + 3):
            body(e, e % (SLOTS + 2), e // (SLOTS + 2), e % 2, (e - 1) % (SLOTS + 2))
        with e_.Fori(1, E // SLOTS - 1) as r:
            for k in range(SLOTS):
                body(SLOTS * r + 3 + k, (1 + k) % SLOTS, r + (k + 1) // SLOTS, (1 + k) % 2, k)
        body(E - 1, 1, E // SLOTS - 1, (E - 1) % 2, 0)

    def is_int(e):
        return isinstance(e, int)

    with nc.Block() as block:

        @block.sync
        def _(sp):
            load_expert(sp, sem, ring, 3, 3, e_W1, e_Wg, e_W2, parts=(2,))
            sp.wait_ge(sem.pads_zero, 1)
            lanes = [slice(32 * j, 32 * j + DH) for j in range(GH)]
            for j in range(GH):
                sp.dma_start(t.bvp[lanes[j], :], d_bv.rearrange("(g j k) -> j k g", j=GH, k=DH)[j],
                             allow_slow_non_contiguous=True).then_inc(sem.slot_bv, 16)
            for j in range(GH):
                sp.dma_start(t.wop[lanes[j], :, :], d_Wo.rearrange("(g j k) n -> j k g n", j=GH, k=DH)[j]) \
                    .then_inc(sem.slot_small, 16)
            sp.dma_start(t.sqb[0:NQ, :], slot_query[0]).then_inc(sem.slot_small, 16)
            sp.dma_start(t.sqb[32:33, :], d_bo.unsqueeze(0)).then_inc(sem.slot_small, 16)
            sp.dma_start(t.ln_g[:, :], e_ln_g).then_inc(sem.slot_bias, 16)
            sp.dma_start(t.ln_b[:, :], e_ln_b).then_inc(sem.slot_bias, 16)
            sp.wait_ge(sem.pads_zero, 2)
            for dst, src in ((t.b1, e_b1), (t.bg, e_bg), (t.eb2, e_b2)):
                sp.dma_start(dst[0:E, :], src).then_inc(sem.slot_bias, 16)

            load_expert(sp, sem, ring, SLOTS, SLOTS, e_W1, e_Wg, e_W2)
            sp.wait_ge(sem.ao_done, 1)
            load_expert(sp, sem, ring, SLOTS + 1, SLOTS + 1, e_W1, e_Wg, e_W2)
            for e in range(SLOTS + 2, E):
                before = e - SLOTS if e >= 2 * SLOTS + 2 else e - SLOTS - 2
                sp.wait_ge(sem.y_done, before + 1)
                load_expert(sp, sem, ring, (e - 2) % SLOTS, e, e_W1, e_Wg, e_W2)
            for n, w in enumerate((c_Wk, c_Wv, c_Wq, c_Wo)):
                sp.dma_start(keep.pT[:, n * C:(n + 1) * C, :], w.rearrange("(c p) n -> p c n", p=P)) \
                    .then_inc(sem.c_w, 16)
            for n, w in enumerate((c_bq, c_bk, c_bv)):
                sp.dma_start(keep.cb[:, n], w.rearrange("(c p) -> p c", p=P), allow_slow_non_contiguous=True) \
                    .then_inc(sem.c_w, 16)
            sp.dma_start(keep.bo_rep[:, :], c_bo.unsqueeze(0).to_broadcast([P, D])).then_inc(sem.c_w, 16)
            for b in range(2):
                load_row(sp, sem, keep, x1_dram, st_dram, b, b)

        @block.gpsimd
        def _(pool):
            g = nc.gpsimd
            g.memset(t.wop[:, :, :], 0.0)
            g.memset(t.sqb[:, :], 0.0)
            g.memset(t.bvp[:, :], 0.0).then_inc(sem.pads_zero, 1)
            g.memset(t.b1[:, :], 0.0)
            g.memset(t.bg[:, :], 0.0).then_inc(sem.pads_zero, 1)
            g.memset(t.xe[:, :, :, :], 0.0)
            g.memset(t.sel[:, :, :], 0.0).then_inc(sem.pads_zero, 1)
            pool.wait_ge(sem.o_var, 1)
            g.tensor_tensor(t.o_r[:, :], t.o_v[:, 0], keep.mhalf[:, 0:TT], ALU.pow).then_inc(sem.o_pow, 1)

        @block.vector
        def _(dve):
            v = nc.vector
            v.memset(ps[:, 0:2, :], 0.0).then_inc(sem.banks_zero, 1)
            v.memset(t.spread[:, :, :], 0.0).then_inc(sem.spread_made, 1)
            dve.wait_ge(sem.spread_made, 1)
            v.memset(t.spread[32:33, :, :], 1.0).then_inc(sem.spread_made, 1)
            v.tensor_copy(t.spread[0:NQ, :, :], keep.ident[0:NQ, 0:NQ].unsqueeze(2).to_broadcast([NQ, NQ, B])) \
                .then_inc(sem.spread_made, 1)
            dve.wait_ge(sem.slot_bv, 16 * GH)
            dve.wait_ge(sem.ao_done, 1)
            for g in range(NG):
                last = v.tensor_scalar(t.ao[:, g], ps[:, g // 2, (g % 2) * D:(g % 2 + 1) * D], t.bvp[:, g:g + 1],
                                       None, ALU.add)
            last.then_inc(sem.ao_kept, 1)
            dve.wait_ge(sem.o_done, 1)
            for m in range(TT):
                last = v.bn_stats(t.o_st[:, m], ps[:, 4 + m, 0:D])
            last.then_inc(sem.o_stats, 1)
            dve.wait_ge(sem.o_stats, 1)
            alone(dve, sem.dve_passed)
            for m in range(TT):
                last = v.bn_aggr(t.o_mv[:, m], t.o_st[:, m])
            last.then_inc(sem.o_mv, 1)
            dve.wait_ge(sem.o_mv, 1)
            v.tensor_scalar(t.o_v[:, 0], t.o_mv[:, :, 1], EPS, None, ALU.add)
            v.tensor_scalar(t.o_v[:, 1], t.o_mv[:, :, 0], -1.0, None, ALU.mult).then_inc(sem.o_var, 1)
            dve.wait_ge(sem.o_pow, 1)
            dve.wait_ge(sem.o_var, 1)
            for m in range(TT):
                last = v.tensor_scalar(oln[:, m], ps[:, 4 + m, 0:D], t.o_v[:, 1, m:m + 1], t.o_r[:, m:m + 1],
                                       ALU.add, ALU.mult)
            last.then_inc(sem.o_centred, 1)
            dve.wait_ge(sem.b2t_done, 1)
            v.tensor_copy(t.b2T[:, :, :], ps[:, 6, 0:C * E].rearrange("p (c e) -> p c e", c=C)).then_inc(sem.b2t_kept, 1)
            dve.wait_ge(sem.ln_spread, 1)
            dve.wait_ge(sem.o_centred, 1)
            v.tensor_tensor(oln[:, :, :], oln[:, :, :], ps[:, 2, :].rearrange("p (m d) -> p m d", d=D), ALU.mult).then_inc(sem.o_scaled, 1)
            dve.wait_ge(sem.o_scaled, 1)
            v.tensor_tensor(oln[:, :, :], oln[:, :, :], ps[:, 3, :].rearrange("p (m d) -> p m d", d=D), ALU.add).then_inc(sem.o_ln, 1)
            dve.wait_ge(sem.ot_done, 1)
            dve.wait_ge(sem.pads_zero, 3)
            lnT = ps[:, 0, :].rearrange("p (c n) -> p c n", c=C)
            v.tensor_copy(t.xe[:, 0, :, 0:B], lnT[:, :, 0:B])
            v.tensor_copy(t.sel[0:E, 0, 0:B], keep.ident[0:E, 0:1].to_broadcast([E, B])).then_inc(sem.xe_made, 1)
            v.tensor_copy(hT[:, :, :], lnT).then_inc(sem.ot_kept, 1)
            dve.wait_ge(sem.ot_kept, 1)

            def prepare(e, q):
                v.tensor_copy(t.xe[:, q, :, 0:B], hT[:, :, bass.ds(e * B, B)])
                v.tensor_copy(t.sel[0:E, q, 0:B], keep.ident[0:E, bass.ds(e, 1)].to_broadcast([E, B])) \
                    .then_inc(sem.xe_made, 1)

            def result(e, q):
                dve.wait_ge(sem.yt_done, e + 1)
                parts = ps[:, 6 + q, 0:C * P].rearrange("p (c j n) -> p c n j", c=C, j=4)[:, :, 0:B, :]
                v.tensor_reduce(t.ysum[:, q], parts, AX, ALU.add).then_inc(sem.y_summed, 1)
                dve.wait_ge(sem.y_summed, e + 1)
                v.tensor_tensor(keep.o2T[:, :, bass.ds(e * B, B)], t.oT[:, :, bass.ds(e * B, B)], t.ysum[:, q],
                                ALU.add).then_inc(sem.o2_made, 1)

            def body(e, q):
                fresh = is_int(e) and e < 2
                dve.wait_ge(sem.ug_silu, e + 1)
                v.tensor_tensor(t.hg[:, q], t.sg[:, q, 0:D], t.sg[:, q, D:2 * D], ALU.mult).then_inc(sem.hg_made, 1)
                if not (is_int(e) and e == 0):
                    result(e - 1, 1 - q)
                dve.wait_ge(sem.hgt_done, e + 1)
                if not fresh:
                    dve.wait_ge(sem.y_done, e - 1)
                v.tensor_copy(t.hgT[:, q], ps[:, 2 + q, 0:D]).then_inc(sem.hgt_kept, 1)
                if not (is_int(e) and e >= E - 2):
                    dve.wait_ge(sem.ug_done, e + 1)
                    prepare(e + 2, q)
                dve.wait_ge(sem.y_done, e + 1)
                if not fresh:
                    dve.wait_ge(sem.yt_done, e - 1)
                v.tensor_copy(t.ye[:, q], ps[:, 4 + q, 0:D]).then_inc(sem.y_kept, 1)

            prepare(1, 1)
            dve.wait_ge(sem.ot_done, 2)
            dve.wait_ge(sem.b2t_kept, 1)
            for c in range(C):
                last = v.tensor_tensor(t.oT[:, c].rearrange("p (q b) -> p q b", b=B),
                                       ps[:, 7, c * NQ * B:(c + 1) * NQ * B].rearrange("p (q b) -> p q b", b=B),
                                       t.b2T[:, c].unsqueeze(2).to_broadcast([P, NQ, B]), ALU.add)
            last.then_inc(sem.ot_kept, 1)
            dve.wait_ge(sem.ot_kept, 2)
            pairs(dve, body)
            result(E - 1, (E - 1) % 2)

        @block.scalar
        def _(act):
            a = nc.scalar

            def body(e, q):
                act.wait_ge(sem.ug_done, e + 1)
                if not (is_int(e) and e < 2):
                    act.wait_ge(sem.hg_made, e - 1)
                a.activation(t.sg[:, q], ps[:, q, :], ACT.Silu).then_inc(sem.ug_silu, 1)

            act.wait_ge(sem.o_centred, 1)
            a.activation(t.o[:, :, :], ps[:, 4:4 + TT, 0:D], ACT.Copy).then_inc(sem.o_kept, 1)
            pairs(act, body)

        @block.tensor
        def _(pe):
            mm, tr = nc.tensor.matmul, nc.tensor.transpose
            pe.wait_ge(sem.slot_w, 16)
            pe.wait_ge(sem.banks_zero, 1)
            for g in range(NG):
                for c in range(C):
                    for j in range(GH):
                        h = GH * g + j
                        last = mm(ps[32 * j:32 * j + DH, g // 2, (g % 2) * D:(g % 2 + 1) * D],
                                  wv[:, c, h * DH:(h + 1) * DH],
                                  keep.UT[:, c, h * NQ:(h + 1) * NQ, :].rearrange("p q b -> p (q b)"),
                                  start=(c == 0), stop=(c == C - 1), skip_group_check=True)
            last.then_inc(sem.ao_done, 1)
            pe.wait_ge(sem.spread_made, 3)
            spread = [t.spread[:, m * QT:(m + 1) * QT, :].rearrange("q s b -> q (s b)") for m in range(TT)]
            pe.wait_ge(sem.ao_kept, 1)
            pe.wait_ge(sem.slot_small, 16 * 6)
            for m in range(TT):
                for g in range(NG):
                    mm(ps[:, 4 + m, 0:D], t.ao[:, g, m * P:(m + 1) * P], t.wop[:, g], start=(g == 0), stop=False)
                last = mm(ps[:, 4 + m, 0:D], spread[m], t.sqb[:, :], start=False, stop=True)
            last.then_inc(sem.o_done, 1)
            pe.wait_ge(sem.slot_bias, 16 * 5)
            for c in range(C):
                last = tr(ps[:, 6, c * E:(c + 1) * E], t.eb2[:, c * P:(c + 1) * P], keep.ident[0:E, 0:E])
            last.then_inc(sem.b2t_done, 1)
            for m in range(TT):
                for bank, rows in ((2, t.ln_g), (3, t.ln_b)):
                    last = mm(ps[:, bank, m * D:(m + 1) * D], spread[m][0:NQ], rows[:, :], start=True, stop=True)
            last.then_inc(sem.ln_spread, 1)
            for n, (src, bank) in enumerate(((oln, 0), (t.o, 7))):
                pe.wait_ge((sem.o_ln, sem.o_kept)[n], 1)
                for m in range(TT):
                    for c in range(C):
                        last = tr(ps[:, bank, c * NQ * B + m * P:c * NQ * B + (m + 1) * P],
                                  src[:, m, c * P:(c + 1) * P], keep.ident[:, :])
                last.then_inc(sem.ot_done, 1)

            def up(e, k, turn, q):
                pe.wait_ge(sem.xe_made, e + 1)
                final = is_int(e) and e == E - 1
                if not final:
                    pe.wait_ge(arrived[k], 48 * (turn + 1))
                if is_int(e) and e == 0:
                    pe.wait_ge(sem.ot_kept, 1)
                    pe.wait_ge(sem.o_kept, 1)
                if not (is_int(e) and e < 2):
                    pe.wait_ge(sem.ug_silu, e - 1)
                for n, (w, bias) in enumerate(((w1[k], t.b1), (wg[k], t.bg))):
                    if final:
                        pe.wait_ge((sem.last_w1, sem.last_wg)[n], 16)
                    for c in range(C + 1):
                        for j in range(4):
                            cols = slice(j * D, (j + 1) * D)
                            lhs = t.xe[:, q, c] if c < C else t.sel[:, q]
                            rhs = w[:, c, cols] if c < C else bias[:, cols]
                            last = mm(ps[32 * j:32 * j + 32, q, n * D:(n + 1) * D], lhs, rhs,
                                      start=(c == 0), stop=(c == C), skip_group_check=True)
                last.then_inc(sem.ug_done, 1)

            def down(e, k, q):
                fresh = is_int(e) and e < 2
                pe.wait_ge(sem.hg_made, e + 1)
                if not fresh:
                    pe.wait_ge(sem.hgt_kept, e - 1)
                for n in range(2):
                    last = tr(ps[:, 2 + q, n * P:(n + 1) * P], t.hg[:, q, n * P:(n + 1) * P], keep.ident[:, :])
                last.then_inc(sem.hgt_done, 1)
                pe.wait_ge(sem.hgt_kept, e + 1)
                if not fresh:
                    pe.wait_ge(sem.y_kept, e - 1)
                if is_int(e) and e == E - 1:
                    pe.wait_ge(sem.last_w2, 16)
                for n in range(2):
                    for j in range(4):
                        last = mm(ps[32 * j:32 * j + 32, 4 + q, 0:D], t.hgT[:, q, n * P + 32 * j:n * P + 32 * j + 32],
                                  w2[k][:, 2 * j + n], start=(n == 0), stop=(n == 1), skip_group_check=True)
                last.then_inc(sem.y_done, 1)

            def down_transposed(e, q):
                pe.wait_ge(sem.y_kept, e + 1)
                if is_int(e) and e < 2:
                    pe.wait_ge(sem.ot_kept, 2)
                else:
                    pe.wait_ge(sem.o2_made, e - 1)
                for c in range(C):
                    last = tr(ps[:, 6 + q, c * P:(c + 1) * P], t.ye[:, q, c * P:(c + 1) * P], keep.ident[:, :])
                last.then_inc(sem.yt_done, 1)

            def body(e, k, turn, q, before):
                up(e, k, turn, q)
                if not (is_int(e) and e < 2):
                    down_transposed(e - 2, q)
                if is_int(e) and e == 0:
                    down(0, 0, 0)
                elif not (is_int(e) and e == 1):
                    down(e - 1, before, 1 - q)

            experts(pe, body)
            down_transposed(E - 2, E % 2)
            down(E - 1, 1, (E - 1) % 2)
            down_transposed(E - 1, (E - 1) % 2)


def combine_phase(nc, ctx, sem, ps, keep, x1_dram, st_dram, out):
    GA, GB, GC, GD = 0, 2, 4, 6
    TOK = NQ * B
    t = tensors(nc, ctx, "combine", [
        ("khT", [P, C, TOK], F32), ("vhT", [P, C, TOK], F32), ("wqT", [P, C, D], F32),
        ("bqp", [P, C, 64], F32),
        ("kb", [P, C, HC, NQ], F32), ("vb", [P, C, HC, NQ], F32),
        ("m_hi", [P, C, HQ], F32R), ("m_lo", [P, C, HQ], F32R),
        ("nv", [P, ROWS, C, D], F32),
        ("crow", [P, HQ], F32R), ("crow_t", [64, HQ], F32R),
        ("n2", [P, T, D], F32), ("n2T_hi", [P, C, S], F32R), ("n2T_lo", [P, C, S], F32R),
        ("p", [P, 2, T * H, NQ], F32),
        ("mx", [P, 2, HT * H], F32), ("sm", [P, 2, HT * H], F32), ("rc", [P, 2, HT * H], F32),
        ("pT", [P, C, S], F32),
        ("o_st", [P, HT, 6], F32), ("o_mv", [P, HT, 2], F32), ("o_v", [P, 2, 2, HT], F32), ("o_r", [P, 2, 2, HT], F32),
        ("y", [P, 2, T, D], F32),
    ])
    xc = combine_rows(keep)
    wk, wv, wq, wo = [keep.pT[:, n * C:(n + 1) * C, :] for n in range(4)]
    bq, bk, bv = [keep.cb[:, n] for n in range(3)]
    rows_loaded = (sem.c_rows0, sem.c_rows1, sem.c_rows2, sem.c_rows3)

    def rows(e, body):
        for i in range(-1, 4):
            body(i, i % ROWS, i // ROWS)
        with e.Fori(1, B // ROWS - 1) as k:
            for s in range(ROWS):
                body(ROWS * k + s, s, k)
        for i in range(B - ROWS, B + 2):
            body(i, i % ROWS, i // ROWS)

    def last_two(b):
        return isinstance(b, int) and b >= B - 2 and b < B

    def out_banks(b, h):
        return (GA, GB)[h] if last_row(b) else (GC, GD)[h]

    def probability_banks(b, h):
        return (GA, GB)[h] if last_row(b) else GC

    with nc.Block() as block:

        @block.sync
        def _(sp):
            def body(i, s, k):
                if last_two(i - 2):
                    for h in range(2):
                        sp.wait_ge(sem.last_added, 2 * (i - B) + h + 1)
                        if i == B and h == 0:
                            sp.wait_ge(sem.oc_stored, 16 * (B - 2))
                        half = slice(h * HT, (h + 1) * HT)
                        sp.dma_start(out[i - 2].rearrange("(j p) d -> p j d", p=P)[:, half],
                                     t.y[:, i % 2, half]).then_inc(sem.oc_stored, 16)
                elif live(i - 2):
                    sp.wait_ge(sem.oc_added, 2 * i - 2)
                    alone(sp, sem.sp_passed)
                if live(i + 2) and not (isinstance(i, int) and i < 0):
                    load_row(sp, sem, keep, x1_dram, st_dram, i + 2, (s + 2) % ROWS)
                if live(i - 2) and not last_two(i - 2):
                    if after_first(i - 2):
                        sp.wait_ge(sem.oc_stored, 16 * (i - 2))
                    alone(sp, sem.sp_passed)
                    sp.dma_start(out[bass.ds(i - 2, 1)].rearrange("o (j p) d -> p (o j) d", p=P),
                                 t.y[:, s % 2]).then_inc(sem.oc_stored, 16)

            rows(sp, body)
            sp.wait_ge(sem.oc_stored, 16 * (B + 2))

        @block.gpsimd
        def _(pool):
            g = nc.gpsimd
            g.memset(t.bqp[:, :, :], 0.0).then_inc(sem.bqp_made, 1)

            def norm_x1(i, s, k, h):
                q = (s + 1) % ROWS
                if h == 0:
                    turn = (k if s < ROWS - 1 else k + 1) + 1
                    pool.wait_ge(rows_loaded[q], 32 * turn)
                if live(i) and after_first(i + 1):
                    pool.wait_ge(sem.t3_done, 2 * i + h + 1)
                alone(pool, sem.pool_passed)
                for j in range(h * HT, (h + 1) * HT):
                    last = g.tensor_scalar(t.n2[:, j], xc[:, q, j], keep.nrm[:, q, 1, j:j + 1],
                                           keep.nrm[:, q, 0, j:j + 1], ALU.add, ALU.mult)
                last.then_inc(sem.n2c_ready, 1)

            def probabilities(b, q, h):
                pool.wait_ge(sem.c_rcp, 2 * b + h + 1)
                half = t.p[:, q, h * HT * H:(h + 1) * HT * H]
                g.tensor_tensor(half, half, t.rc[:, h].unsqueeze(2).to_broadcast([P, HT * H, NQ]), ALU.mult) \
                    .then_inc(sem.c_prob, 1)

            def norm_out(b, h):
                n = 2 * b + h
                pool.wait_ge(sem.oc_var, n + 1)
                if last_row(b):
                    pool.wait_ge(sem.yc_ready, n - 1)
                g.tensor_tensor(t.o_r[:, h, 0], t.o_v[:, h, 0], keep.mhalf[:, 0:HT], ALU.pow).then_inc(sem.oc_pow, 1)
                pool.wait_ge(sem.oc_pow, n + 1)
                g.tensor_tensor(t.o_r[:, h, 1], t.o_v[:, h, 1], t.o_r[:, h, 0], ALU.mult).then_inc(sem.oc_norm, 1)

            def residual(b, q, h):
                pool.wait_ge(sem.yc_ready, 2 * b + h + 1)
                half = slice(h * HT, (h + 1) * HT)
                g.tensor_tensor(t.y[:, q % 2, half], xc[:, q, half], t.y[:, q % 2, half], ALU.add) \
                    .then_inc(sem.oc_added, 1)

            def body(i, s, k):
                opening = isinstance(i, int) and i < 0
                if opening:
                    norm_x1(i, s, k, 0)
                    norm_x1(i, s, k, 1)
                    pool.wait_ge(sem.kv_kept, 2)
                if live(i - 1) and not last_row(i - 1):
                    probabilities(i - 1, (s + 1) % 2, 1)
                if live(i + 1):
                    if live(i):
                        pool.wait_ge(sem.cr_done, i + 1)
                    for dst, src in ((t.kb, t.khT), (t.vb, t.vhT)):
                        for c in range(C):
                            cols = src[:, c].rearrange("p (k b) -> p b k", b=B)[:, bass.ds(i + 1, 1), :]
                            last = g.tensor_tensor(dst[:, c], cols.to_broadcast([P, HC, NQ]), keep.hmask[:, :, :],
                                                   ALU.mult)
                    last.then_inc(sem.kb_made, 1)
                if live(i - 2):
                    norm_out(i - 2, 1)
                if live(i + 1) and not opening:
                    norm_x1(i, s, k, 0)
                if live(i - 2) and not last_two(i - 2):
                    residual(i - 2, (s - 2) % ROWS, 0)
                if live(i + 1) and not opening:
                    norm_x1(i, s, k, 1)
                if live(i) and not last_row(i):
                    probabilities(i, s % 2, 0)
                if last_row(i):
                    residual(i - 2, (s - 2) % ROWS, 1)
                if live(i - 1):
                    norm_out(i - 1, 0)
                if live(i - 2) and not last_row(i) and not last_two(i - 2):
                    residual(i - 2, (s - 2) % ROWS, 1)

            rows(pool, body)

        @block.scalar
        def _(act):
            a = nc.scalar

            def exp(i, s, h):
                act.wait_ge(sem.c_sub, 2 * i + h + 1)
                half = t.p[:, s % 2, h * HT * H:(h + 1) * HT * H]
                a.activation(half, half, ACT.Exp).then_inc(sem.c_exp, 1)

            def keep_hi(i, h):
                act.wait_ge(sem.t3_done, 2 * i + h + 3)
                if live(i):
                    act.wait_ge(sem.sc_done, 2 * i + h + 1)
                a.activation(t.n2T_hi[:, :, h * HS:(h + 1) * HS], ps[:, (GA, GB)[h]:(GA, GB)[h] + 2, :], ACT.Copy) \
                    .then_inc(sem.t3_hi, 1)

            def keep_probabilities(b, h):
                act.wait_ge(sem.tp_done, 2 * b + h + 1)
                if live(b - 1):
                    act.wait_ge(sem.oc_done, 2 * b + h - 1)
                bank = probability_banks(b, h)
                a.activation(t.pT[:, :, h * HS:(h + 1) * HS], ps[:, bank:bank + 2, :], ACT.Copy) \
                    .then_inc(sem.tp_kept, 1)

            def centre_out(b, q, h):
                act.wait_ge(sem.oc_norm, 2 * b + h + 1)
                if live(b - 2):
                    act.wait_ge(sem.oc_stored, 16 * (b - 1))
                for j in range(HT):
                    last = a.activation(t.y[:, q, h * HT + j],
                                        ps[:, out_banks(b, h) + j // 2, (j % 2) * D:(j % 2 + 1) * D],
                                        ACT.Identity, scale=t.o_r[:, h, 0, j:j + 1], bias=t.o_r[:, h, 1, j:j + 1])
                last.then_inc(sem.yc_ready, 1)

            act.wait_ge(sem.c_w, 16 * 8)
            act.wait_ge(sem.kv_done, 2)
            for c in range(C):
                last = a.activation(t.vhT[:, c], ps[:, 1, c * TOK:(c + 1) * TOK], ACT.Identity, bias=bv[:, c:c + 1])
            last.then_inc(sem.kv_kept, 1)

            def body(i, s, k):
                if live(i - 1):
                    keep_probabilities(i - 1, 1)
                if live(i):
                    exp(i, s, 0)
                if last_row(i - 1):
                    centre_out(i - 2, s % 2, 0)
                if live(i - 2):
                    centre_out(i - 2, s % 2, 1)
                opening = isinstance(i, int) and i < 0
                if opening:
                    keep_hi(i, 0)
                    keep_hi(i, 1)
                if live(i + 1):
                    act.wait_ge(sem.mn_done, i + 2)
                    a.activation(t.m_hi[:, :, :], ps[:, GA, :].rearrange("p (c q) -> p c q", c=C), ACT.Copy) \
                        .then_inc(sem.m_hi, 1)
                if live(i):
                    exp(i, s, 1)
                if live(i + 1) and not opening:
                    keep_hi(i, 0)
                if live(i - 1) and not last_row(i):
                    centre_out(i - 1, (s + 1) % 2, 0)
                if live(i + 1) and not opening:
                    keep_hi(i, 1)
                if live(i):
                    keep_probabilities(i, 0)

            rows(act, body)

        @block.vector
        def _(dve):
            v = nc.vector
            dve.wait_ge(sem.c_w, 16 * 8)
            dve.wait_ge(sem.kv_done, 1)
            for c in range(C):
                last = v.tensor_scalar(t.khT[:, c], ps[:, 0, c * TOK:(c + 1) * TOK], bk[:, c:c + 1], None, ALU.add)
            last.then_inc(sem.kv_kept, 1)
            dve.wait_ge(sem.wqT_done, 1)
            v.tensor_scalar(t.wqT[:, :, :], ps[:, 4:6, 0:D], KEY_SCALE, None, ALU.mult).then_inc(sem.wqT_kept, 1)
            v.tensor_scalar(keep.bo_rep[:, :], keep.bo_rep[:, :], 1.0 / H, None, ALU.mult).then_inc(sem.bo_made, 1)
            dve.wait_ge(sem.bqp_made, 1)
            v.tensor_scalar(t.bqp[:, :, 0:64:32], bq.unsqueeze(2).to_broadcast([P, C, 2]), KEY_SCALE, None,
                            ALU.mult)
            v.tensor_copy(t.crow[:, :], keep.zero[:, :]).then_inc(sem.bqp_made, 1)
            dve.wait_ge(sem.bqp_made, 2)
            dve.wait_ge(sem.bo_made, 1)

            def keep_lo(i, h):
                dve.wait_ge(sem.t3_hi, 2 * i + h + 3)
                half = slice(h * HS, (h + 1) * HS)
                v.tensor_tensor(t.n2T_lo[:, :, half], ps[:, (GA, GB)[h]:(GA, GB)[h] + 2, :], t.n2T_hi[:, :, half],
                                ALU.subtract).then_inc(sem.t3_lo, 1)

            def less_max(i, s, h):
                n, group = 2 * i + h, (GA, GB)[h]
                scores = ps[:, group:group + 2, :].rearrange("p b (g q) -> p (b g) q", q=NQ)
                dve.wait_ge(sem.sc_done, n + 1)
                v.tensor_reduce(t.mx[:, h], scores, AX, ALU.max).then_inc(sem.c_max, 1)
                dve.wait_ge(sem.c_max, n + 1)
                v.tensor_tensor(t.p[:, s % 2, h * HT * H:(h + 1) * HT * H], scores,
                                t.mx[:, h].unsqueeze(2).to_broadcast([P, HT * H, NQ]), ALU.subtract) \
                    .then_inc(sem.c_sub, 1)

            def sums(i, s, h):
                n = 2 * i + h
                dve.wait_ge(sem.c_exp, n + 1)
                v.tensor_reduce(t.sm[:, h], t.p[:, s % 2, h * HT * H:(h + 1) * HT * H], AX, ALU.add) \
                    .then_inc(sem.c_sum, 1)
                dve.wait_ge(sem.c_sum, n + 1)
                if live(i - 1):
                    dve.wait_ge(sem.c_prob, n - 1)
                v.reciprocal(t.rc[:, h], t.sm[:, h]).then_inc(sem.c_rcp, 1)

            def last_probabilities(h):
                dve.wait_ge(sem.c_rcp, 2 * (B - 1) + h + 1)
                half = t.p[:, (B - 1) % 2, h * HT * H:(h + 1) * HT * H]
                v.tensor_tensor(half, half, t.rc[:, h].unsqueeze(2).to_broadcast([P, HT * H, NQ]), ALU.mult) \
                    .then_inc(sem.last_prob, 1)

            def last_residual(b, h):
                dve.wait_ge(sem.yc_ready, 2 * b + h + 1)
                half, q = slice(h * HT, (h + 1) * HT), b % ROWS
                v.tensor_tensor(t.y[:, q % 2, half], xc[:, q, half], t.y[:, q % 2, half], ALU.add) \
                    .then_inc(sem.last_added, 1)

            def stats_out(b, h):
                n = 2 * b + h
                dve.wait_ge(sem.oc_done, n + 1)
                for j in range(HT):
                    last = v.bn_stats(t.o_st[:, j], ps[:, out_banks(b, h) + j // 2, (j % 2) * D:(j % 2 + 1) * D])
                last.then_inc(sem.oc_stats, 1)
                dve.wait_ge(sem.oc_stats, n + 1)
                alone(dve, sem.dve_passed)
                for j in range(HT):
                    last = v.bn_aggr(t.o_mv[:, j], t.o_st[:, j])
                last.then_inc(sem.oc_mv, 1)
                dve.wait_ge(sem.oc_mv, n + 1)
                if live(b - 1):
                    dve.wait_ge(sem.oc_norm, n - 1)
                v.tensor_scalar(t.o_v[:, h, 0], t.o_mv[:, :, 1], EPS, None, ALU.add)
                v.tensor_scalar(t.o_v[:, h, 1], t.o_mv[:, :, 0], -1.0, None, ALU.mult).then_inc(sem.oc_var, 1)

            def body(i, s, k):
                if live(i):
                    less_max(i, s, 0)
                    less_max(i, s, 1)
                opening = isinstance(i, int) and i < 0
                if opening:
                    keep_lo(i, 0)
                    keep_lo(i, 1)
                if live(i + 1):
                    dve.wait_ge(sem.mn_done, i + 2)
                    v.tensor_tensor(t.nv[:, (s + 1) % ROWS], ps[:, GA + 1, :].rearrange("p (c d) -> p c d", c=C),
                                    keep.bo_rep[:, :].unsqueeze(1).to_broadcast([P, C, D]), ALU.add) \
                        .then_inc(sem.n_kept, 1)
                    dve.wait_ge(sem.m_hi, i + 2)
                    v.tensor_tensor(t.m_lo[:, :, :], ps[:, GA, :].rearrange("p (c q) -> p c q", c=C), t.m_hi[:, :, :],
                                    ALU.subtract).then_inc(sem.m_kept, 1)
                if live(i):
                    sums(i, s, 0)
                if last_row(i):
                    last_probabilities(0)
                    sums(i, s, 1)
                    last_probabilities(1)
                if live(i - 1):
                    stats_out(i - 1, 0)
                if live(i + 1):
                    dve.wait_ge(sem.cr_done, i + 2)
                    v.tensor_copy(t.crow_t[32:64, :], ps[32:64, GB, 0:HQ]).then_inc(sem.cr_hi, 1)
                    v.tensor_copy(t.crow[0:32, :], ps[0:32, GB, 0:HQ])
                    dve.wait_ge(sem.cr_hi, i + 2)
                    v.tensor_tensor(t.crow[32:64, :], ps[32:64, GB, 0:HQ], t.crow_t[32:64, :], ALU.subtract) \
                        .then_inc(sem.cr_kept, 1)
                    if not opening:
                        keep_lo(i, 0)
                if live(i) and not last_row(i):
                    sums(i, s, 1)
                if live(i + 1) and not opening:
                    keep_lo(i, 1)
                if last_row(i - 1):
                    last_residual(B - 2, 0)
                if live(i - 1):
                    stats_out(i - 1, 1)
                if last_row(i - 1):
                    last_residual(B - 2, 1)
                    for h in range(2):
                        last_residual(B - 1, h)

            rows(dve, body)

        @block.tensor
        def _(pe):
            mm, tr = nc.tensor.matmul, nc.tensor.transpose
            pe.wait_ge(sem.c_w, 16 * 8)
            for bank, w in ((0, wk), (1, wv)):
                for f in range(C):
                    for c in range(C):
                        last = mm(ps[:, bank, f * TOK:(f + 1) * TOK], w[:, c, f * P:(f + 1) * P], keep.o2T[:, c],
                                  start=(c == 0), stop=(c == C - 1))
                last.then_inc(sem.kv_done, 1)
            for f in range(C):
                for c in range(C):
                    last = tr(ps[:, 4 + f, c * P:(c + 1) * P], wq[:, c, f * P:(f + 1) * P], keep.ident[:, :])
            last.then_inc(sem.wqT_done, 1)

            def transposed(h):
                for j in range(HT):
                    for c in range(C):
                        last = tr(ps[:, (GA, GB)[h] + c, j * P:(j + 1) * P], t.n2[:, h * HT + j, c * P:(c + 1) * P],
                                  keep.ident[:, :])
                last.then_inc(sem.t3_done, 1)

            def scores(h):
                for b in range(2):
                    bank = (GA, GB)[h] + b
                    mm(ps[:, bank, :], keep.selrow[:, :], t.crow[:, :].unsqueeze(1).to_broadcast([P, 2, HQ]),
                       start=True, stop=False, skip_group_check=True)
                    for jj in range(2):
                        at = slice((h * HT + 2 * b + jj) * P, (h * HT + 2 * b + jj + 1) * P)
                        for c in range(C):
                            last = three_passes(nc, ps[:, bank, jj * HQ:(jj + 1) * HQ], t.n2T_hi[:, c, at],
                                                t.n2T_lo[:, c, at], t.m_hi[:, c], t.m_lo[:, c],
                                                False, c == C - 1, skip=True)
                last.then_inc(sem.sc_done, 1)

            def probabilities_transposed(b, q, h):
                bank = probability_banks(b, h)
                for j in range(HT):
                    src = t.p[:, q, (h * HT + j) * H:(h * HT + j + 1) * H].rearrange("p g q -> p (g q)")
                    for c in range(C):
                        last = tr(ps[:, bank + c, j * P:(j + 1) * P], src[:, c * P:(c + 1) * P], keep.ident[:, :])
                last.then_inc(sem.tp_done, 1)

            def outputs(b, q, h):
                for j in range(HT):
                    for c in range(C):
                        last = mm(ps[:, out_banks(b, h) + j // 2, (j % 2) * D:(j % 2 + 1) * D],
                                  t.pT[:, c, (h * HT + j) * P:(h * HT + j + 1) * P], t.nv[:, q, c],
                                  start=(c == 0), stop=(c == C - 1))
                last.then_inc(sem.oc_done, 1)

            def body(i, s, k):
                if live(i):
                    pe.wait_ge(sem.cr_kept, i + 1)
                    pe.wait_ge(sem.t3_lo, 2 * i + 1)
                    if not live(i - 1):
                        pe.wait_ge(sem.m_kept, 1)
                        pe.wait_ge(sem.n_kept, 1)
                    scores(0)
                if last_row(i - 1):
                    pe.wait_ge(sem.last_prob, 2)
                    pe.wait_ge(sem.c_sub, 2 * B)
                    probabilities_transposed(B - 1, (s + 1) % 2, 1)
                elif live(i - 1):
                    pe.wait_ge(sem.c_prob, 2 * i)
                    pe.wait_ge(sem.tp_kept, 2 * i - 1)
                    probabilities_transposed(i - 1, (s + 1) % 2, 1)
                if live(i):
                    pe.wait_ge(sem.t3_lo, 2 * i + 2)
                    scores(1)
                opening = isinstance(i, int) and i < 0
                if opening:
                    for h in range(2):
                        pe.wait_ge(sem.n2c_ready, h + 1)
                        pe.wait_ge(sem.kv_kept, 2)
                        transposed(h)
                    pe.wait_ge(sem.wqT_kept, 1)
                    pe.wait_ge(sem.bqp_made, 2)
                    pe.wait_ge(sem.t3_lo, 1)
                if live(i + 1):
                    pe.wait_ge(sem.kb_made, i + 2)
                    if live(i):
                        pe.wait_ge(sem.c_sub, 2 * i + 1)
                    for f in range(C):
                        for c in range(C):
                            mm(ps[:, GA, c * HQ + f * P:c * HQ + (f + 1) * P], t.wqT[:, f, c * P:(c + 1) * P],
                               t.kb[:, f].rearrange("p h q -> p (h q)"), start=True, stop=True)
                        last = mm(ps[:, GA + 1, f * D:(f + 1) * D], t.vb[:, f].rearrange("p h q -> p (h q)"), wo[:, f],
                                  start=True, stop=True)
                    last.then_inc(sem.mn_done, 1)
                if live(i - 1):
                    pe.wait_ge(sem.tp_kept, 2 * i - 1 if last_row(i - 1) else 2 * i)
                    outputs(i - 1, (s - 1) % ROWS, 0)
                if live(i + 1):
                    if live(i):
                        pe.wait_ge(sem.c_sub, 2 * i + 2)
                    else:
                        pe.wait_ge(sem.t3_lo, 2)
                    for f in range(C):
                        last = mm(ps[0:64, GB, f * P:(f + 1) * P], t.bqp[:, f], t.kb[:, f].rearrange("p h q -> p (h q)"),
                                  start=True, stop=True)
                    last.then_inc(sem.cr_done, 1)
                if live(i + 1) and not opening:
                    pe.wait_ge(sem.n2c_ready, 2 * i + 3)
                    pe.wait_ge(sem.m_kept, i + 2)
                    pe.wait_ge(sem.n_kept, i + 2)
                    transposed(0)
                if live(i - 1):
                    if last_row(i - 1):
                        pe.wait_ge(sem.tp_kept, 2 * B)
                    elif live(i - 2):
                        pe.wait_ge(sem.yc_ready, 2 * i - 2)
                    outputs(i - 1, (s - 1) % ROWS, 1)
                if live(i + 1) and not opening:
                    pe.wait_ge(sem.n2c_ready, 2 * i + 4)
                    pe.wait_ge(sem.cr_kept, i + 2)
                    transposed(1)
                if last_row(i):
                    pe.wait_ge(sem.last_prob, 1)
                    pe.wait_ge(sem.c_sub, 2 * B - 1)
                    probabilities_transposed(i, s % 2, 0)
                elif live(i):
                    pe.wait_ge(sem.c_prob, 2 * i + 1)
                    if live(i - 1):
                        pe.wait_ge(sem.yc_ready, 2 * i - 1)
                    probabilities_transposed(i, s % 2, 0)

            rows(pe, body)


_INS = ['L0_attn_x', 'L0_attn_Wz', 'L0_attn_bz', 'L0_attn_Wh', 'L0_attn_bh', 'L0_ffn_slot_query',
        'L0_ffn_d_Wq', 'L0_ffn_d_Wk', 'L0_ffn_d_Wv', 'L0_ffn_d_Wo', 'L0_ffn_d_bq', 'L0_ffn_d_bk', 'L0_ffn_d_bv',
        'L0_ffn_d_bo', 'L0_ffn_c_Wq', 'L0_ffn_c_Wk', 'L0_ffn_c_Wv', 'L0_ffn_c_Wo', 'L0_ffn_c_bq', 'L0_ffn_c_bk',
        'L0_ffn_c_bv', 'L0_ffn_c_bo', 'L0_ffn_e_ln_g', 'L0_ffn_e_ln_b', 'L0_ffn_e_W1', 'L0_ffn_e_b1',
        'L0_ffn_e_Wg', 'L0_ffn_e_bg', 'L0_ffn_e_W2', 'L0_ffn_e_b2']


def kernel(**inputs):
    import numpy as _np
    import concourse.bacc as _bacc
    from concourse import mybir as _mybir
    from concourse.bass_utils import run_bass_kernel_spmd as _run

    nc = _bacc.Bacc("TRN2", target_bir_lowering=False, num_devices=1)
    arrays, args = {}, []
    for name in _INS:
        a = _np.ascontiguousarray(inputs[name])
        arrays[f"in_{name}_dram"] = a
        args.append(nc.dram_tensor(f"in_{name}_dram", a.shape, _mybir.dt.from_np(a.dtype), kind="ExternalInput").ap())
    out = nc.dram_tensor("out_0_dram", (B, S, D), _mybir.dt.float32, kind="ExternalOutput").ap()
    mixer_moe(nc, *args, out)
    r = _run(nc, [arrays], core_ids=[0])
    return r.results[0]["out_0_dram"]
```
